# Optimizing a Trainium2 kernel written in Bass

```python
import numpy as np
import jax
import jax.numpy as jnp

def _softmax(x, axis=-1):
    return jax.nn.softmax(x, axis=axis)

def _gelu(x):
    return jax.nn.gelu(x, approximate=True)

def _silu(x):
    return jax.nn.silu(x)

def _sigmoid(x):
    return jax.nn.sigmoid(x)

def _layernorm(x, axis=-1, eps=1e-05):
    m = jnp.mean(x, axis=axis, keepdims=True)
    v = jnp.var(x, axis=axis, keepdims=True)
    return (x - m) / jnp.sqrt(v + eps)

def _scatter_add(tgt, idx, src, axis=0):
    return tgt.at[idx].add(src)

def _segment_sum(src, seg, n):
    return jax.ops.segment_sum(src, seg, n)
kernel_name = 'mk_flamingo_gated_d2_seqx_r4_a01b9a'

def setup_inputs(seed: int=0):
    np.random.seed(seed)
    _w = jnp.asarray

    def _rec_inputs():
        import jax
        import jax.numpy as jnp
        _rk = jax.random.key(seed)
        x = -0.0002928 + 1 * jax.random.normal(jax.random.fold_in(_rk, 1), (4, 512, 256), jnp.float32)
        _lenS = 512 - jax.random.randint(jax.random.fold_in(_rk, 7), (4,), 0, max(1, 512 // 4) + 1, jnp.int32)
        _lenS2 = 512 - jax.random.randint(jax.random.fold_in(_rk, 8), (4,), 0, max(1, 512 // 4) + 1, jnp.int32)
        _ctx_1024P = jax.random.normal(jax.random.fold_in(_rk, 11), (4, 16, 256), jnp.float32)
        _ctx_1024c = jax.random.dirichlet(jax.random.fold_in(_rk, 511), 0.3 * jnp.ones((16,), jnp.float32), (4, 512))
        _ctx_1024t = jnp.einsum('bsk,bkd->bsd', _ctx_1024c, _ctx_1024P)
        _ctx_1024t = _ctx_1024t * jax.lax.rsqrt(jnp.mean(jnp.square(_ctx_1024t)) + 1e-12) * 0.953939
        ctx_1024 = -1.39393e-06 + 0.999914 * (_ctx_1024t + 0.3 * jax.random.normal(jax.random.fold_in(_rk, 611), (4, 512, 256), jnp.float32))
        _validS = jnp.arange(512)[None, :] < _lenS[:, None]
        _validS2 = jnp.arange(512)[None, :] < _lenS2[:, None]
        _causal = jnp.tril(jnp.ones((512, 512), dtype=bool))
        mask_BxS2_bf1 = jnp.ones((4, 512), dtype=bool)
        mask_Bx1xSxS2_if1 = jnp.where(jnp.ones((4, 1, 512, 512), dtype=bool), 1, 0).astype(jnp.int32)
        _g = jax.random.normal(jax.random.fold_in(_rk, 9001), (2, 2), jnp.float32)
        _g = jnp.sign(_g) * jnp.maximum(jnp.abs(_g), 1.0) + (_g == 0) * 1.0
        g_xattn = _g[0]
        g_ffn = _g[1]
        return (x, ctx_1024, mask_BxS2_bf1, mask_Bx1xSxS2_if1, g_xattn, g_ffn)
    x, ctx_1024, mask_BxS2_bf1, mask_Bx1xSxS2_if1, g_xattn, g_ffn = _rec_inputs()

    def _L0_xattn_setup():
        import jax, jax.numpy as jnp
        import numpy as np
        DIM = 256
        HEADS = 16
        HEAD_DIM = DIM // HEADS
        ROPE_BASE = 10000.0

        def _rope_cos_sin(seq_len, head_dim, dtype=jnp.float32):
            inv_freq = 1.0 / ROPE_BASE ** (jnp.arange(0, head_dim, 2, dtype=jnp.float32) / head_dim)
            t = jnp.arange(seq_len, dtype=jnp.float32)
            freqs = jnp.outer(t, inv_freq)
            emb = jnp.concatenate([freqs, freqs], axis=-1)
            return (jnp.cos(emb).astype(dtype), jnp.sin(emb).astype(dtype))

        def _rotate_half(x):
            x1, x2 = jnp.split(x, 2, axis=-1)
            return jnp.concatenate([-x2, x1], axis=-1)

        def _apply_rope(x, cos, sin):
            return x * cos[None, None, :, :] + _rotate_half(x) * sin[None, None, :, :]
        key = jax.random.key(seed)
        ks = jax.random.split(key, 10)
        B, L, K = (2, 512, 512)
        s = 1.0 / np.sqrt(DIM)
        inp = {'target': jax.random.normal(ks[0], (B, L, DIM), jnp.float32), 'context': jax.random.normal(ks[1], (B, K, DIM), jnp.float32), 'target_mask': jnp.ones((B, L), dtype=bool), 'context_mask': jnp.ones((B, K), dtype=bool), 'Wq': jax.random.normal(ks[2], (DIM, DIM), jnp.float32) * s, 'bq': jnp.zeros((DIM,), jnp.float32), 'Wk': jax.random.normal(ks[3], (DIM, DIM), jnp.float32) * s, 'bk': jnp.zeros((DIM,), jnp.float32), 'Wv': jax.random.normal(ks[4], (DIM, DIM), jnp.float32) * s, 'bv': jnp.zeros((DIM,), jnp.float32), 'Wp': jax.random.normal(ks[5], (DIM, DIM), jnp.float32) * s, 'bp': jnp.zeros((DIM,), jnp.float32)}
        return inp
    _L0_xattn_all = _L0_xattn_setup()
    _L0_xattn_in = {k: v for k, v in _L0_xattn_all.items() if k in ('Wq', 'bq', 'Wk', 'bk', 'Wv', 'bv', 'Wp', 'bp')}
    del _L0_xattn_all

    def _L0_ffn_setup():
        import jax, jax.numpy as jnp
        import numpy as np

        def _binarize(w):
            alpha = jax.lax.stop_gradient(jnp.mean(jnp.abs(w), axis=1, keepdims=True))
            bw = alpha * jnp.sign(w)
            return w + jax.lax.stop_gradient(bw - w)
        key = jax.random.key(seed)
        k1, k2, k3, k4, k5 = jax.random.split(key, 5)
        D, H = (256, 1024)
        x = jax.random.normal(k1, (64, 196, D), dtype=jnp.float32)
        w1 = jax.random.normal(k2, (H, D), dtype=jnp.float32) * 0.02
        b1 = jax.random.normal(k3, (H,), dtype=jnp.float32) * 0.02
        w2 = jax.random.normal(k4, (D, H), dtype=jnp.float32) * 0.02
        b2 = jax.random.normal(k5, (D,), dtype=jnp.float32) * 0.02
        return {'x': x, 'w1': w1, 'b1': b1, 'w2': w2, 'b2': b2}
    _L0_ffn_all = _L0_ffn_setup()
    _L0_ffn_in = {k: v for k, v in _L0_ffn_all.items() if k in ('w1', 'b1', 'w2', 'b2')}
    del _L0_ffn_all

    def _L1_xattn_setup():
        import jax, jax.numpy as jnp
        import numpy as np
        D_MODEL = 256
        HEADS = 16
        D_K = D_MODEL // HEADS
        NEG = -1000000000.0
        key = jax.random.key(seed)
        ks = jax.random.split(key, 12)
        B, S = (2, 512)
        inp = {'q': jax.random.normal(ks[0], (B, S, D_MODEL), jnp.float32), 'k': jax.random.normal(ks[1], (B, S, D_MODEL), jnp.float32), 'v': jax.random.normal(ks[2], (B, S, D_MODEL), jnp.float32), 'mask': jnp.ones((B, 1, S, S), jnp.int32), 'W_q': jax.random.normal(ks[3], (D_MODEL, D_MODEL), jnp.float32) / np.sqrt(D_MODEL), 'b_q': jnp.zeros((D_MODEL,), jnp.float32), 'W_k': jax.random.normal(ks[4], (D_MODEL, D_MODEL), jnp.float32) / np.sqrt(D_MODEL), 'b_k': jnp.zeros((D_MODEL,), jnp.float32), 'W_v': jax.random.normal(ks[5], (D_MODEL, D_MODEL), jnp.float32) / np.sqrt(D_MODEL), 'b_v': jnp.zeros((D_MODEL,), jnp.float32), 'W_o': jax.random.normal(ks[6], (D_MODEL, D_MODEL), jnp.float32) / np.sqrt(D_MODEL), 'b_o': jnp.zeros((D_MODEL,), jnp.float32)}
        return inp
    _L1_xattn_all = _L1_xattn_setup()
    _L1_xattn_in = {k: v for k, v in _L1_xattn_all.items() if k in ('W_q', 'b_q', 'W_k', 'b_k', 'W_v', 'b_v', 'W_o', 'b_o')}
    del _L1_xattn_all

    def _L1_ffn_setup():
        import jax, jax.numpy as jnp
        import numpy as np
        B, T, C = (2, 512, 256)
        E, F = (8, 256)
        FS = 512
        TOP_K = 2
        key = jax.random.key(seed)
        ks = jax.random.split(key, 6)
        s = lambda *d: 1.0 / np.sqrt(d[-1])
        return {'hidden_tensor': jax.random.normal(ks[0], (B, T, C), jnp.float32), 'w_router': jax.random.normal(ks[1], (E, C), jnp.float32) * s(C), 'w1_stack': jax.random.normal(ks[2], (E, F, C), jnp.float32) * s(C), 'w2_stack': jax.random.normal(ks[3], (E, C, F), jnp.float32) * s(F), 'ws1': jax.random.normal(ks[4], (FS, C), jnp.float32) * s(C), 'ws2': jax.random.normal(ks[5], (C, FS), jnp.float32) * s(FS)}
    _L1_ffn_all = _L1_ffn_setup()
    _L1_ffn_in = {k: v for k, v in _L1_ffn_all.items() if k in ('w_router', 'w1_stack', 'w2_stack', 'ws1', 'ws2')}
    del _L1_ffn_all
    return {'x': x, 'ctx_1024': ctx_1024, 'mask_BxS2_bf1': mask_BxS2_bf1, 'mask_Bx1xSxS2_if1': mask_Bx1xSxS2_if1, 'g_xattn': g_xattn, 'g_ffn': g_ffn, 'L0_xattn_Wq': _L0_xattn_in['Wq'], 'L0_xattn_bq': _L0_xattn_in['bq'], 'L0_xattn_Wk': _L0_xattn_in['Wk'], 'L0_xattn_bk': _L0_xattn_in['bk'], 'L0_xattn_Wv': _L0_xattn_in['Wv'], 'L0_xattn_bv': _L0_xattn_in['bv'], 'L0_xattn_Wp': _L0_xattn_in['Wp'], 'L0_xattn_bp': _L0_xattn_in['bp'], 'L0_ffn_w1': _L0_ffn_in['w1'], 'L0_ffn_b1': _L0_ffn_in['b1'], 'L0_ffn_w2': _L0_ffn_in['w2'], 'L0_ffn_b2': _L0_ffn_in['b2'], 'L1_xattn_W_q': _L1_xattn_in['W_q'], 'L1_xattn_b_q': _L1_xattn_in['b_q'], 'L1_xattn_W_k': _L1_xattn_in['W_k'], 'L1_xattn_b_k': _L1_xattn_in['b_k'], 'L1_xattn_W_v': _L1_xattn_in['W_v'], 'L1_xattn_b_v': _L1_xattn_in['b_v'], 'L1_xattn_W_o': _L1_xattn_in['W_o'], 'L1_xattn_b_o': _L1_xattn_in['b_o'], 'L1_ffn_w_router': _L1_ffn_in['w_router'], 'L1_ffn_w1_stack': _L1_ffn_in['w1_stack'], 'L1_ffn_w2_stack': _L1_ffn_in['w2_stack'], 'L1_ffn_ws1': _L1_ffn_in['ws1'], 'L1_ffn_ws2': _L1_ffn_in['ws2']}

def reference(x, ctx_1024, mask_BxS2_bf1, mask_Bx1xSxS2_if1, g_xattn, g_ffn, L0_xattn_Wq, L0_xattn_bq, L0_xattn_Wk, L0_xattn_bk, L0_xattn_Wv, L0_xattn_bv, L0_xattn_Wp, L0_xattn_bp, L0_ffn_w1, L0_ffn_b1, L0_ffn_w2, L0_ffn_b2, L1_xattn_W_q, L1_xattn_b_q, L1_xattn_W_k, L1_xattn_b_k, L1_xattn_W_v, L1_xattn_b_v, L1_xattn_W_o, L1_xattn_b_o, L1_ffn_w_router, L1_ffn_w1_stack, L1_ffn_w2_stack, L1_ffn_ws1, L1_ffn_ws2):
    import jax
    import jax.numpy as jnp

    def _L0_xattn_ref(target, context, target_mask, context_mask, Wq, bq, Wk, bk, Wv, bv, Wp, bp):
        import jax, jax.numpy as jnp
        import numpy as np
        DIM = 256
        HEADS = 16
        HEAD_DIM = DIM // HEADS
        ROPE_BASE = 10000.0

        def _rope_cos_sin(seq_len, head_dim, dtype=jnp.float32):
            inv_freq = 1.0 / ROPE_BASE ** (jnp.arange(0, head_dim, 2, dtype=jnp.float32) / head_dim)
            t = jnp.arange(seq_len, dtype=jnp.float32)
            freqs = jnp.outer(t, inv_freq)
            emb = jnp.concatenate([freqs, freqs], axis=-1)
            return (jnp.cos(emb).astype(dtype), jnp.sin(emb).astype(dtype))

        def _rotate_half(x):
            x1, x2 = jnp.split(x, 2, axis=-1)
            return jnp.concatenate([-x2, x1], axis=-1)

        def _apply_rope(x, cos, sin):
            return x * cos[None, None, :, :] + _rotate_half(x) * sin[None, None, :, :]
        B, L, C = target.shape
        K = context.shape[1]
        H, D = (HEADS, HEAD_DIM)
        q = (target @ Wq.T + bq).reshape(B, L, H, D).transpose(0, 2, 1, 3)
        k = (context @ Wk.T + bk).reshape(B, K, H, D).transpose(0, 2, 1, 3)
        v = (context @ Wv.T + bv).reshape(B, K, H, D).transpose(0, 2, 1, 3)
        cos_q, sin_q = _rope_cos_sin(L, D)
        cos_k, sin_k = _rope_cos_sin(K, D)
        q = _apply_rope(q, cos_q, sin_q)
        k = _apply_rope(k, cos_k, sin_k)
        scale = D ** (-0.5)
        attn = jnp.einsum('bhld,bhkd->bhlk', q, k) * scale
        attn = jnp.where(context_mask[:, None, None, :], attn, -jnp.inf)
        attn = jax.nn.softmax(attn, axis=-1)
        x = jnp.einsum('bhlk,bhkd->bhld', attn, v)
        x = x.transpose(0, 2, 1, 3).reshape(B, L, C)
        x = x @ Wp.T + bp
        x = x * target_mask[:, :, None].astype(x.dtype)
        return x

    def _L0_ffn_ref(x, w1, b1, w2, b2):
        import jax, jax.numpy as jnp
        import numpy as np

        def _binarize(w):
            alpha = jax.lax.stop_gradient(jnp.mean(jnp.abs(w), axis=1, keepdims=True))
            bw = alpha * jnp.sign(w)
            return w + jax.lax.stop_gradient(bw - w)
        bw1 = _binarize(w1)
        h = jnp.einsum('bsd,hd->bsh', x, bw1) + b1
        h = jax.nn.gelu(h, approximate=False)
        bw2 = _binarize(w2)
        out = jnp.einsum('bsh,dh->bsd', h, bw2) + b2
        return out

    def _L1_xattn_ref(q, k, v, mask, W_q, b_q, W_k, b_k, W_v, b_v, W_o, b_o):
        import jax, jax.numpy as jnp
        import numpy as np
        D_MODEL = 256
        HEADS = 16
        D_K = D_MODEL // HEADS
        NEG = -1000000000.0
        B, S, _ = q.shape
        query = q @ W_q + b_q
        key_ = k @ W_k + b_k
        value = v @ W_v + b_v
        query = query.reshape(B, S, HEADS, D_K).transpose(0, 2, 1, 3)
        key_ = key_.reshape(B, S, HEADS, D_K).transpose(0, 2, 1, 3)
        value = value.reshape(B, S, HEADS, D_K).transpose(0, 2, 1, 3)
        scores = jnp.einsum('bhqd,bhkd->bhqk', query, key_) / np.sqrt(D_K).astype(np.float32)
        scores = jnp.where(mask == 0, jnp.float32(NEG), scores)
        attn = jax.nn.softmax(scores, axis=-1)
        x = jnp.einsum('bhqk,bhkd->bhqd', attn, value)
        x = x.transpose(0, 2, 1, 3).reshape(B, S, HEADS * D_K)
        return x @ W_o + b_o

    def _L1_ffn_ref(hidden_tensor, w_router, w1_stack, w2_stack, ws1, ws2):
        import jax, jax.numpy as jnp
        import numpy as np
        B, T, C = (2, 512, 256)
        E, F = (8, 256)
        FS = 512
        TOP_K = 2
        Bb, Tt, Cc = hidden_tensor.shape
        x = hidden_tensor.reshape(-1, Cc)
        t = x.shape[0]
        logits = x @ w_router.T
        probs = jax.nn.softmax(logits, axis=-1)
        expert_weight, expert_idx = jax.lax.top_k(probs, TOP_K)
        expert_weight = expert_weight / jnp.sum(expert_weight, axis=-1, keepdims=True)
        flat_e = expert_idx.reshape(-1)
        order = jnp.argsort(flat_e, stable=True)
        sorted_e = flat_e[order]
        flat_tok = jnp.repeat(jnp.arange(t), TOP_K)
        sorted_tok = flat_tok[order]
        sorted_w = expert_weight.reshape(-1)[order]
        counts = jnp.bincount(sorted_e, length=E)
        offsets = jnp.concatenate([jnp.zeros((1,), counts.dtype), jnp.cumsum(counts)])
        local_pos = jnp.arange(t * TOP_K) - offsets[sorted_e]
        cap = t * TOP_K
        binned = jnp.zeros((E, cap, Cc), x.dtype).at[sorted_e, local_pos].set(x[sorted_tok])
        inter = jnp.einsum('ecd,efd->ecf', binned, w1_stack)
        inter = jnp.square(jax.nn.relu(inter))
        outb = jnp.einsum('ecf,edf->ecd', inter, w2_stack)
        flat_out = outb[sorted_e, local_pos] * sorted_w[:, None]
        moe_out = jnp.zeros((t, Cc), x.dtype).at[sorted_tok].add(flat_out)
        moe_out = moe_out.reshape(Bb, Tt, Cc)
        sh = jnp.square(jax.nn.relu(jnp.einsum('btc,fc->btf', hidden_tensor, ws1)))
        shared_out = jnp.einsum('btf,cf->btc', sh, ws2)
        return shared_out + moe_out
    x = x + jnp.tanh(g_xattn[0]) * _L0_xattn_ref(_layernorm(x, axis=-1), ctx_1024, mask_BxS2_bf1, mask_BxS2_bf1, L0_xattn_Wq, L0_xattn_bq, L0_xattn_Wk, L0_xattn_bk, L0_xattn_Wv, L0_xattn_bv, L0_xattn_Wp, L0_xattn_bp)
    x = x + jnp.tanh(g_ffn[0]) * _L0_ffn_ref(_layernorm(x, axis=-1), L0_ffn_w1, L0_ffn_b1, L0_ffn_w2, L0_ffn_b2)
    x = x + jnp.tanh(g_xattn[1]) * _L1_xattn_ref(_layernorm(x, axis=-1), ctx_1024, ctx_1024, mask_Bx1xSxS2_if1, L1_xattn_W_q, L1_xattn_b_q, L1_xattn_W_k, L1_xattn_b_k, L1_xattn_W_v, L1_xattn_b_v, L1_xattn_W_o, L1_xattn_b_o)
    x = x + jnp.tanh(g_ffn[1]) * _L1_ffn_ref(_layernorm(x, axis=-1), L1_ffn_w_router, L1_ffn_w1_stack, L1_ffn_w2_stack, L1_ffn_ws1, L1_ffn_ws2)
    return x

_drawn_inputs = setup_inputs


def setup_inputs(seed=0):
    import zlib

    import numpy as np

    out = dict(_drawn_inputs(seed))
    spreads = {'g_ffn': (-1.0, 0.2),
     'L0_xattn_bq': (0.0, 0.1),
     'L0_xattn_bk': (0.0, 0.419),
     'L0_xattn_bv': (0.0, 0.1),
     'L0_xattn_bp': (0.0, 0.1),
     'L1_xattn_b_q': (0.0, 0.1),
     'L1_xattn_b_k': (0.0, 0.8),
     'L1_xattn_b_v': (0.0, 0.1),
     'L1_xattn_b_o': (0.0, 0.1)}
    factors = {'L0_ffn_b1': 3.38}
    for name, (base, spread) in spreads.items():
        noise = np.random.default_rng([zlib.crc32(name.encode()), seed]).standard_normal(out[name].shape)
        drawn = base * np.exp(spread * noise) if base else spread * noise
        out[name] = jnp.asarray(drawn.astype(out[name].dtype))
    for name, factor in factors.items():
        out[name] = (out[name] * factor).astype(out[name].dtype)
    return out
```

```python
from contextlib import ExitStack

import numpy as np
import concourse.bass as bass
from concourse import mybir

F32 = mybir.dt.float32
BF16 = mybir.dt.bfloat16
I32 = mybir.dt.int32
U32 = mybir.dt.uint32
U16 = mybir.dt.uint16
U8 = mybir.dt.uint8
ALU = mybir.AluOpType
ACT = mybir.ActivationFunctionType
AX = mybir.AxisListType

P = 128
B, S, D = 4, 512, 256
HEADS, HD = 16, 16
NT = S // P
KT = D // P
HID = 1024
HT = HID // P
EXPERTS, EF, SF = 8, 256, 512
UNITS = EXPERTS + 1
EPS = 1e-5
BIG = 1e30
LOWEST = -3e38
SCALE = HD ** -0.5
VW = HD + 1

PARTS = 6 * HD
MAX_K = PARTS + 1
ST_K = MAX_K + 3
Q_PART = [0, 1, 2, 0, 1, 0]
K_PART = [0, 0, 0, 1, 1, 2]
ITEMS = 4
FILLS = (6 + 6 + 1, 6 + 6)
CONSTS = 8
LN_LINKS, GATE_LINKS = 21, 20
LAG = 6
EARLY = 10
STEPS = 16


def unit_tiles(e):
    return (SF if e == 0 else EF) // P


def unit_start(e):
    return sum(unit_tiles(j) for j in range(e))


TILES = unit_start(UNITS)


def plan_layer(masked):
    rot = not masked
    prep = {2: [("LN", 0)], 3: [("T", 0), ("T", 1)], 4: [("J", 0)], 5: [("J", 1)], 6: [("H", 0)],
            7: [("D", 0), ("H", 1)], 8: [("D", 1)], 9: [("J", 2)], 10: [("J", 3)],
            11: [("H", 2)], 12: [("D", 2), ("H", 3)], 13: [("D", 3)]}
    if rot:
        for at, k in ((5, 0), (6, 1), (10, 2), (11, 3)):
            prep[at] = [("R", k)] + prep[at] if at in (6, 11) else prep[at] + [("R", k)]
        prep[6] = [("H", 0), ("R", 1)]
        prep[11] = [("H", 2), ("R", 3)]
    else:
        for at, k in ((8, 0), (10, 1), (11, 2), (12, 3)):
            prep[at] = prep.get(at, []) + [("C", k)]
        prep[12] = [("C", 3)]
        prep[13] = [("C", 4), ("H", 2)]
        prep[14] = [("D", 2), ("H", 3)]
        prep[15] = [("D", 3)]
        prep[11] = [("C", 2)]

    plan = [(kind, 0, k) for v in sorted(prep) for kind, k in prep[v]]
    plan += [("F", 0, 0), ("F", 0, 1), ("V", 0, 0), ("V", 0, 1)]
    for q in range(2 - EARLY, B * STEPS + 5):
        if -LAG <= q < 0:
            plan.append(("MAX", 0, q + LAG))
        elif 0 <= q < B * STEPS:
            plan.append(("STEP", q // STEPS, q % STEPS))
        if q == B * STEPS:
            plan.append(("PV", B - 1, STEPS - 1))
        done = q + LAG - 1
        if 0 <= done < B * STEPS and done % 4 == 3:
            plan.append(("M", done // STEPS, done % STEPS // 4))
        if q >= 4 and q % 4 == 0 and q <= B * STEPS:
            plan.append(("E", (q - 1) // STEPS, (q - 1) % STEPS // 4))
        if q >= 5 and q % 4 == 1 and q <= B * STEPS + 1:
            plan.append(("OT", (q - 2) // STEPS, (q - 2) % STEPS // 4))
        n, s = q // STEPS, q % STEPS
        if n >= 1:
            plan += {2: [("OF", n - 1, 0), ("OF", n - 1, 1)], 3: [("OP", n - 1, 0)], 4: [("OP", n - 1, 1)]}.get(s, [])
        if n + 1 < B and q >= 0 and s in (13, 14):
            plan.append(("V", n + 1, s - 13))
        if 0 <= q and n + 2 < B:
            plan += [(kind, n + 2, k) for kind, k in prep.get(s, [])]
        plan += [(kind, 1, k) for kind, k in prep.get(q + EARLY, [])]
        if n >= 1 and n + 1 < B and s in (0, 2):
            plan.append(("F", n + 1, s // 2))
        if q in (6, 7):
            plan.append(("F", 1, q - 6))
    return plan


def bass_flamingo(nc, d, out):
    ctx = ExitStack()
    with ctx:
        def sb(name, shape, dt=F32):
            return ctx.enter_context(nc.sbuf_tensor(name, shape, dt))

        def sem(name):
            return ctx.enter_context(nc.semaphore(name))

        x = sb("x_tok", [P, B * NT, D])
        big = sb("operands", [P, 2 * 2 * HEADS * S], BF16)
        q_op = big[:, 0:2 * HEADS * S].rearrange("p (s h n) -> p s h n", s=2, h=HEADS)
        k_op = big[:, 2 * HEADS * S:].rearrange("p (s h n) -> p s h n", s=2, h=HEADS)
        probs = sb("probs", [P, 2, 4, S])
        parts = sb("parts", [P, ITEMS, 3, S], BF16)
        ctx_k = sb("ctx_k", [P, KT, S])
        ctx_v = sb("ctx_v", [P, KT, S])
        xn = sb("xn", [P, NT, D])
        xnT = sb("xnT", [P, KT, S])
        f = sb("f", [P, ITEMS, S])
        rotated = sb("rotated", [P, S])
        rest = sb("rest", [P, S])
        values = sb("values", [P, 2, NT, HEADS, VW])
        v_tmp = sb("v_tmp", [P, 2, D])
        o_tok = sb("o_tok", [P, NT, D])
        o_heads = sb("o_heads", [P, 2, S])
        o_feat = sb("o_feat", [P, KT, S])
        w_att = sb("w_att", [P, 4, KT, D])
        bqk = sb("bqk", [P, 2, ITEMS])
        bv_bc = sb("bv_bc", [P, D])
        bo_bc = sb("bo_bc", [P, D])
        tables = sb("tables", [P, 2, S])
        cos_t, sin_t = tables[:, 0, :], tables[:, 1, :]
        rot_m = sb("rot_m", [P, P])
        ident = sb("ident", [P, P])
        ident_b = sb("ident_b", [P, P], BF16)
        ones_b = sb("ones_b", [P, P], BF16)
        gates = sb("gates", [P, 4])
        tanhg = sb("tanhg", [P, 4])
        km8 = sb("km8", [P, B * NT], U8)
        key_on = sb("key_on", [P, B * NT])
        tok_gate = sb("tok_gate", [P, B * NT])
        mrow8 = sb("mrow8", [1, S], U8)
        mask_row = sb("mask_row", [1, S], BF16)
        stats = sb("stats", [P, NT, 6])
        mv = sb("mv", [P, NT, 2])
        nw = sb("nw", [P, 4, NT])
        max_q = sb("max_q", [P, HEADS * NT])
        m_rest = sb("m_rest", [4 * NT, 2, P])
        m_parts = sb("m_parts", [4 * NT, 2, 3, P], BF16)
        rec = sb("rec", [P, NT, 4])
        upd = v_tmp
        m_stage = sb("m_stage", [P, 2, S], I32)
        rot_tmp = m_stage[:, 0, :].bitcast(F32)
        m_on = sb("m_on", [P, NT, S], BF16)
        m_add_q = sb("m_add_q", [P, 2, NT, S], BF16)
        m_add_k = sb("m_add_k", [P, 3, NT, S], BF16)
        row_any = sb("row_any", [P, 2, NT])
        any_bc, any_big = tables[:, 0, :], tables[:, 1, :]
        junk = v_tmp[:, 0, :].bitcast(BF16)

        ps = ctx.enter_context(nc.psum_tensor("ps", [P, 8, S], F32))
        ST_BANK, MAX_BANK, PV_BANK, A_BANK, B_BANK = (0, 1, 2), (3, 4), 5, 6, 7

        x_in = [sem(f"x_in{n}") for n in range(B)]
        const_in = sem("const_in")
        w_in = sem("w_in")
        const_ok = sem("const_ok")
        gate_ok = sem("gate_ok")
        chain = sem("dve_chain")
        ln_done = sem("ln_done")
        a_filled, a_drained = sem("a_filled"), sem("a_drained")
        b_filled, b_drained = sem("b_filled"), sem("b_drained")
        ctxk_in, ctxv_in = sem("ctxk_in"), sem("ctxv_in")
        hi_done, mid_done = sem("hi_done"), sem("mid_done")
        rest_done, split_done = sem("rest_done"), sem("split_done")
        spill = [sem(f"spill{i}") for i in range(ITEMS)]
        slot_in = [[sem(f"slot_in{i}{h}") for h in range(2)] for i in range(2)]
        maxrow_in = [sem(f"maxrow_in{i}") for i in range(2)]
        maskrow = sem("maskrow")
        mrow_in = sem("mrow_in")
        max_filled, max_drained = sem("max_filled"), sem("max_drained")
        st_filled, exp_done = sem("st_filled"), sem("exp_done")
        pv_done, heads_out = sem("pv_done"), sem("heads_out")
        v_ready = sem("v_ready")
        m_split = sem("m_split")
        key_ok = sem("key_ok")
        x_upd = sem("x_upd")
        mstage_in = sem("mstage_in")
        m_stage_free = sem("m_stage_free")
        rows_in = sem("rows_in")
        out_done = sem("out_done")
        m_ready = sem("m_ready")

        plans = [[(l, *e) for e in plan_layer(masked=l == 1)] for l in range(2)]
        plan = plans[0] + plans[1]
        a_order = {e: j + 1 for j, e in enumerate(e for e in plan if e[1] in ("T", "J", "OF"))}
        b_order = {e: j + 1 for j, e in enumerate(e for e in plan if e[1] in ("R", "V", "M", "OT", "OP") or e[1:4:2] == ("C", 4))}
        A_END, B_END = [], []
        for l in range(2):
            A_END.append(max(v for e, v in a_order.items() if e[0] == l))
            B_END.append(max(v for e, v in b_order.items() if e[0] == l))

        scratch = nc.dram_tensor("qk_parts", [2 * B * ITEMS, 8, HD, 3, S], BF16, kind="Internal").ap()

        def batch(l, n):
            return l * B + n

        ff = [dict((k, sem(f"ff{l}_{k}")) for k in (
            "ln", "t_filled", "t_drained", "u_filled", "u_drained", "h_ready", "d_filled", "d_drained",
            "w_in", "w_ok", "r_filled", "g_diff", "g_exp", "gate", "x_done")) for l in range(2)]
        FROM_ONE = {"pe": ("t_filled", "d_filled"), "act": ("t_drained", "u_drained"), "dve": ("d_drained", "gate")}

        def count_from_one(eng, who):
            for l in range(2):
                for k in FROM_ONE[who]:
                    eng.sem_inc(ff[l][k], 1)

        alpha_ok = sem("alpha_ok")
        w2_sums = sem("w2_sums")
        stood = sem("stood")
        chain0, chain1 = sem("dve_chain_ff0"), sem("dve_chain_ff1")

        U_BANK, D_BANK, T_BANK, R_BANK = (0, 1, 2, 3), (4, 5), 6, 7

        fview = big[:, :].bitcast(F32)
        hid = fview[:, 0:HT * S].rearrange("p (t n) -> p t n", t=HT)
        hid_e = fview[:, 0:2 * 4 * S].rearrange("p (b t n) -> p b t n", b=2, t=4)
        w1_s = fview[:, 4096:4096 + KT * HID].rearrange("p (k n) -> p k n", k=KT)
        w2_s = fview[:, 6144:6144 + HT * D].rearrange("p (k n) -> p k n", k=HT)
        w1_n = fview[:, 8192:8192 + HT * D].rearrange("p (k n) -> p k n", k=HT)
        w1_abs = fview[:, 10240:10240 + HT * D].rearrange("p (k n) -> p k n", k=HT)
        w2_abs = fview[:, 12288:12288 + HT * D].rearrange("p (k n) -> p k n", k=HT)
        we1 = fview[:, 4096:4096 + EXPERTS * KT * EF].rearrange("p (e k n) -> p e k n", e=EXPERTS, k=KT)
        we2 = fview[:, 8192:8192 + EXPERTS * KT * D].rearrange("p (e k n) -> p e k n", e=EXPERTS, k=KT)
        ws1 = fview[:, 12288:12288 + KT * SF].rearrange("p (k n) -> p k n", k=KT)
        ws2 = fview[:, 13312:13312 + 4 * D].rearrange("p (k n) -> p k n", k=4)
        alpha1 = sb("alpha1", [P, HT])
        b1_col = sb("b1_col", [P, HT])
        alpha2 = fview[:, 14336:14336 + D]
        b2_bc = fview[:, 14336 + D:14336 + 2 * D]
        w_rt = sb("w_rt", [P, KT, EXPERTS])
        logit = sb("logit", [P, NT, EXPERTS])
        top = sb("top", [P, NT, 8])
        top_i = sb("top_i", [P, NT, 8], U32)
        top_f = sb("top_f", [P, NT, 2])
        g_w = sb("g_w", [P, NT, 4])
        hot = sb("hot", [P, 2, EXPERTS])
        gate = sb("gate", [P, NT, UNITS])
        iota_e = sb("iota_e", [P, EXPERTS])
        ones_f = sb("ones_f", [P, HEADS])

        block = ctx.enter_context(nc.Block())

        @block.sync
        def _(sp):
            def load(dst, src, s):
                sp.dma_start(dst, src).then_inc(s, 16)

            def load_weights(l):
                if l:
                    sp.wait_ge(b_drained, B_END[0])
                    sp.wait_ge(x_upd, 2 * B)
                for j, w in enumerate(("wq", "wk", "wv", "wo")):
                    load(w_att[:, j, :, :], d[f"l{l}_{w}"].rearrange("(k p) n -> p k n", p=P), w_in)
                load(bqk[:, l, :], d[f"l{l}_bqk"], w_in)
                load(bv_bc[:, :], d[f"l{l}_bv"].partition_broadcast(P), w_in)
                load(bo_bc[:, :], d[f"l{l}_bo"].partition_broadcast(P), w_in)

            def load_ctx(dst, n, s):
                load(dst[:, :, :], d["ctxT"][n].rearrange("(k p) n -> p k n", p=P), s)

            def ctx_k_load(l, n):
                if batch(l, n):
                    pl, pn = divmod(batch(l, n) - 1, B)
                    sp.wait_ge(a_filled, a_order[(pl, "J", pn, 1)])
                load_ctx(ctx_k, n, ctxk_in)

            def ctx_v_load(l, n):
                if batch(l, n):
                    pl, pn = divmod(batch(l, n) - 1, B)
                    sp.wait_ge(b_filled, b_order[(pl, "V", pn, 1)])
                load_ctx(ctx_v, n, ctxv_in)

            def mask_load(n, j):
                if n or j:
                    sp.wait_ge(m_stage_free, 4 * n + j)
                else:
                    sp.wait_ge(b_drained, B_END[0])
                src = d["mask_q"] if j < 2 else d["mask_k"]
                h = j % 2
                load(m_stage[:, :, :], src[n].rearrange("(t p) k -> p t k", p=P)[:, 2 * h:2 * h + 2, :], mstage_in)

            def spill_parts(g, k):
                sp.wait_ge(split_done, ITEMS * g + k + 1)
                load(scratch[ITEMS * g + k].rearrange("h d j n -> (h d) j n"), parts[:, k, :, :], spill[k])

            def fill_slot(g, half):
                sl = g % 2
                if g >= 2:
                    sp.wait_ge(st_filled, 64 * (g - 1))
                arrives = slot_in[sl][half]
                if half == 0:
                    sp.wait_ge(maskrow, g + 1)
                    load(k_op[PARTS:PARTS + 1, sl, :, :], mask_row[:, :].unsqueeze(1).to_broadcast([1, HEADS, S]), arrives)
                for item, operand, order in ((half, k_op, K_PART), (2 + half, q_op, Q_PART)):
                    sp.wait_ge(spill[item], 16 * (g + 1))
                    src = scratch[ITEMS * g + item]
                    for b, j in enumerate(order):
                        load(operand[b * HD:(b + 1) * HD, sl, 8 * half:8 * half + 8, :],
                             src[:, :, j, :].rearrange("h d n -> d h n"), arrives)

            def fill_max_rows(g, gg):
                mg = 4 * g + gg
                sp.wait_ge(m_split, mg + 1)
                for j in range(3):
                    r = MAX_K + j
                    load(q_op[r:r + 1, g % 2, 4 * gg:4 * gg + 4, :].rearrange("p h (t n) -> p (h t) n", n=P),
                         m_parts[:, mg % 2, j, :], maxrow_in[mg % 2])

            def row_mask(l, n):
                g = batch(l, n)
                if g:
                    sp.wait_ge(maskrow, g)
                load(mrow8[:, :], d["mask_row"][n:n + 1, :], mrow_in)

            load(x[:, 0:NT, :], d["x"][0].rearrange("(t p) n -> p t n", p=P), x_in[0])
            load(ident[:, :], d["ident"], const_in)
            load(rot_m[:, :], d["rot"], const_in)
            load(cos_t, d["cosT"], const_in)
            load(sin_t, d["sinT"], const_in)
            load(gates[:, 0:2], d["g_xattn"].partition_broadcast(P), const_in)
            load(gates[:, 2:4], d["g_ffn"].partition_broadcast(P), const_in)
            load(km8[:, :], d["mask_col"], const_in)
            load(iota_e[:, :], d["iota"].partition_broadcast(P), const_in)
            load_weights(0)
            ctx_k_load(0, 0)
            for n in range(1, B):
                load(x[:, n * NT:(n + 1) * NT, :], d["x"][n].rearrange("(t p) n -> p t n", p=P), x_in[n])

            for l in range(2):
                if l:
                    load_weights(1)
                    mask_load(0, 0)
                    sp.wait_ge(ff[0]["x_done"], 2 * B)
                load(q_op[PARTS:MAX_K, :, :, :].bitcast(U16), d["ones_row"][0:1], rows_in)
                load(k_op[PARTS:ST_K, :, :, :].bitcast(U16), d["ones_row"], rows_in)
                sp.wait_ge(rows_in, 32 * (l + 1))
                ctx_v_load(l, 0)
                for _, kind, n, k in plans[l]:
                    g = batch(l, n)
                    if kind == "LN":
                        if g:
                            ctx_k_load(l, n)
                    if kind == "J" and k == 2:
                        row_mask(l, n)
                    if kind == "C" and k < 4 and (k < 3 or n + 1 < B):
                        mask_load(n + (k == 3), (k + 1) % 4)
                    if kind == "D":
                        spill_parts(g, k)
                    if kind == "F":
                        fill_slot(g, k)
                    if kind == "M":
                        fill_max_rows(g, k)
                    if kind == "V" and k == 1 and n + 1 < B:
                        ctx_v_load(l, n + 1)
                sp.wait_ge(st_filled, 64 * B * (l + 1))
                w = ff[l]["w_in"]
                if l == 0:
                    load(w1_s, d["w1T"].rearrange("(k p) n -> p k n", p=P), w)
                    load(w1_n, d["w1"].rearrange("(k p) n -> p k n", p=P), w)
                    load(w2_s, d["w2T"].rearrange("(k p) n -> p k n", p=P), w)
                    load(b1_col[:, :], d["b1"], w)
                    load(b2_bc[:, :], d["b2"].partition_broadcast(P), w)
                else:
                    load(w_rt[:, :, :], d["w_router"].rearrange("(k p) n -> p k n", p=P), w)
                    load(ws1, d["ws1T"].rearrange("(k p) n -> p k n", p=P), w)
                    load(ws2, d["ws2T"].rearrange("(k p) n -> p k n", p=P), w)
                    load(we1, d["we1T"].rearrange("e (k p) n -> p (e k) n", p=P), w)
                    load(we2, d["we2T"].rearrange("e (k p) n -> p (e k) n", p=P), w)
            with sp.Fori(0, B) as n:
                sp.wait_ge(ff[1]["d_drained"], 1 + n * 2 * UNITS + 2 * UNITS)
                sp.dma_start(out[bass.ds(n, 1), :, :].rearrange("a (t p) n -> p (a t) n", p=P),
                             x[:, bass.ds(n * NT, NT), :]).then_inc(out_done, 16)
            sp.wait_ge(out_done, 16 * B)

        @block.gpsimd
        def _(pool):
            pool.memset(ones_b[:, :], 1.0).then_inc(const_ok, 1)
            pool.memset(ones_f[:, :], 1.0).then_inc(const_ok, 1)
            pool.wait_ge(const_in, 16 * CONSTS)
            pool.tensor_copy(ident_b[:, :], ident[:, :]).then_inc(const_ok, 1)

            def attention(l):
                for _, kind, n, k in plans[l]:
                    g = batch(l, n)
                    item = ITEMS * g + k
                    if kind == "H":
                        src = f[:, k, :] if l == 1 and k < 2 else rotated[:, :]
                        pool.wait_ge(hi_done, item + 1)
                        if item:
                            pool.wait_ge(mid_done, item)
                            pool.wait_ge(split_done, item)
                        pool.tensor_tensor(rest[:, :], src, parts[:, k, 0, :], ALU.subtract).then_inc(rest_done, 1)
                    if kind == "D":
                        pool.wait_ge(mid_done, item + 1)
                        pool.wait_ge(rest_done, item + 1)
                        pool.tensor_tensor(parts[:, k, 2, :], rest[:, :], parts[:, k, 1, :],
                                           ALU.subtract).then_inc(split_done, 1)

            attention(0)
            attention(1)
            s = ff[1]
            with pool.Fori(0, B) as n:
                for e in range(UNITS):
                    for t in range(unit_tiles(e)):
                        o = unit_start(e) + t
                        pool.wait_ge(s["u_drained"], 1 + n * TILES + o + 1)
                        h = hid_e[:, e % 2, t, :]
                        pool.tensor_tensor(h, h, h, ALU.mult).then_inc(s["h_ready"], 1)

        @block.scalar
        def _(act):
            count_from_one(act, "act")
            act.wait_ge(const_in, 16 * CONSTS)
            act.activation(tanhg[:, :], gates[:, :], ACT.Tanh).then_inc(gate_ok, 1)

            def attention(l):
                for e in plans[l]:
                    _, kind, n, k = e
                    g = batch(l, n)
                    if kind == "T":
                        act.wait_ge(a_filled, a_order[e])
                        act.copy(xnT[:, k, :], ps[:, A_BANK, :]).then_inc(a_drained, 1)
                    if kind == "J":
                        act.wait_ge(a_filled, a_order[e])
                        if g:
                            act.wait_ge(split_done, ITEMS * (g - 1) + k + 1)
                        act.activation(f[:, k, :], ps[:, A_BANK, :], ACT.Identity,
                                       bias=bqk[:, l, k:k + 1]).then_inc(a_drained, 1)
                    if kind == "STEP":
                        G = STEPS * g + k
                        for j in range(4):
                            o = 4 * G + j
                            act.wait_ge(st_filled, o + 1)
                            if G >= 2 and j == 0:
                                act.wait_ge(pv_done, G - 1)
                            act.activation(probs[:, G % 2, j, :], ps[:, ST_BANK[o % 3], :], ACT.Exp,
                                           scale=SCALE).then_inc(exp_done, 1)
                    if kind == "E":
                        act.wait_ge(pv_done, STEPS * g + 4 * k + 4)
                        if 4 * g + k >= 2:
                            pl, pn = divmod((4 * g + k - 2) // 4, B)
                            act.wait_ge(b_filled, b_order[(pl, "OT", pn, (k - 2) % 4)])
                        act.copy(o_heads[:, k % 2, :], ps[:, PV_BANK, :]).then_inc(heads_out, 1)
                    if kind == "OF":
                        act.wait_ge(a_filled, a_order[e])
                        if g:
                            pl, pn = divmod(g - 1, B)
                            act.wait_ge(b_filled, b_order[(pl, "OP", pn, 1)])
                        act.copy(o_feat[:, k, :], ps[:, A_BANK, :]).then_inc(a_drained, 1)

            def transposed(s, n):
                for k in range(KT):
                    act.wait_ge(s["t_filled"], 1 + n * KT + k + 1)
                    act.copy(xnT[:, k, :], ps[:, T_BANK, :]).then_inc(s["t_drained"], 1)

            def gelu(n):
                s = ff[0]
                for t in range(HT):
                    act.wait_ge(s["u_filled"], n * HT + t + 1)
                    if t == 0:
                        act.wait_ge(s["d_filled"], 1 + n * 2)
                    act.activation(hid[:, t, :], ps[:, U_BANK[t % 4], :], ACT.Gelu, bias=b1_col[:, t:t + 1],
                                   scale=alpha1[:, t:t + 1]).then_inc(s["u_drained"], 1)

            attention(0)
            s = ff[0]
            act.wait_ge(s["w_in"], 16 * 5)
            act.activation(w2_abs, w2_s, ACT.Abs).then_inc(s["w_ok"], 1)
            act.activation(w1_s, w1_s, ACT.Sign).then_inc(s["w_ok"], 1)
            act.wait_ge(s["w_ok"], 1)
            act.activation(w2_s, w2_s, ACT.Sign).then_inc(s["w_ok"], 1)
            act.wait_ge(alpha_ok, 1)
            transposed(s, 0)
            with act.Fori(0, B - 1) as n:
                gelu(n)
                transposed(s, n + 1)
            gelu(B - 1)

            attention(1)
            s = ff[1]
            transposed(s, 0)

            def rectify(n, e):
                for t in range(unit_tiles(e)):
                    o = unit_start(e) + t
                    act.wait_ge(s["u_filled"], n * TILES + o + 1)
                    if t == 0:
                        act.wait_ge(s["d_filled"], 1 + n * 2 * UNITS + max(0, 2 * (e - 1)))
                    act.activation(hid_e[:, e % 2, t, :], ps[:, U_BANK[o % 4], :],
                                   ACT.Relu).then_inc(s["u_drained"], 1)

            def second_weight(n):
                act.wait_ge(s["g_diff"], n * 1 + 1)
                act.activation(g_w[:, :, 1:2], g_w[:, :, 0:1], ACT.Exp).then_inc(s["g_exp"], 1)

            second_weight(0)
            with act.Fori(0, B - 1) as n:
                for e in range(UNITS):
                    rectify(n, e)
                transposed(s, n + 1)
                second_weight(n + 1)
            for e in range(UNITS):
                rectify(B - 1, e)

        @block.tensor
        def _(pe):
            def bank_a(e):
                if a_order[e] > 1:
                    pe.wait_ge(a_drained, a_order[e] - 1)
                return ps[:, A_BANK, :]

            def bank_b(e):
                if b_order[e] > 1:
                    pe.wait_ge(b_drained, b_order[e] - 1)
                return ps[:, B_BANK, :]

            def max_scores(l, q, qt):
                g, s = l * B + q // STEPS, q % STEPS
                o, sl = 64 * g + 4 * s + qt, g % 2
                if s % 8 == 0 and qt == 0:
                    pe.wait_ge(slot_in[sl][s // 8], 16 * FILLS[s // 8] * (g // 2 + 1))
                if o >= 2:
                    pe.wait_ge(max_drained, o - 1)
                pe.matmul(ps[:, MAX_BANK[o % 2], :], q_op[0:MAX_K, sl, s, qt * P:(qt + 1) * P],
                          k_op[0:MAX_K, sl, s, :], start=True, stop=True).then_inc(max_filled, 1)

            def scores(l, g, s, j):
                o, sl, h, kt = 64 * g + 4 * s + j, g % 2, 4 * (s // 4) + j, s % 4
                if kt == 0 and j == 0:
                    mg = 4 * g + s // 4
                    pe.wait_ge(maxrow_in[mg % 2], 48 * (mg // 2 + 1))
                    if l and s == 0:
                        pe.wait_ge(m_ready, g - B + 1)
                if o >= 3:
                    pe.wait_ge(exp_done, o - 2)
                mm = pe.matmul(ps[:, ST_BANK[o % 3], :], k_op[0:ST_K, sl, h, kt * P:(kt + 1) * P],
                               q_op[0:ST_K, sl, h, :], start=True, stop=(l == 0))
                if l:
                    mm = pe.matmul(ps[:, ST_BANK[o % 3], :], ident_b[:, :], m_add_k[:, g % 3, kt, :],
                                   start=False, stop=True)
                mm.then_inc(st_filled, 1)

            def value_product(g, s):
                G, kt = STEPS * g + s, s % 4
                if s == 0:
                    pe.wait_ge(v_ready, g + 1)
                pe.wait_ge(exp_done, 4 * G + 4)
                if kt == 0 and G:
                    pe.wait_ge(heads_out, G // 4)
                for j in range(4):
                    mm = pe.matmul(ps[32 * j:32 * j + VW, PV_BANK, :], values[:, g % 2, kt, 4 * (s // 4) + j, :],
                                   probs[:, G % 2, j, :], start=(kt == 0), stop=(kt == 3))
                mm.then_inc(pv_done, 1)

            def attention(l):
                for e in plans[l]:
                    _, kind, n, k = e
                    g = batch(l, n)
                    if kind == "T":
                        bank = bank_a(e)
                        pe.wait_ge(ln_done, g + 1)
                        for t in range(NT):
                            mm = pe.transpose(bank[:, t * P:(t + 1) * P], xn[:, t, k * P:(k + 1) * P], ident[:, :])
                        mm.then_inc(a_filled, 1)
                    if kind == "C" and k == 4:
                        bank = bank_b(e)
                        pe.wait_ge(m_stage_free, 4 * n + 4)
                        for t in range(NT):
                            mm = pe.matmul(bank, ones_b[:, :], m_on[:, t, :], start=(t == 0), stop=(t == NT - 1))
                        mm.then_inc(b_filled, 1)
                    if kind == "J":
                        bank = bank_a(e)
                        if k == 0:
                            pe.wait_ge(w_in, 16 * 7 * (l + 1))
                            pe.wait_ge(ctxk_in, 16 * (g + 1))
                        if k == 2:
                            pe.wait_ge(a_drained, a_order[(l, "T", n, 1)])
                        src, w, ft = (xnT if k >= 2 else ctx_k), 1 - k // 2, k % 2
                        for c in range(KT):
                            mm = pe.matmul(bank, w_att[:, w, c, ft * P:(ft + 1) * P], src[:, c, :],
                                           start=(c == 0), stop=(c == KT - 1))
                        mm.then_inc(a_filled, 1)
                    if kind == "R":
                        bank = bank_b(e)
                        pe.wait_ge(a_drained, a_order[(l, "J", n, k)])
                        pe.matmul(bank, rot_m[:, :], f[:, k, :], start=True, stop=True).then_inc(b_filled, 1)
                    if kind == "MAX":
                        for qt in range(NT):
                            max_scores(l, k, qt)
                    if kind == "M":
                        bank = bank_b(e)
                        pe.wait_ge(max_drained, 64 * g + 16 * (k + 1))
                        pe.transpose(bank[0:4 * NT, 0:P], max_q[:, 16 * k:16 * k + 16], ident[:, :]).then_inc(b_filled, 1)
                    if kind == "V":
                        bank = bank_b(e)
                        pe.wait_ge(ctxv_in, 16 * (g + 1))
                        for t in range(2):
                            tok = (2 * k + t) * P
                            for c in range(KT):
                                mm = pe.matmul(bank[:, t * D:(t + 1) * D], ctx_v[:, c, tok:tok + P],
                                               w_att[:, 2, c, :], start=(c == 0), stop=(c == KT - 1))
                        mm.then_inc(b_filled, 1)
                    if kind == "STEP":
                        q = STEPS * n + k
                        ahead = q + LAG
                        has_max = ahead < B * STEPS
                        scores(l, g, k, 0)
                        scores(l, g, k, 1)
                        if has_max:
                            max_scores(l, ahead, 0)
                        scores(l, g, k, 2)
                        if has_max:
                            max_scores(l, ahead, 1)
                        if q:
                            value_product(l * B + (q - 1) // STEPS, (q - 1) % STEPS)
                        if has_max:
                            max_scores(l, ahead, 2)
                        scores(l, g, k, 3)
                        if has_max:
                            max_scores(l, ahead, 3)
                    if kind == "PV":
                        value_product(g, k)
                    if kind == "OT":
                        bank = bank_b(e)
                        pe.wait_ge(heads_out, 4 * g + k + 1)
                        for t in range(NT):
                            mm = pe.transpose(bank[:, t * P:(t + 1) * P], o_heads[:, k % 2, t * P:(t + 1) * P],
                                              ident[:, :])
                        mm.then_inc(b_filled, 1)
                    if kind == "OF":
                        bank = bank_a(e)
                        pe.wait_ge(b_drained, b_order[(l, "OT", n, 3)])
                        for t in range(NT):
                            mm = pe.transpose(bank[:, t * P:(t + 1) * P], o_tok[:, t, k * P:(k + 1) * P], ident[:, :])
                        mm.then_inc(a_filled, 1)
                    if kind == "OP":
                        bank = bank_b(e)
                        pe.wait_ge(a_drained, a_order[(l, "OF", n, 1)])
                        for t in range(2):
                            tok = (2 * k + t) * P
                            for c in range(KT):
                                mm = pe.matmul(bank[:, t * D:(t + 1) * D], o_feat[:, c, tok:tok + P],
                                               w_att[:, 3, c, :], start=(c == 0), stop=(c == KT - 1))
                        mm.then_inc(b_filled, 1)

            def leave_attention(l):
                pe.wait_ge(a_drained, A_END[l])
                pe.wait_ge(b_drained, B_END[l])
                pe.wait_ge(exp_done, 64 * B * (l + 1))
                pe.wait_ge(max_drained, 64 * B * (l + 1))
                pe.wait_ge(heads_out, 4 * B * (l + 1))

            def tokens(s, n):
                pe.wait_ge(s["ln"], n * 1 + 1)
                for k in range(KT):
                    pe.wait_ge(s["t_drained"], 1 + n * KT + k)
                    for t in range(NT):
                        mm = pe.transpose(ps[:, T_BANK, t * P:(t + 1) * P], xn[:, t, k * P:(k + 1) * P], ident[:, :])
                    mm.then_inc(s["t_filled"], 1)

            def up0(n):
                s = ff[0]
                pe.wait_ge(s["t_drained"], 1 + n * KT + KT)
                for t in range(HT):
                    pe.wait_ge(s["u_drained"], 1 + n * HT + max(0, t - 3))
                    for c in range(KT):
                        mm = pe.matmul(ps[:, U_BANK[t % 4], :], w1_s[:, c, t * P:(t + 1) * P], xnT[:, c, :],
                                       start=(c == 0), stop=(c == KT - 1))
                    mm.then_inc(s["u_filled"], 1)

            def down0(n):
                s = ff[0]
                pe.wait_ge(s["u_drained"], 1 + n * HT + HT)
                for half in range(2):
                    pe.wait_ge(s["d_drained"], 1 + n * 2)
                    for t in range(2):
                        tok = (2 * half + t) * P
                        for c in range(HT):
                            mm = pe.matmul(ps[:, D_BANK[half], t * D:(t + 1) * D], hid[:, c, tok:tok + P],
                                           w2_s[:, c, :], start=(c == 0), stop=(c == HT - 1))
                    mm.then_inc(s["d_filled"], 1)

            count_from_one(pe, "pe")
            pe.wait_ge(const_in, 16 * CONSTS)
            pe.wait_ge(const_ok, 3)
            attention(0)

            leave_attention(0)
            s = ff[0]
            pe.wait_ge(s["w_ok"], 1)
            for c in range(HT):
                mm = pe.matmul(ps[:, D_BANK[0], 0:D], ones_f[:, 0:1].to_broadcast([P, P]), w2_abs[:, c, :], start=(c == 0), stop=(c == HT - 1))
            mm.then_inc(w2_sums, 1)
            tokens(s, 0)
            pe.wait_ge(s["w_ok"], 3)
            pe.wait_ge(alpha_ok, 2)
            with pe.Fori(0, B - 1) as n:
                up0(n)
                tokens(s, n + 1)
                down0(n)
            up0(B - 1)
            down0(B - 1)

            pe.wait_ge(s["u_drained"], 1 + HT * B)
            pe.wait_ge(s["d_drained"], 1 + 2 * B)
            pe.wait_ge(s["t_drained"], 1 + KT * B)
            attention(1)

            leave_attention(1)
            s = ff[1]

            def route(n):
                pe.wait_ge(s["t_drained"], 1 + n * KT + KT)
                pe.wait_ge(s["gate"], 1 + n * 1)
                for t in range(NT):
                    for c in range(KT):
                        mm = pe.matmul(ps[:, R_BANK, t * EXPERTS:(t + 1) * EXPERTS], xnT[:, c, t * P:(t + 1) * P],
                                       w_rt[:, c, :], start=(c == 0), stop=(c == KT - 1))
                mm.then_inc(s["r_filled"], 1)

            def up1(n, e):
                for t in range(unit_tiles(e)):
                    o = unit_start(e) + t
                    pe.wait_ge(s["u_drained"], 1 + n * TILES + max(0, o - 3))
                    for c in range(KT):
                        w = ws1[:, c, t * P:(t + 1) * P] if e == 0 else we1[:, e - 1, c, t * P:(t + 1) * P]
                        mm = pe.matmul(ps[:, U_BANK[o % 4], :], w, xnT[:, c, :], start=(c == 0), stop=(c == KT - 1))
                    mm.then_inc(s["u_filled"], 1)

            def down1(n, e):
                pe.wait_ge(s["h_ready"], n * TILES + unit_start(e) + unit_tiles(e))
                for half in range(2):
                    pe.wait_ge(s["d_drained"], 1 + n * 2 * UNITS + max(0, 2 * e + half - 1))
                    for t in range(2):
                        tok, last = (2 * half + t) * P, unit_tiles(e) - 1
                        for c in range(unit_tiles(e)):
                            w = ws2[:, c, :] if e == 0 else we2[:, e - 1, c, :]
                            mm = pe.matmul(ps[:, D_BANK[half], t * D:(t + 1) * D], hid_e[:, e % 2, c, tok:tok + P],
                                           w, start=(c == 0), stop=(c == last))
                    mm.then_inc(s["d_filled"], 1)

            tokens(s, 0)
            pe.wait_ge(s["w_in"], 16 * 5)
            route(0)

            def experts(n, last):
                up1(n, 0)
                for e in range(1, UNITS):
                    up1(n, e)
                    down1(n, e - 1)
                if not last:
                    tokens(s, n + 1)
                    route(n + 1)
                down1(n, UNITS - 1)

            with pe.Fori(0, B - 1) as n:
                experts(n, False)
            experts(B - 1, True)

        @block.vector
        def _(dve):
            links = [0]

            def link(ins):
                links[0] += 1
                ins.then_inc(chain, 1)
                dve.wait_ge(chain, links[0])

            def stand():
                dve.sem_inc(stood, 1)

            def layer_norm(rows, count):
                for t in range(NT):
                    last = dve.bn_stats(stats[:, t, :], rows[:, t, :])
                count(last)
                stand()
                for t in range(NT):
                    last = dve.bn_aggr(mv[:, t, :], stats[:, t, :])
                count(last)
                v, y, a = nw[:, 0, :], nw[:, 1, :], nw[:, 2, :]
                count(dve.tensor_scalar(v, mv[:, :, 1], EPS, None, ALU.add))
                count(dve.tensor_scalar(nw[:, 3, :].bitcast(I32), v.bitcast(I32), 1, None, ALU.arith_shift_right))
                count(dve.tensor_scalar(y.bitcast(I32), nw[:, 3, :].bitcast(I32), -1.0, float(0x5F3759DF),
                                        ALU.mult, ALU.add))
                for _ in range(4):
                    count(dve.tensor_tensor(a, y, y, ALU.mult))
                    count(dve.tensor_tensor(a, a, v, ALU.mult))
                    count(dve.tensor_scalar(a, a, -0.5, 1.5, ALU.mult, ALU.add))
                    count(dve.tensor_tensor(y, y, a, ALU.mult))
                for t in range(NT):
                    last = dve.tensor_scalar(xn[:, t, :], rows[:, t, :], mv[:, t, 0:1], nw[:, 1, t:t + 1],
                                             ALU.subtract, ALU.mult)
                return last

            def attention(l):
                for e in plans[l]:
                    _, kind, n, k = e
                    g = batch(l, n)
                    item = ITEMS * g + k
                    if kind == "LN":
                        if l == 0:
                            dve.wait_ge(x_in[n], 16)
                        else:
                            dve.wait_ge(ff[0]["x_done"], 2 * n + 2)
                        if n:
                            dve.wait_ge(a_filled, a_order[(l, "T", n - 1, 1)])
                        elif l:
                            dve.wait_ge(ff[0]["t_filled"], 1 + KT * B)
                        layer_norm(x[:, n * NT:(n + 1) * NT, :], link).then_inc(ln_done, 1)
                    if kind == "C":
                        mask_piece(e, n, k)
                    if kind == "R":
                        dve.wait_ge(b_filled, b_order[e])
                        if item:
                            dve.wait_ge(rest_done, item)
                        dve.tensor_tensor(rot_tmp, ps[:, B_BANK, :], sin_t, ALU.mult).then_inc(b_drained, 1)
                        link(dve.tensor_tensor(rotated[:, :], f[:, k, :], cos_t, ALU.mult))
                        dve.wait_ge(b_drained, b_order[e])
                        link(dve.tensor_tensor(rotated[:, :], rotated[:, :], rot_tmp, ALU.add))
                    if kind == "H":
                        dve.wait_ge(a_drained, a_order[(l, "J", n, k)])
                        if g:
                            dve.wait_ge(spill[k], 16 * g)
                        if l and k >= 2:
                            dve.wait_ge(rest_done, item)
                            link(dve.tensor_tensor(rotated[:, :], f[:, k, :], any_bc, ALU.mult))
                        src = f[:, k, :] if l and k < 2 else rotated[:, :]
                        dve.tensor_copy(parts[:, k, 0, :], src).then_inc(hi_done, 1)
                    if kind == "D":
                        dve.wait_ge(rest_done, item + 1)
                        dve.tensor_copy(parts[:, k, 1, :], rest[:, :]).then_inc(mid_done, 1)
                        if k == ITEMS - 1:
                            key_mask_row(l, g)
                    if kind == "MAX":
                        for qt in range(NT):
                            row_max(l, k, qt)
                    if kind == "STEP" and STEPS * n + k + LAG < B * STEPS:
                        for qt in range(NT):
                            row_max(l, STEPS * n + k + LAG, qt)
                    if kind == "M":
                        mg = 4 * g + k
                        dve.wait_ge(b_filled, b_order[e])
                        if mg >= 2:
                            dve.wait_ge(maxrow_in[mg % 2], 48 * (mg // 2))
                        dve.tensor_scalar(m_rest[:, 0, :], ps[0:4 * NT, B_BANK, 0:P], -1.0, None,
                                          ALU.mult).then_inc(b_drained, 1)
                        dve.wait_ge(b_drained, b_order[e])
                        part = m_parts[:, mg % 2, :, :]
                        link(dve.tensor_copy(part[:, 0, :], m_rest[:, 0, :]))
                        link(dve.tensor_tensor(m_rest[:, 1, :], m_rest[:, 0, :], part[:, 0, :], ALU.subtract))
                        link(dve.tensor_copy(part[:, 1, :], m_rest[:, 1, :]))
                        dve.tensor_tensor(part[:, 2, :], m_rest[:, 1, :], part[:, 1, :],
                                          ALU.subtract).then_inc(m_split, 1)
                        dve.wait_ge(m_split, mg + 1)
                    if kind == "V":
                        dve.wait_ge(b_filled, b_order[e])
                        if g >= 2 and k == 0:
                            dve.wait_ge(pv_done, STEPS * (g - 1))
                        junk_written()
                        dve.tensor_tensor(v_tmp[:, :, :], ps[:, B_BANK, :].rearrange("p (t n) -> p t n", t=2),
                                          bv_bc[:, :].unsqueeze(1).to_broadcast([P, 2, D]), ALU.add).then_inc(b_drained, 1)
                        dve.wait_ge(b_drained, b_order[e])
                        for t in range(2):
                            tile = 2 * k + t
                            on = key_on[:, n * NT + tile:n * NT + tile + 1] if l == 0 else 1.0
                            dve.tensor_scalar(values[:, g % 2, tile, :, 0:HD], v_tmp[:, t, :].rearrange("p (h c) -> p h c", h=HEADS),
                                              on, None, ALU.mult)
                            last = dve.tensor_scalar(values[:, g % 2, tile, :, HD:HD + 1], ones_f[:, 0:HEADS].unsqueeze(2),
                                                     on, None, ALU.mult)
                        if k:
                            last.then_inc(v_ready, 1)
                            dve.wait_ge(v_ready, g + 1)
                        else:
                            link(last)
                    if kind == "OT":
                        dve.wait_ge(b_filled, b_order[e])
                        if g and k == 0:
                            pl, pn = divmod(g - 1, B)
                            dve.wait_ge(a_filled, a_order[(pl, "OF", pn, 1)])
                        heads = ps[:, B_BANK, :].rearrange("p (t j c) -> p t j c", t=NT, j=4)
                        link(dve.reciprocal(rec[:, :, :].unsqueeze(3), heads[:, :, :, HD:HD + 1]))
                        dve.tensor_tensor(o_tok[:, :, 64 * k:64 * k + 64].rearrange("p t (j c) -> p t j c", j=4),
                                          heads[:, :, :, 0:HD], rec[:, :, :].unsqueeze(3).to_broadcast([P, NT, 4, HD]),
                                          ALU.mult).then_inc(b_drained, 1)
                    if kind == "OP":
                        dve.wait_ge(b_filled, b_order[e])
                        junk_written()
                        dve.tensor_tensor(upd[:, :, :], ps[:, B_BANK, :].rearrange("p (t n) -> p t n", t=2),
                                          bo_bc[:, :].unsqueeze(1).to_broadcast([P, 2, D]), ALU.add).then_inc(b_drained, 1)
                        dve.wait_ge(b_drained, b_order[e])
                        for t in range(2):
                            r = n * NT + 2 * k + t
                            gt = tok_gate[:, r:r + 1] if l == 0 else tanhg[:, 1:2]
                            last = dve.scalar_tensor_tensor(x[:, r, :], upd[:, t, :], gt, x[:, r, :], ALU.mult, ALU.add)
                        last.then_inc(x_upd, 1)
                        dve.wait_ge(x_upd, 2 * g + k + 1)

            def key_mask_row(l, g):
                dve.wait_ge(mrow_in, 16 * (g + 1))
                if g:
                    dve.wait_ge(slot_in[(g - 1) % 2][0], 16 * FILLS[0] * ((g - 1) // 2 + 1))
                ops = (-1.0, BIG, ALU.add, ALU.mult) if l == 0 else (0.0, None, ALU.mult)
                dve.tensor_scalar(mask_row[:, :], mrow8[:, :], *ops).then_inc(maskrow, 1)

            def mask_piece(e, n, k):
                if k < 4:
                    h = k % 2
                    dve.wait_ge(mstage_in, 16 * (4 * n + k + 1))
                    if k == 0 and n:
                        dve.wait_ge(m_ready, n)
                    dve.tensor_scalar(m_on[:, 2 * h:2 * h + 2, :], m_stage[:, :, :], 0.0, None,
                                      ALU.not_equal).then_inc(m_stage_free, 1)
                if k == 1:
                    dve.wait_ge(m_stage_free, 4 * n + 2)
                    link(dve.tensor_reduce(row_any[:, 0, :], m_on[:, :, :], AX.X, ALU.max))
                    link(dve.tensor_scalar(row_any[:, 1, :], row_any[:, 0, :], BIG, None, ALU.mult))
                    for t in range(NT):
                        last = dve.tensor_scalar(m_add_q[:, n % 2, t, :], m_on[:, t, :], -1.0, row_any[:, 1, t:t + 1],
                                                 ALU.add, ALU.mult)
                    link(last)
                if k == 4:
                    dve.wait_ge(b_filled, b_order[e])
                    dve.tensor_scalar(any_bc, ps[:, B_BANK, :], 1.0, None, ALU.min).then_inc(b_drained, 1)
                    dve.wait_ge(b_drained, b_order[e])
                    link(dve.tensor_scalar(any_big, any_bc, BIG, None, ALU.mult))
                    for t in range(NT):
                        last = dve.scalar_tensor_tensor(m_add_k[:, (B + n) % 3, t, :], m_on[:, t, :], -1.0, any_big,
                                                        ALU.add, ALU.mult)
                    last.then_inc(m_ready, 1)

            maxima = [0]

            def junk_written():
                if maxima[0]:
                    dve.wait_ge(max_drained, maxima[0])

            def row_max(l, q, qt):
                g, h = l * B + q // STEPS, q % STEPS
                o = 64 * g + 4 * h + qt
                maxima[0] = o + 1
                if h % 4 == 0 and qt == 0 and g:
                    pl, pn = divmod(g - 1, B)
                    dve.wait_ge(b_filled, b_order[(pl, "M", pn, h // 4)])
                dve.wait_ge(max_filled, o + 1)
                to, bank = max_q[:, 4 * h + qt:4 * h + qt + 1], ps[:, MAX_BANK[o % 2], :]
                if l == 0:
                    dve.tensor_reduce(to, bank, AX.X, ALU.max).then_inc(max_drained, 1)
                else:
                    dve.wait_ge(max_drained, o)
                    dve.tensor_tensor_reduce(junk, bank, m_add_q[:, (g - B) % 2, qt, :], 1.0, LOWEST,
                                             ALU.add, ALU.max, to).then_inc(max_drained, 1)

            count_from_one(dve, "dve")
            dve.wait_ge(const_in, 16 * CONSTS)
            dve.wait_ge(const_ok, 3)
            link(dve.memset(ps[:, PV_BANK, :], 0.0))
            link(dve.tensor_copy(key_on[:, :], km8[:, :]))
            dve.wait_ge(gate_ok, 1)
            link(dve.tensor_scalar(tok_gate[:, :], key_on[:, :], tanhg[:, 0:1], None, ALU.mult))
            attention(0)

            def ff_norm(s, l, n, count):
                dve.wait_ge(x_upd, n * 2 + 2 + 2 * B * l)
                dve.wait_ge(s["t_filled"], 1 + n * KT)
                layer_norm(x[:, bass.ds(n * NT, NT), :], count).then_inc(s["ln"], 1)

            s = ff[0]
            dve.wait_ge(a_filled, A_END[0])
            ff_norm(s, 0, 0, link)
            dve.wait_ge(s["w_in"], 16 * 5)
            link(dve.tensor_reduce(alpha1[:, :], w1_n, AX.X, ALU.add, apply_absolute_value=True))
            dve.tensor_scalar(alpha1[:, :], alpha1[:, :], 1.0 / D, None, ALU.mult).then_inc(alpha_ok, 1)
            dve.wait_ge(w2_sums, 1)
            dve.tensor_scalar(alpha2[:, :], ps[:, D_BANK[0], 0:D], 1.0 / HID, None, ALU.mult).then_inc(alpha_ok, 1)
            dve.wait_ge(alpha_ok, 2)

            def looped(sem_, per, n, start):
                made = [start]

                def count(ins):
                    made[0] += 1
                    ins.then_inc(sem_, 1)
                    dve.wait_ge(sem_, n * per + made[0])
                return count

            def output0(n, count):
                for half in range(2):
                    dve.wait_ge(s["d_filled"], 1 + n * 2 + half + 1)
                    dve.tensor_tensor(upd[:, :, :], ps[:, D_BANK[half], :].rearrange("p (t n) -> p t n", t=2),
                                      alpha2[:, :].unsqueeze(1).to_broadcast([P, 2, D]), ALU.mult).then_inc(s["d_drained"], 1)
                    dve.wait_ge(s["d_drained"], 1 + n * 2 + half + 1)
                    count(dve.tensor_tensor(upd[:, :, :], upd[:, :, :], b2_bc[:, :].unsqueeze(1).to_broadcast([P, 2, D]),
                                            ALU.add))
                    rows = x[:, bass.ds(n * NT + 2 * half, 2), :]
                    dve.scalar_tensor_tensor(rows, upd[:, :, :], tanhg[:, 2:3], rows, ALU.mult,
                                             ALU.add).then_inc(s["x_done"], 1)
                    dve.wait_ge(s["x_done"], n * 2 + half + 1)

            PER0 = LN_LINKS + 2
            with dve.Fori(0, B - 1) as n:
                c = looped(chain0, PER0, n, 0)
                ff_norm(s, 0, n + 1, c)
                output0(n, c)
            output0(B - 1, looped(chain0, PER0, B - 1, 0))

            attention(1)

            s = ff[1]

            def gating(n, count):
                dve.wait_ge(s["r_filled"], n * 1 + 1)
                count(dve.tensor_copy(logit[:, :, :], ps[:, R_BANK, 0:NT * EXPERTS].rearrange("p (t n) -> p t n", t=NT)))
                stand()
                for t in range(NT):
                    last = dve.max(top[:, t, :], logit[:, t, :])
                count(last)
                stand()
                for t in range(NT):
                    last = dve.max_index(top_i[:, t, :], top[:, t, :], logit[:, t, :])
                count(last)
                count(dve.tensor_copy(top_f[:, :, :], top_i[:, :, 0:2]))
                dve.tensor_tensor(g_w[:, :, 0:1], top[:, :, 1:2], top[:, :, 0:1], ALU.subtract).then_inc(s["g_diff"], 1)
                dve.wait_ge(s["g_exp"], n * 1 + 1)
                count(dve.tensor_scalar(g_w[:, :, 2:3], g_w[:, :, 1:2], 1.0, None, ALU.add))
                count(dve.reciprocal(g_w[:, :, 2:3], g_w[:, :, 2:3]))
                count(dve.tensor_scalar(g_w[:, :, 2:3], g_w[:, :, 2:3], tanhg[:, 3:4], None, ALU.mult))
                count(dve.tensor_tensor(g_w[:, :, 3:4], g_w[:, :, 1:2], g_w[:, :, 2:3], ALU.mult))
                for t in range(NT):
                    count(dve.tensor_scalar(hot[:, 0, :], iota_e[:, :], top_f[:, t, 0:1], g_w[:, t, 2:3], ALU.is_equal, ALU.mult))
                    count(dve.tensor_scalar(hot[:, 1, :], iota_e[:, :], top_f[:, t, 1:2], g_w[:, t, 3:4], ALU.is_equal, ALU.mult))
                    count(dve.tensor_tensor(gate[:, t, 1:UNITS], hot[:, 0, :], hot[:, 1, :], ALU.add))
                    last = dve.tensor_scalar(gate[:, t, 0:1], ones_f[:, 0:1], tanhg[:, 3:4], None, ALU.mult)
                last.then_inc(s["gate"], 1)
                dve.wait_ge(s["gate"], 1 + n * 1 + 1)

            def output1(n, e):
                for half in range(2):
                    u = 2 * e + half
                    dve.wait_ge(s["d_filled"], 1 + n * 2 * UNITS + u + 1)
                    dve.wait_ge(s["d_drained"], 1 + n * 2 * UNITS + u)
                    for t in range(2):
                        rows = x[:, bass.ds(n * NT + 2 * half + t, 1), :]
                        last = dve.scalar_tensor_tensor(rows, ps[:, D_BANK[half], t * D:(t + 1) * D].unsqueeze(1),
                                                        gate[:, 2 * half + t, e:e + 1], rows, ALU.mult, ALU.add)
                    last.then_inc(s["d_drained"], 1)

            PER1 = LN_LINKS + GATE_LINKS
            dve.wait_ge(a_filled, A_END[1])
            ff_norm(s, 1, 0, link)
            gating(0, link)
            with dve.Fori(0, B - 1) as n:
                c = looped(chain1, PER1, n, 0)
                for e in range(UNITS):
                    output1(n, e)
                    if e == 2:
                        ff_norm(s, 1, n + 1, c)
                gating(n + 1, c)
            for e in range(UNITS):
                output1(B - 1, e)


def tables_of_shape():
    inv = (1.0 / np.float32(10000.0) ** (np.arange(0, HD, 2, dtype=np.float32) / np.float32(HD))).astype(np.float32)
    angle = np.outer(np.arange(S, dtype=np.float32), inv).astype(np.float32)
    angle = np.concatenate([angle, angle], axis=1)
    rot = np.zeros((P, P), np.float32)
    for m in range(P):
        low = m % HD < HD // 2
        rot[m + HD // 2 if low else m - HD // 2, m] = -1.0 if low else 1.0
    return {
        "ident": np.eye(P, dtype=np.float32), "rot": rot,
        "cosT": np.tile(np.cos(angle).T, (P // HD, 1)).astype(np.float32),
        "sinT": np.tile(np.sin(angle).T, (P // HD, 1)).astype(np.float32),
        "iota": np.arange(EXPERTS, dtype=np.float32),
        "ones_row": np.full((4, 2 * HEADS * S), 0x3F80, np.uint16)
    }


def kernel(x, ctx_1024, mask_BxS2_bf1, mask_Bx1xSxS2_if1, g_xattn, g_ffn,
           L0_xattn_Wq, L0_xattn_bq, L0_xattn_Wk, L0_xattn_bk, L0_xattn_Wv, L0_xattn_bv, L0_xattn_Wp, L0_xattn_bp,
           L0_ffn_w1, L0_ffn_b1, L0_ffn_w2, L0_ffn_b2,
           L1_xattn_W_q, L1_xattn_b_q, L1_xattn_W_k, L1_xattn_b_k, L1_xattn_W_v, L1_xattn_b_v, L1_xattn_W_o, L1_xattn_b_o,
           L1_ffn_w_router, L1_ffn_w1_stack, L1_ffn_w2_stack, L1_ffn_ws1, L1_ffn_ws2):
    import concourse.bacc as bacc
    from concourse.bass_utils import run_bass_kernel_spmd

    A = np.asarray
    key_mask = A(mask_BxS2_bf1).view(np.uint8)
    pair_mask = A(mask_Bx1xSxS2_if1)[:, 0]
    arrays = {
        "x": A(x), "ctxT": A(ctx_1024).transpose(0, 2, 1), "g_xattn": A(g_xattn), "g_ffn": A(g_ffn),
        "mask_col": key_mask.reshape(B * NT, P).T, "mask_row": key_mask,
        "mask_q": pair_mask, "mask_k": pair_mask.transpose(0, 2, 1),
        "l0_wq": A(L0_xattn_Wq).T, "l0_wk": A(L0_xattn_Wk).T, "l0_wv": A(L0_xattn_Wv).T, "l0_wo": A(L0_xattn_Wp).T,
        "l0_bqk": np.concatenate([A(L0_xattn_bk).reshape(KT, P), A(L0_xattn_bq).reshape(KT, P)]).T,
        "l0_bv": A(L0_xattn_bv), "l0_bo": A(L0_xattn_bp),
        "l1_wq": A(L1_xattn_W_q), "l1_wk": A(L1_xattn_W_k), "l1_wv": A(L1_xattn_W_v), "l1_wo": A(L1_xattn_W_o),
        "l1_bqk": np.concatenate([A(L1_xattn_b_k).reshape(KT, P), A(L1_xattn_b_q).reshape(KT, P)]).T,
        "l1_bv": A(L1_xattn_b_v), "l1_bo": A(L1_xattn_b_o),
        "w1": A(L0_ffn_w1), "w1T": A(L0_ffn_w1).T, "b1": A(L0_ffn_b1).reshape(HT, P).T, "w2T": A(L0_ffn_w2).T, "b2": A(L0_ffn_b2),
        "w_router": A(L1_ffn_w_router).T, "we1T": A(L1_ffn_w1_stack).transpose(0, 2, 1),
        "we2T": A(L1_ffn_w2_stack).transpose(0, 2, 1), "ws1T": A(L1_ffn_ws1).T, "ws2T": A(L1_ffn_ws2).T,
        **tables_of_shape(),
    }
    arrays = {name: np.ascontiguousarray(a) for name, a in arrays.items()}
    nc = bacc.Bacc("TRN2", target_bir_lowering=False, num_devices=1)
    d = {name: nc.dram_tensor(f"in_{name}", a.shape, mybir.dt.from_np(a.dtype), kind="ExternalInput").ap()
         for name, a in arrays.items()}
    out = nc.dram_tensor("out", [B, S, D], F32, kind="ExternalOutput").ap()
    bass_flamingo(nc, d, out)
    r = run_bass_kernel_spmd(nc, [{f"in_{name}": a for name, a in arrays.items()}], core_ids=[0])
    return r.results[0]["out"]
```

```python
from contextlib import ExitStack

import numpy as np
import concourse.bass as bass
from concourse import mybir

F32 = mybir.dt.float32
F32R = mybir.dt.float32r
BF16 = mybir.dt.bfloat16
I32 = mybir.dt.int32
U32 = mybir.dt.uint32
U16 = mybir.dt.uint16
U8 = mybir.dt.uint8
ALU = mybir.AluOpType
ACT = mybir.ActivationFunctionType
AX = mybir.AxisListType

P = 128
B, S, D = 4, 512, 256
HEADS, HD = 16, 16
NT = S // P
KT = D // P
HID = 1024
HT = HID // P
EXPERTS, EF, SF = 8, 256, 512
SHARED = SF // EF
UNITS = SHARED + EXPERTS
UT = EF // P
EPS = 1e-5
BIG = 1e30
LOWEST = -3e38
SCALE = HD ** -0.5
VW = HD + 1

PARTS = 6 * HD
MAX_K = PARTS + 1
ST_K = MAX_K + 3
Q_PART = [0, 1, 2, 0, 1, 0]
K_PART = [0, 0, 0, 1, 1, 2]
ITEMS = 4
FILLS = (6 + 6 + 1, 6 + 6)
CONSTS = 8
NEWTON = 3
LN_LINKS, GATE_LINKS = 5 + 4 * NEWTON, 20
LAG = 8
EARLY = 13
STEPS = 16


def plan_layer(masked):
    prep = {1: [("LN", 0), ("LN", 1)], 2: [("LN", 2), ("LN", 3)], 3: [("T", 0), ("T", 1)]}
    if not masked:
        prep |= {4: [("J", 0)], 5: [("J", 1), ("R", 0)], 6: [("H", 0), ("R", 1)], 7: [("D", 0), ("H", 1)],
                 8: [("D", 1)], 9: [("J", 2)], 10: [("J", 3), ("R", 2)], 11: [("H", 2), ("R", 3)],
                 12: [("D", 2), ("H", 3)], 13: [("D", 3)]}
    else:
        prep |= {4: [("J", 0), ("C", 0)], 5: [("J", 1), ("H", 0)], 6: [("D", 0), ("C", 1)], 7: [("H", 1)],
                 8: [("D", 1), ("C", 2)], 9: [("J", 2)], 10: [("J", 3), ("C", 3)], 11: [("C", 4)],
                 12: [("H", 2)], 13: [("D", 2), ("H", 3)], 14: [("D", 3)]}

    plan = [(kind, 0, k) for v in sorted(prep) for kind, k in prep[v]]
    plan += [("F", 0, 0), ("F", 0, 1), ("V", 0, 0), ("V", 0, 1)]
    for q in range(1 - EARLY, B * STEPS + 5):
        n, s = q // STEPS, q % STEPS
        side = []
        done = q + LAG - 2
        if 0 <= done < B * STEPS and done % 4 == 3:
            side.append(("M", done // STEPS, done % STEPS // 4))
        if q >= 5 and q % 4 == 1 and q <= B * STEPS + 1:
            side.append(("OT", (q - 2) // STEPS, (q - 2) % STEPS // 4))
        if n >= 1:
            side += {2: [("OF", n - 1, 0), ("OF", n - 1, 1)], 3: [("OP", n - 1, 0)], 4: [("OP", n - 1, 1)]}.get(s, [])
        if n + 1 < B and q >= 0 and s in (14, 15):
            side.append(("V", n + 1, s - 14))
        if 0 <= q and n + 2 < B:
            side += [(kind, n + 2, k) for kind, k in prep.get(s, [])]
        side += [(kind, 1, k) for kind, k in prep.get(q + EARLY, [])]
        if n >= 1 and n + 1 < B and s in (0, 1):
            side.append(("F", n + 1, s))
        if q in (2, 3):
            side.append(("F", 1, q - 2))
        for j in range(4):
            if 0 <= q < B * STEPS:
                plan.append(("SCORE", n, 4 * s + j))
            if 0 <= q + LAG < B * STEPS:
                plan.append(("MAX", (q + LAG) // STEPS, 4 * ((q + LAG) % STEPS) + j))
            if j == 1 and 0 < q <= B * STEPS:
                plan.append(("PV", (q - 1) // STEPS, (q - 1) % STEPS))
            plan += side[j * len(side) // 4:(j + 1) * len(side) // 4]
        if q >= 4 and q % 4 == 0 and q <= B * STEPS:
            plan.append(("E", (q - 1) // STEPS, (q - 1) % STEPS // 4))
    return plan


def bass_flamingo(nc, d, out):
    ctx = ExitStack()
    with ctx:
        def sb(name, shape, dt=F32):
            return ctx.enter_context(nc.sbuf_tensor(name, shape, dt))

        def sem(name):
            return ctx.enter_context(nc.semaphore(name))

        x = sb("x_tok", [P, B * NT, D])
        xn = sb("xn", [P, NT, D])
        v_tmp = sb("v_tmp", [P, 2, D])
        upd = v_tmp
        junk = v_tmp[:, 0, :].bitcast(BF16)
        ident = sb("ident", [P, P])
        ident_b = sb("ident_b", [P, P], BF16)
        ones_b = sb("ones_b", [P, P], BF16)
        ones_f = sb("ones_f", [P, HEADS])
        gates = sb("gates", [P, 4])
        tanhg = sb("tanhg", [P, 4])
        km8 = sb("km8", [P, B * NT], U8)
        key_on = sb("key_on", [P, B * NT])
        tok_gate = sb("tok_gate", [P, B * NT])
        stats = sb("stats", [P, NT, 6])
        mv = sb("mv", [P, NT, 2])
        nw = sb("nw", [P, 4, NT])
        alpha1 = sb("alpha1", [P, HT])
        b1_col = sb("b1_col", [P, HT])
        w_rt = sb("w_rt", [P, KT, EXPERTS])
        logit = sb("logit", [P, NT, EXPERTS])
        top = sb("top", [P, NT, 8])
        top_i = sb("top_i", [P, NT, 8], U32)
        top_f = sb("top_f", [P, NT, 2])
        g_w = sb("g_w", [P, NT, 4])
        hot = sb("hot", [P, 2, EXPERTS])
        gate = sb("gate", [P, NT, UNITS])
        iota_e = sb("iota_e", [P, EXPERTS])

        with ExitStack() as stack:
            def over(name, shape, dt=F32):
                return stack.enter_context(nc.sbuf_tensor(name, shape, dt))
            xT_hi = over("xT_hi", [P, KT, S], F32R)
            xT_lo = over("xT_lo", [P, KT, S], F32R)
            w1_s = over("w1_sign", [P, KT, HID], F32R)
            w2_s = over("w2_sign", [P, HT, D], F32R)
            w1_f = over("w1_float", [P, KT, HID])
            w1_n = over("w1_natural", [P, HT, D])
            w2_f = over("w2_float", [P, HT, D])
            alpha2 = over("alpha2", [P, D])
            b2_bc = over("b2_bc", [P, D])
        with ExitStack() as stack:
            def over(name, shape, dt=F32):
                return stack.enter_context(nc.sbuf_tensor(name, shape, dt))
            we_f = over("we_float", [P, UNITS, 2, UT * D])
            xT = over("xT", [P, KT, S])
            xT_hi1 = over("xT_hi1", [P, KT, S], F32R)
            xT_lo1 = over("xT_lo1", [P, KT, S], F32R)
            raw1 = over("raw1", [P, 4, S])

        big = sb("operands", [P, 2 * 2 * HEADS * S], BF16)
        q_op = big[:, 0:2 * HEADS * S].rearrange("p (s h n) -> p s h n", s=2, h=HEADS)
        k_op = big[:, 2 * HEADS * S:].rearrange("p (s h n) -> p s h n", s=2, h=HEADS)

        with ExitStack() as stack:
            def over(name, shape, dt=F32):
                return stack.enter_context(nc.sbuf_tensor(name, shape, dt))
            we = over("we_parts", [P, UNITS, 2, 2, UT * D], F32R)
            hid1 = over("hid1", [P, 2, 2, UT, S], F32R)

        w_att = sb("w_att", [P, 4, KT, D])
        bqk = sb("bqk", [P, 2, ITEMS])
        bv_bc = sb("bv_bc", [P, D])
        bo_bc = sb("bo_bc", [P, D])
        tables = sb("tables", [P, 2, S])
        cos_t, sin_t = tables[:, 0, :], tables[:, 1, :]
        any_bc, any_big = tables[:, 0, :], tables[:, 1, :]
        rot_m = sb("rot_m", [P, P])
        parts = sb("parts", [P, ITEMS, 3, S], BF16)
        ctx_k = sb("ctx_k", [P, KT, S])
        ctx_v = sb("ctx_v", [P, KT, S])
        xnT = sb("xnT", [P, KT, S])
        f = sb("f", [P, ITEMS, S])
        rotated = sb("rotated", [P, S])
        rest = sb("rest", [P, S])
        mrow8 = sb("mrow8", [1, S], U8)
        mask_row = sb("mask_row", [1, S], BF16)
        m_stage = sb("m_stage", [P, 2, S], I32)
        rot_tmp = m_stage[:, 0, :].bitcast(F32)
        m_on = sb("m_on", [P, NT, S], BF16)
        m_add_q = sb("m_add_q", [P, 2, NT, S], BF16)
        row_any = sb("row_any", [P, 2, NT])

        with ExitStack() as stack:
            def over(name, shape, dt=F32):
                return stack.enter_context(nc.sbuf_tensor(name, shape, dt))
            raw0 = over("raw0", [P, 4, S])
            hid0_hi = over("hid0_hi", [P, HT, S], F32R)
            hid0_lo = over("hid0_lo", [P, HT, S], F32R)

        probs = sb("probs", [P, 2, 4, S])
        values = sb("values", [P, 2, NT, HEADS, VW])
        m_add_k = sb("m_add_k", [P, 3, NT, S], BF16)
        o_tok = sb("o_tok", [P, NT, D])
        o_heads = sb("o_heads", [P, 2, S])
        o_feat = sb("o_feat", [P, KT, S])
        max_q = sb("max_q", [P, HEADS * NT])
        m_rest = sb("m_rest", [4 * NT, 2, P])
        m_parts = sb("m_parts", [4 * NT, 2, 3, P], BF16)
        rec = sb("rec", [P, NT, 4])

        ps = ctx.enter_context(nc.psum_tensor("ps", [P, 8, S], F32))
        ST_BANK, MAX_BANK, PV_BANK, A_BANK, B_BANK = (0, 1, 2), (3, 4), 5, 6, 7

        x_in = [sem(f"x_in{n}") for n in range(B)]
        const_in = sem("const_in")
        w_in = sem("w_in")
        const_ok = sem("const_ok")
        gate_ok = sem("gate_ok")
        chain = sem("dve_chain")
        ln_done = sem("ln_done")
        a_filled, a_drained = sem("a_filled"), sem("a_drained")
        b_filled, b_drained = sem("b_filled"), sem("b_drained")
        ctxk_in, ctxv_in = sem("ctxk_in"), sem("ctxv_in")
        cos_done = sem("cos_done")
        source_ok = sem("source_ok")
        hi_done, mid_done = sem("hi_done"), sem("mid_done")
        rest_done, split_done = sem("rest_done"), sem("split_done")
        spill = [sem(f"spill{i}") for i in range(ITEMS)]
        slot_in = [[sem(f"slot_in{i}{h}") for h in range(2)] for i in range(2)]
        maxrow_in = [sem(f"maxrow_in{i}") for i in range(2)]
        maskrow = sem("maskrow")
        mrow_in = sem("mrow_in")
        max_filled, max_drained = sem("max_filled"), sem("max_drained")
        st_filled, exp_done = sem("st_filled"), sem("exp_done")
        pv_done, heads_out = sem("pv_done"), sem("heads_out")
        v_ready = sem("v_ready")
        m_split = sem("m_split")
        key_ok = sem("key_ok")
        x_upd = sem("x_upd")
        mstage_in = sem("mstage_in")
        m_stage_free = sem("m_stage_free")
        rows_in = sem("rows_in")
        out_done = sem("out_done")
        m_ready = sem("m_ready")

        plans = [[(l, *e) for e in plan_layer(masked=l == 1)] for l in range(2)]
        plan = plans[0] + plans[1]
        a_order = {e: j + 1 for j, e in enumerate(e for e in plan if e[1] in ("T", "J", "OF"))}
        b_order = {e: j + 1 for j, e in enumerate(e for e in plan if e[1] in ("R", "V", "M", "OT", "OP") or e[1:4:2] == ("C", 4))}
        A_END, B_END = [], []
        for l in range(2):
            A_END.append(max(v for e, v in a_order.items() if e[0] == l))
            B_END.append(max(v for e, v in b_order.items() if e[0] == l))

        scratch = nc.dram_tensor("qk_parts", [2 * B * ITEMS, 8, HD, 3, S], BF16, kind="Internal").ap()

        def batch(l, n):
            return l * B + n

        def sources(l, n, k):
            return ITEMS * n + k + 1 if l == 0 else ITEMS * B + 2 * n + k - 1

        ff = [dict((k, sem(f"ff{l}_{k}")) for k in (
            "ln",
            "t_filled",
            "t_hi", "t_drained",
            "u_filled",
            "u_drained",
            "squared",
            "h_hi", "h_lo",
            "d_filled",
            "d_drained",
            "w_in", "w_hi", "w_lo", "r_filled", "g_diff", "g_exp", "gate", "x_done")) for l in range(2)]
        units_in = [sem(f"units_in{j}") for j in range(UNITS // 2)]
        FROM_ONE = {"pe": [(0, "t_filled"), (0, "d_filled"), (1, "t_filled"), (1, "d_filled")],
                    "act": [(0, "u_drained"), (1, "u_drained")],
                    "dve": [(0, "t_drained"), (0, "d_drained"), (1, "t_drained"), (1, "d_drained"), (1, "gate")],
                    "pool": [(0, "h_lo"), (1, "h_lo")]}

        def count_from_one(eng, who):
            for l, k in FROM_ONE[who]:
                eng.sem_inc(ff[l][k], 1)

        alpha_ok = sem("alpha_ok")
        w2_sums = sem("w2_sums")
        stood = sem("stood")
        chain0, chain1 = sem("dve_chain_ff0"), sem("dve_chain_ff1")

        U_BANK, D_BANK, T_BANK, R_BANK = (0, 1, 2, 3), (4, 5), 6, 7

        block = ctx.enter_context(nc.Block())

        @block.sync
        def _(sp):
            def load(dst, src, s):
                sp.dma_start(dst, src).then_inc(s, 16)

            def load_weights(l):
                if l:
                    sp.wait_ge(b_drained, B_END[0])
                    sp.wait_ge(x_upd, 2 * B)
                for j, w in enumerate(("wq", "wk", "wv", "wo")):
                    load(w_att[:, j, :, :], d[f"l{l}_{w}"].rearrange("(k p) n -> p k n", p=P), w_in)
                load(bqk[:, l, :], d[f"l{l}_bqk"], w_in)
                load(bv_bc[:, :], d[f"l{l}_bv"].partition_broadcast(P), w_in)
                load(bo_bc[:, :], d[f"l{l}_bo"].partition_broadcast(P), w_in)

            def load_ctx(dst, n, s):
                load(dst[:, :, :], d["ctxT"][n].rearrange("(k p) n -> p k n", p=P), s)

            def ctx_k_load(l, n):
                if batch(l, n):
                    pl, pn = divmod(batch(l, n) - 1, B)
                    sp.wait_ge(a_filled, a_order[(pl, "J", pn, 1)])
                load_ctx(ctx_k, n, ctxk_in)

            def ctx_v_load(l, n):
                if batch(l, n):
                    pl, pn = divmod(batch(l, n) - 1, B)
                    sp.wait_ge(b_filled, b_order[(pl, "V", pn, 1)])
                load_ctx(ctx_v, n, ctxv_in)

            def mask_load(n, j):
                if n or j:
                    sp.wait_ge(m_stage_free, 4 * n + j)
                else:
                    sp.wait_ge(b_drained, B_END[0])
                src = d["mask_q"] if j < 2 else d["mask_k"]
                h = j % 2
                load(m_stage[:, :, :], src[n].rearrange("(t p) k -> p t k", p=P)[:, 2 * h:2 * h + 2, :], mstage_in)

            def spill_parts(g, k):
                sp.wait_ge(split_done, ITEMS * g + k + 1)
                load(scratch[ITEMS * g + k].rearrange("h d j n -> (h d) j n"), parts[:, k, :, :], spill[k])

            def fill_slot(g, half):
                sl = g % 2
                if g >= 2:
                    sp.wait_ge(st_filled, 64 * (g - 1))
                arrives = slot_in[sl][half]
                if half == 0:
                    sp.wait_ge(maskrow, g + 1)
                    load(k_op[PARTS:PARTS + 1, sl, :, :], mask_row[:, :].unsqueeze(1).to_broadcast([1, HEADS, S]), arrives)
                for item, operand, order in ((half, k_op, K_PART), (2 + half, q_op, Q_PART)):
                    sp.wait_ge(spill[item], 16 * (g + 1))
                    src = scratch[ITEMS * g + item]
                    for b, j in enumerate(order):
                        load(operand[b * HD:(b + 1) * HD, sl, 8 * half:8 * half + 8, :],
                             src[:, :, j, :].rearrange("h d n -> d h n"), arrives)

            def fill_max_rows(g, gg):
                mg = 4 * g + gg
                sp.wait_ge(m_split, mg + 1)
                for j in range(3):
                    r = MAX_K + j
                    load(q_op[r:r + 1, g % 2, 4 * gg:4 * gg + 4, :].rearrange("p h (t n) -> p (h t) n", n=P),
                         m_parts[:, mg % 2, j, :], maxrow_in[mg % 2])

            def row_mask(l, n):
                g = batch(l, n)
                if g:
                    sp.wait_ge(maskrow, g)
                load(mrow8[:, :], d["mask_row"][n:n + 1, :], mrow_in)

            load(x[:, 0:NT, :], d["x"][0].rearrange("(t p) n -> p t n", p=P), x_in[0])
            load(ident[:, :], d["ident"], const_in)
            load(rot_m[:, :], d["rot"], const_in)
            load(cos_t, d["cosT"], const_in)
            load(sin_t, d["sinT"], const_in)
            load(gates[:, 0:2], d["g_xattn"].partition_broadcast(P), const_in)
            load(gates[:, 2:4], d["g_ffn"].partition_broadcast(P), const_in)
            load(km8[:, :], d["mask_col"], const_in)
            load(iota_e[:, :], d["iota"].partition_broadcast(P), const_in)
            load_weights(0)
            ctx_k_load(0, 0)
            for n in range(1, B):
                load(x[:, n * NT:(n + 1) * NT, :], d["x"][n].rearrange("(t p) n -> p t n", p=P), x_in[n])

            for l in range(2):
                if l:
                    load_weights(1)
                    mask_load(0, 0)
                    sp.wait_ge(ff[0]["x_done"], 2 * B)
                load(q_op[PARTS:MAX_K, :, :, :].bitcast(U16), d["ones_row"][0:1], rows_in)
                load(k_op[PARTS:ST_K, :, :, :].bitcast(U16), d["ones_row"], rows_in)
                sp.wait_ge(rows_in, 32 * (l + 1))
                ctx_v_load(l, 0)
                for _, kind, n, k in plans[l]:
                    g = batch(l, n)
                    if kind == "LN" and k == 0 and g:
                        ctx_k_load(l, n)
                    if kind == "J" and k == 2:
                        row_mask(l, n)
                    if kind == "C" and k < 4 and (k < 3 or n + 1 < B):
                        mask_load(n + (k == 3), (k + 1) % 4)
                    if kind == "D":
                        spill_parts(g, k)
                    if kind == "F":
                        fill_slot(g, k)
                    if kind == "M":
                        fill_max_rows(g, k)
                    if kind == "V" and k == 1 and n + 1 < B:
                        ctx_v_load(l, n + 1)
                sp.wait_ge(st_filled, 64 * B * (l + 1))
                w = ff[l]["w_in"]
                if l == 0:
                    load(w1_f[:, :, :], d["w1T"].rearrange("(k p) n -> p k n", p=P), w)
                    load(w1_n[:, :, :], d["w1"].rearrange("(k p) n -> p k n", p=P), w)
                    load(w2_f[:, :, :], d["w2T"].rearrange("(k p) n -> p k n", p=P), w)
                    load(b1_col[:, :], d["b1"], w)
                    load(b2_bc[:, :], d["b2"].partition_broadcast(P), w)
                else:
                    load(w_rt[:, :, :], d["w_router"].rearrange("(k p) n -> p k n", p=P), w)
                    for e in range(0, UNITS, 2):
                        load(we_f[:, e:e + 2, :, :], d["units"][e:e + 2].rearrange("e j p c -> p (e j) c"),
                             units_in[e // 2])
            with sp.Fori(0, B) as n:
                sp.wait_ge(ff[1]["d_drained"], 1 + n * 2 * UNITS + 2 * UNITS)
                sp.dma_start(out[bass.ds(n, 1), :, :].rearrange("a (t p) n -> p (a t) n", p=P),
                             x[:, bass.ds(n * NT, NT), :]).then_inc(out_done, 16)
            sp.wait_ge(out_done, 16 * B)

        @block.gpsimd
        def _(pool):
            count_from_one(pool, "pool")
            pool.memset(ones_b[:, :], 1.0).then_inc(const_ok, 1)
            pool.memset(ones_f[:, :], 1.0).then_inc(const_ok, 1)
            pool.wait_ge(const_in, 16 * CONSTS)
            pool.tensor_copy(ident_b[:, :], ident[:, :]).then_inc(const_ok, 1)

            def attention(l):
                for _, kind, n, k in plans[l]:
                    g = batch(l, n)
                    item = ITEMS * g + k
                    if kind == "R" or kind == "H" and l == 1 and k >= 2:
                        if item:
                            pool.wait_ge(hi_done, item)
                            pool.wait_ge(rest_done, item)
                        pool.wait_ge(a_drained, a_order[(l, "J", n, k)])
                        if l == 0:
                            pool.tensor_tensor(rotated[:, :], f[:, k, :], cos_t, ALU.mult).then_inc(cos_done, 1)
                            pool.wait_ge(cos_done, item + 1)
                            pool.wait_ge(b_drained, b_order[(l, "R", n, k)])
                            pool.tensor_tensor(rotated[:, :], rotated[:, :], rot_tmp, ALU.add).then_inc(source_ok, 1)
                        else:
                            pool.wait_ge(b_drained, b_order[(l, "C", n, 4)])
                            pool.tensor_tensor(rotated[:, :], f[:, k, :], any_bc, ALU.mult).then_inc(source_ok, 1)
                    if kind == "H":
                        src = f[:, k, :] if l == 1 and k < 2 else rotated[:, :]
                        pool.wait_ge(hi_done, item + 1)
                        if item:
                            pool.wait_ge(mid_done, item)
                            pool.wait_ge(split_done, item)
                        pool.tensor_tensor(rest[:, :], src, parts[:, k, 0, :], ALU.subtract).then_inc(rest_done, 1)
                    if kind == "D":
                        pool.wait_ge(mid_done, item + 1)
                        pool.wait_ge(rest_done, item + 1)
                        pool.tensor_tensor(parts[:, k, 2, :], rest[:, :], parts[:, k, 1, :],
                                           ALU.subtract).then_inc(split_done, 1)

            attention(0)

            s0 = ff[0]

            def hidden_rest(n):
                for t in range(HT):
                    pool.wait_ge(s0["h_hi"], n * HT + t + 1)
                    pool.tensor_tensor(hid0_lo[:, t, :], raw0[:, t % 4, :], hid0_hi[:, t, :].bitcast(F32),
                                       ALU.subtract).then_inc(s0["h_lo"], 1)

            with pool.Fori(0, B) as n:
                hidden_rest(n)

            attention(1)
            s1 = ff[1]

            def weight_rest(e):
                pool.wait_ge(s1["w_hi"], e + 1)
                pool.tensor_tensor(we[:, e, 1, :, :], we_f[:, e, :, :], we[:, e, 0, :, :].bitcast(F32),
                                   ALU.subtract).then_inc(s1["w_lo"], 1)

            def unit_rest(n, e):
                for t in range(UT):
                    o = UT * e + t
                    pool.wait_ge(s1["h_hi"], n * UNITS * UT + o + 1)
                    pool.tensor_tensor(hid1[:, 1, e % 2, t, :], raw1[:, o % 4, :], hid1[:, 0, e % 2, t, :].bitcast(F32),
                                       ALU.subtract).then_inc(s1["h_lo"], 1)

            weight_rest(0)
            weight_rest(1)
            for e in range(UNITS):
                unit_rest(0, e)
                if e + 2 < UNITS:
                    weight_rest(e + 2)
            with pool.Fori(1, B) as n:
                for e in range(UNITS):
                    unit_rest(n, e)

        @block.scalar
        def _(act):
            count_from_one(act, "act")
            act.wait_ge(const_in, 16 * CONSTS)
            act.activation(tanhg[:, :], gates[:, :], ACT.Tanh).then_inc(gate_ok, 1)

            def attention(l):
                for e in plans[l]:
                    _, kind, n, k = e
                    g = batch(l, n)
                    if kind == "T":
                        act.wait_ge(a_filled, a_order[e])
                        act.copy(xnT[:, k, :], ps[:, A_BANK, :]).then_inc(a_drained, 1)
                    if kind == "J":
                        act.wait_ge(a_filled, a_order[e])
                        if g:
                            act.wait_ge(split_done, ITEMS * (g - 1) + k + 1)
                        act.activation(f[:, k, :], ps[:, A_BANK, :], ACT.Identity,
                                       bias=bqk[:, l, k:k + 1]).then_inc(a_drained, 1)
                    if kind == "SCORE":
                        o = 64 * g + k
                        G, j = o // 4, o % 4
                        act.wait_ge(st_filled, o + 1)
                        if G >= 2 and j == 0:
                            act.wait_ge(pv_done, G - 1)
                        act.activation(probs[:, G % 2, j, :], ps[:, ST_BANK[o % 3], :], ACT.Exp,
                                       scale=SCALE).then_inc(exp_done, 1)
                    if kind == "E":
                        act.wait_ge(pv_done, STEPS * g + 4 * k + 4)
                        if 4 * g + k >= 2:
                            pl, pn = divmod((4 * g + k - 2) // 4, B)
                            act.wait_ge(b_filled, b_order[(pl, "OT", pn, (k - 2) % 4)])
                        act.copy(o_heads[:, k % 2, :], ps[:, PV_BANK, :]).then_inc(heads_out, 1)
                    if kind == "OF":
                        act.wait_ge(a_filled, a_order[e])
                        if g:
                            pl, pn = divmod(g - 1, B)
                            act.wait_ge(b_filled, b_order[(pl, "OP", pn, 1)])
                        act.copy(o_feat[:, k, :], ps[:, A_BANK, :]).then_inc(a_drained, 1)

            def transposed(s, n, high):
                for k in range(KT):
                    act.wait_ge(s["t_filled"], 1 + n * KT + k + 1)
                    act.copy(high[:, k, :], ps[:, T_BANK, :]).then_inc(s["t_hi"], 1)

            def gelu(n):
                s = ff[0]
                for t in range(HT):
                    act.wait_ge(s["u_filled"], n * HT + t + 1)
                    act.wait_ge(s["h_lo"], 1 + n * HT + max(0, t - 3))
                    act.activation(raw0[:, t % 4, :], ps[:, U_BANK[t % 4], :], ACT.Gelu, bias=b1_col[:, t:t + 1],
                                   scale=alpha1[:, t:t + 1]).then_inc(s["u_drained"], 1)
                    act.wait_ge(s["u_drained"], 1 + n * HT + t + 1)
                    if t == 0:
                        act.wait_ge(s["d_filled"], 1 + n * 2)
                    act.copy(hid0_hi[:, t, :], raw0[:, t % 4, :]).then_inc(s["h_hi"], 1)

            attention(0)
            s = ff[0]
            act.wait_ge(s["w_in"], 16 * 5)
            act.activation(w1_s[:, :, :], w1_f[:, :, :], ACT.Sign).then_inc(s["w_hi"], 1)
            act.activation(w2_s[:, :, :], w2_f[:, :, :], ACT.Sign).then_inc(s["w_hi"], 1)
            act.wait_ge(s["w_hi"], 2)
            act.activation(w2_f[:, :, :], w2_f[:, :, :], ACT.Abs).then_inc(s["w_hi"], 1)
            act.wait_ge(alpha_ok, 1)
            transposed(s, 0, xT_hi)
            with act.Fori(0, B - 1) as n:
                gelu(n)
                transposed(s, n + 1, xT_hi)
            gelu(B - 1)

            attention(1)
            s = ff[1]
            act.wait_ge(x_upd, 4 * B)
            for e in range(UNITS):
                if e % 2 == 0:
                    act.wait_ge(units_in[e // 2], 16)
                act.copy(we[:, e, 0, :, :], we_f[:, e, :, :]).then_inc(s["w_hi"], 1)
                if e == 3:
                    transposed(s, 0, xT_hi1)

            def rectify(n, e):
                for t in range(UT):
                    o = UT * e + t
                    act.wait_ge(s["u_filled"], n * UNITS * UT + o + 1)
                    act.wait_ge(s["h_lo"], 1 + n * UNITS * UT + max(0, o - 3))
                    act.activation(raw1[:, o % 4, :], ps[:, U_BANK[o % 4], :], ACT.Relu).then_inc(s["u_drained"], 1)

            def high_parts(n, e):
                for t in range(UT):
                    o = UT * e + t
                    act.wait_ge(s["squared"], n * UNITS * UT + o + 1)
                    if t == 0:
                        act.wait_ge(s["d_filled"], 1 + n * 2 * UNITS + max(0, 2 * (e - 1)))
                    act.copy(hid1[:, 0, e % 2, t, :], raw1[:, o % 4, :]).then_inc(s["h_hi"], 1)

            def second_weight(n):
                act.wait_ge(s["g_diff"], n * 1 + 1)
                act.activation(g_w[:, :, 1:2], g_w[:, :, 0:1], ACT.Exp).then_inc(s["g_exp"], 1)

            def experts(n, last):
                for e in range(UNITS):
                    rectify(n, e)
                    high_parts(n, e)
                    if e == 1:
                        second_weight(n)
                if not last:
                    transposed(s, n + 1, xT_hi1)

            with act.Fori(0, B - 1) as n:
                experts(n, False)
            experts(B - 1, True)

        @block.tensor
        def _(pe):
            def bank_a(e):
                if a_order[e] > 1:
                    pe.wait_ge(a_drained, a_order[e] - 1)
                return ps[:, A_BANK, :]

            def bank_b(e):
                if b_order[e] > 1:
                    pe.wait_ge(b_drained, b_order[e] - 1)
                return ps[:, B_BANK, :]

            def max_scores(l, g, s, qt):
                o, sl = 64 * g + 4 * s + qt, g % 2
                if s % 8 == 0 and qt == 0:
                    pe.wait_ge(slot_in[sl][s // 8], 16 * FILLS[s // 8] * (g // 2 + 1))
                if o >= 2:
                    pe.wait_ge(max_drained, o - 1)
                pe.matmul(ps[:, MAX_BANK[o % 2], :], q_op[0:MAX_K, sl, s, qt * P:(qt + 1) * P],
                          k_op[0:MAX_K, sl, s, :], start=True, stop=True).then_inc(max_filled, 1)

            def scores(l, g, s, j):
                o, sl, h, kt = 64 * g + 4 * s + j, g % 2, 4 * (s // 4) + j, s % 4
                if kt == 0 and j == 0:
                    mg = 4 * g + s // 4
                    pe.wait_ge(maxrow_in[mg % 2], 48 * (mg // 2 + 1))
                    if l and s == 0:
                        pe.wait_ge(m_ready, g - B + 1)
                if o >= 3:
                    pe.wait_ge(exp_done, o - 2)
                mm = pe.matmul(ps[:, ST_BANK[o % 3], :], k_op[0:ST_K, sl, h, kt * P:(kt + 1) * P],
                               q_op[0:ST_K, sl, h, :], start=True, stop=(l == 0))
                if l:
                    mm = pe.matmul(ps[:, ST_BANK[o % 3], :], ident_b[:, :], m_add_k[:, g % 3, kt, :],
                                   start=False, stop=True)
                mm.then_inc(st_filled, 1)

            def value_product(g, s):
                G, kt = STEPS * g + s, s % 4
                if s == 0:
                    pe.wait_ge(v_ready, g + 1)
                pe.wait_ge(exp_done, 4 * G + 4)
                if kt == 0 and G:
                    pe.wait_ge(heads_out, G // 4)
                for j in range(4):
                    mm = pe.matmul(ps[32 * j:32 * j + VW, PV_BANK, :], values[:, g % 2, kt, 4 * (s // 4) + j, :],
                                   probs[:, G % 2, j, :], start=(kt == 0), stop=(kt == 3))
                mm.then_inc(pv_done, 1)

            def attention(l):
                for e in plans[l]:
                    _, kind, n, k = e
                    g = batch(l, n)
                    if kind == "T":
                        bank = bank_a(e)
                        pe.wait_ge(ln_done, g + 1)
                        for t in range(NT):
                            mm = pe.transpose(bank[:, t * P:(t + 1) * P], xn[:, t, k * P:(k + 1) * P], ident[:, :])
                        mm.then_inc(a_filled, 1)
                    if kind == "C" and k == 4:
                        bank = bank_b(e)
                        pe.wait_ge(m_stage_free, 4 * n + 4)
                        for t in range(NT):
                            mm = pe.matmul(bank, ones_b[:, :], m_on[:, t, :], start=(t == 0), stop=(t == NT - 1))
                        mm.then_inc(b_filled, 1)
                    if kind == "J":
                        bank = bank_a(e)
                        if k == 0:
                            pe.wait_ge(w_in, 16 * 7 * (l + 1))
                            pe.wait_ge(ctxk_in, 16 * (g + 1))
                        if k == 2:
                            pe.wait_ge(a_drained, a_order[(l, "T", n, 1)])
                        src, w, ft = (xnT if k >= 2 else ctx_k), 1 - k // 2, k % 2
                        for c in range(KT):
                            mm = pe.matmul(bank, w_att[:, w, c, ft * P:(ft + 1) * P], src[:, c, :],
                                           start=(c == 0), stop=(c == KT - 1))
                        mm.then_inc(a_filled, 1)
                    if kind == "R":
                        bank = bank_b(e)
                        pe.wait_ge(a_drained, a_order[(l, "J", n, k)])
                        pe.matmul(bank, rot_m[:, :], f[:, k, :], start=True, stop=True).then_inc(b_filled, 1)
                    if kind == "MAX":
                        max_scores(l, g, k // 4, k % 4)
                    if kind == "M":
                        bank = bank_b(e)
                        pe.wait_ge(max_drained, 64 * g + 16 * (k + 1))
                        pe.transpose(bank[0:4 * NT, 0:P], max_q[:, 16 * k:16 * k + 16], ident[:, :]).then_inc(b_filled, 1)
                    if kind == "V":
                        bank = bank_b(e)
                        pe.wait_ge(ctxv_in, 16 * (g + 1))
                        for t in range(2):
                            tok = (2 * k + t) * P
                            for c in range(KT):
                                mm = pe.matmul(bank[:, t * D:(t + 1) * D], ctx_v[:, c, tok:tok + P],
                                               w_att[:, 2, c, :], start=(c == 0), stop=(c == KT - 1))
                        mm.then_inc(b_filled, 1)
                    if kind == "SCORE":
                        scores(l, g, k // 4, k % 4)
                    if kind == "PV":
                        value_product(g, k)
                    if kind == "OT":
                        bank = bank_b(e)
                        pe.wait_ge(heads_out, 4 * g + k + 1)
                        for t in range(NT):
                            mm = pe.transpose(bank[:, t * P:(t + 1) * P], o_heads[:, k % 2, t * P:(t + 1) * P],
                                              ident[:, :])
                        mm.then_inc(b_filled, 1)
                    if kind == "OF":
                        bank = bank_a(e)
                        pe.wait_ge(b_drained, b_order[(l, "OT", n, 3)])
                        for t in range(NT):
                            mm = pe.transpose(bank[:, t * P:(t + 1) * P], o_tok[:, t, k * P:(k + 1) * P], ident[:, :])
                        mm.then_inc(a_filled, 1)
                    if kind == "OP":
                        bank = bank_b(e)
                        pe.wait_ge(a_drained, a_order[(l, "OF", n, 1)])
                        for t in range(2):
                            tok = (2 * k + t) * P
                            for c in range(KT):
                                mm = pe.matmul(bank[:, t * D:(t + 1) * D], o_feat[:, c, tok:tok + P],
                                               w_att[:, 3, c, :], start=(c == 0), stop=(c == KT - 1))
                        mm.then_inc(b_filled, 1)

            def leave_attention(l):
                pe.wait_ge(a_drained, A_END[l])
                pe.wait_ge(b_drained, B_END[l])
                pe.wait_ge(exp_done, 64 * B * (l + 1))
                pe.wait_ge(max_drained, 64 * B * (l + 1))
                pe.wait_ge(heads_out, 4 * B * (l + 1))

            def tokens(s, n):
                pe.wait_ge(s["ln"], n * 1 + 1)
                for k in range(KT):
                    pe.wait_ge(s["t_drained"], 1 + n * KT + k)
                    for t in range(NT):
                        mm = pe.transpose(ps[:, T_BANK, t * P:(t + 1) * P], xn[:, t, k * P:(k + 1) * P], ident[:, :])
                    mm.then_inc(s["t_filled"], 1)

            def up0(n):
                s = ff[0]
                pe.wait_ge(s["t_drained"], 1 + n * KT + KT)
                for t in range(HT):
                    pe.wait_ge(s["u_drained"], 1 + n * HT + max(0, t - 3))
                    for c in range(KT):
                        for tokens_part in (xT_hi, xT_lo):
                            mm = pe.matmul(ps[:, U_BANK[t % 4], :], w1_s[:, c, t * P:(t + 1) * P], tokens_part[:, c, :],
                                           start=(c == 0 and tokens_part is xT_hi),
                                           stop=(c == KT - 1 and tokens_part is xT_lo))
                    mm.then_inc(s["u_filled"], 1)

            def down0(n):
                s = ff[0]
                for half in range(2):
                    pe.wait_ge(s["d_drained"], 1 + n * 2)
                    for t in range(2):
                        tok = (2 * half + t) * P
                        for c in range(HT):
                            if half == 0 and t == 0:
                                pe.wait_ge(s["h_lo"], 1 + n * HT + c + 1)
                            for part in (hid0_hi, hid0_lo):
                                mm = pe.matmul(ps[:, D_BANK[half], t * D:(t + 1) * D], part[:, c, tok:tok + P],
                                               w2_s[:, c, :], start=(c == 0 and part is hid0_hi),
                                               stop=(c == HT - 1 and part is hid0_lo))
                    mm.then_inc(s["d_filled"], 1)

            count_from_one(pe, "pe")
            pe.wait_ge(const_in, 16 * CONSTS)
            pe.wait_ge(const_ok, 3)
            attention(0)

            leave_attention(0)
            s = ff[0]
            pe.wait_ge(s["w_hi"], 3)
            for c in range(HT):
                mm = pe.matmul(ps[:, D_BANK[0], 0:D], ones_f[:, 0:1].to_broadcast([P, P]), w2_f[:, c, :], start=(c == 0), stop=(c == HT - 1))
            mm.then_inc(w2_sums, 1)
            tokens(s, 0)
            pe.wait_ge(alpha_ok, 2)
            with pe.Fori(0, B - 1) as n:
                up0(n)
                tokens(s, n + 1)
                down0(n)
            up0(B - 1)
            down0(B - 1)

            pe.wait_ge(s["u_drained"], 1 + HT * B)
            pe.wait_ge(s["d_drained"], 1 + 2 * B)
            pe.wait_ge(s["t_drained"], 1 + KT * B)
            attention(1)

            leave_attention(1)
            s = ff[1]

            def route(n):
                pe.wait_ge(s["t_drained"], 1 + n * KT + KT)
                pe.wait_ge(s["gate"], 1 + n * 1)
                for t in range(NT):
                    for c in range(KT):
                        mm = pe.matmul(ps[:, R_BANK, t * EXPERTS:(t + 1) * EXPERTS], xT[:, c, t * P:(t + 1) * P],
                                       w_rt[:, c, :], start=(c == 0), stop=(c == KT - 1))
                mm.then_inc(s["r_filled"], 1)

            HI_LO = ((0, 0), (0, 1), (1, 0))

            def up1(n, e):
                pe.wait_ge(s["w_lo"], e + 1)
                for t in range(UT):
                    o = UT * e + t
                    pe.wait_ge(s["u_drained"], 1 + n * UNITS * UT + max(0, o - 3))
                    for c in range(KT):
                        for j, (a, b) in enumerate(HI_LO):
                            w = we[:, e, a, 0, c * EF + t * P:c * EF + (t + 1) * P]
                            mm = pe.matmul(ps[:, U_BANK[o % 4], :], w, (xT_hi1, xT_lo1)[b][:, c, :],
                                           start=(c == 0 and j == 0), stop=(c == KT - 1 and j == 2))
                    mm.then_inc(s["u_filled"], 1)

            def down1(n, e):
                pe.wait_ge(s["h_lo"], 1 + n * UNITS * UT + UT * (e + 1))
                for half in range(2):
                    pe.wait_ge(s["d_drained"], 1 + n * 2 * UNITS + max(0, 2 * e + half - 1))
                    for t in range(2):
                        tok = (2 * half + t) * P
                        for c in range(UT):
                            for j, (a, b) in enumerate(HI_LO):
                                mm = pe.matmul(ps[:, D_BANK[half], t * D:(t + 1) * D], hid1[:, b, e % 2, c, tok:tok + P],
                                               we[:, e, a, 1, c * D:(c + 1) * D],
                                               start=(c == 0 and j == 0), stop=(c == UT - 1 and j == 2))
                    mm.then_inc(s["d_filled"], 1)

            tokens(s, 0)
            pe.wait_ge(s["w_in"], 16)
            route(0)

            def experts(n, last):
                up1(n, 0)
                up1(n, 1)
                for e in range(2, UNITS):
                    up1(n, e)
                    down1(n, e - 2)
                if not last:
                    tokens(s, n + 1)
                down1(n, UNITS - 2)
                down1(n, UNITS - 1)
                if not last:
                    route(n + 1)

            with pe.Fori(0, B - 1) as n:
                experts(n, False)
            experts(B - 1, True)

        @block.vector
        def _(dve):
            links = [0]

            def link(ins):
                links[0] += 1
                ins.then_inc(chain, 1)
                dve.wait_ge(chain, links[0])

            def stand():
                dve.sem_inc(stood, 1)

            def layer_norm(rows, count, piece):
                v, y, a = nw[:, 0, :], nw[:, 1, :], nw[:, 2, :]

                def newton(steps):
                    for _ in range(steps):
                        count(dve.tensor_tensor(a, y, y, ALU.mult))
                        count(dve.tensor_tensor(a, a, v, ALU.mult))
                        count(dve.tensor_scalar(a, a, -0.5, 1.5, ALU.mult, ALU.add))
                        count(dve.tensor_tensor(y, y, a, ALU.mult))

                if piece == 0:
                    for t in range(NT):
                        last = dve.bn_stats(stats[:, t, :], rows[:, t, :])
                    count(last)
                if piece == 1:
                    stand()
                    for t in range(NT):
                        last = dve.bn_aggr(mv[:, t, :], stats[:, t, :])
                    count(last)
                    count(dve.tensor_scalar(v, mv[:, :, 1], EPS, None, ALU.add))
                    count(dve.tensor_scalar(nw[:, 3, :].bitcast(I32), v.bitcast(I32), 1, None, ALU.arith_shift_right))
                    count(dve.tensor_scalar(y.bitcast(I32), nw[:, 3, :].bitcast(I32), -1.0, float(0x5F3759DF),
                                            ALU.mult, ALU.add))
                    newton(1)
                if piece == 2:
                    newton(NEWTON - 1)
                if piece == 3:
                    for t in range(NT):
                        last = dve.tensor_scalar(xn[:, t, :], rows[:, t, :], mv[:, t, 0:1], nw[:, 1, t:t + 1],
                                                 ALU.subtract, ALU.mult)
                    return last

            def attention(l):
                for e in plans[l]:
                    _, kind, n, k = e
                    g = batch(l, n)
                    item = ITEMS * g + k
                    if kind == "LN":
                        if k == 0 and l == 0:
                            dve.wait_ge(x_in[n], 16)
                        elif k == 0:
                            dve.wait_ge(ff[0]["x_done"], 2 * n + 2)
                        if k == 3 and n:
                            dve.wait_ge(a_filled, a_order[(l, "T", n - 1, 1)])
                        elif k == 3 and l:
                            dve.wait_ge(ff[0]["t_filled"], 1 + KT * B)
                        last = layer_norm(x[:, n * NT:(n + 1) * NT, :], link, k)
                        if k == 3:
                            last.then_inc(ln_done, 1)
                    if kind == "C":
                        mask_piece(e, n, k)
                    if kind == "R":
                        dve.wait_ge(b_filled, b_order[e])
                        if item:
                            dve.wait_ge(source_ok, item)
                        dve.tensor_tensor(rot_tmp, ps[:, B_BANK, :], sin_t, ALU.mult).then_inc(b_drained, 1)
                    if kind == "H":
                        if g:
                            dve.wait_ge(spill[k], 16 * g)
                        if l and k < 2:
                            src = f[:, k, :]
                            dve.wait_ge(a_drained, a_order[(l, "J", n, k)])
                        else:
                            src = rotated[:, :]
                            dve.wait_ge(source_ok, sources(l, n, k))
                        dve.tensor_copy(parts[:, k, 0, :], src).then_inc(hi_done, 1)
                    if kind == "D":
                        dve.wait_ge(rest_done, item + 1)
                        dve.tensor_copy(parts[:, k, 1, :], rest[:, :]).then_inc(mid_done, 1)
                        if k == ITEMS - 1:
                            key_mask_row(l, g)
                    if kind == "MAX":
                        row_max(l, g, k // 4, k % 4)
                    if kind == "M":
                        mg = 4 * g + k
                        dve.wait_ge(b_filled, b_order[e])
                        if mg >= 2:
                            dve.wait_ge(maxrow_in[mg % 2], 48 * (mg // 2))
                        dve.tensor_scalar(m_rest[:, 0, :], ps[0:4 * NT, B_BANK, 0:P], -1.0, None,
                                          ALU.mult).then_inc(b_drained, 1)
                        dve.wait_ge(b_drained, b_order[e])
                        part = m_parts[:, mg % 2, :, :]
                        link(dve.tensor_copy(part[:, 0, :], m_rest[:, 0, :]))
                        link(dve.tensor_tensor(m_rest[:, 1, :], m_rest[:, 0, :], part[:, 0, :], ALU.subtract))
                        link(dve.tensor_copy(part[:, 1, :], m_rest[:, 1, :]))
                        dve.tensor_tensor(part[:, 2, :], m_rest[:, 1, :], part[:, 1, :],
                                          ALU.subtract).then_inc(m_split, 1)
                        dve.wait_ge(m_split, mg + 1)
                    if kind == "V":
                        dve.wait_ge(b_filled, b_order[e])
                        if g >= 2 and k == 0:
                            dve.wait_ge(pv_done, STEPS * (g - 1))
                        dve.tensor_tensor(values[:, g % 2, 2 * k:2 * k + 2, :, 0:HD],
                                          ps[:, B_BANK, :].rearrange("p (t h c) -> p t h c", t=2, h=HEADS),
                                          bv_bc[:, :].rearrange("p (h c) -> p h c", h=HEADS).unsqueeze(1).to_broadcast([P, 2, HEADS, HD]),
                                          ALU.add).then_inc(b_drained, 1)
                        if k:
                            dve.wait_ge(b_drained, b_order[e])
                            on = key_on[:, n * NT:(n + 1) * NT] if l == 0 else ones_f[:, 0:NT]
                            dve.tensor_copy(values[:, g % 2, :, :, HD], on.unsqueeze(2).to_broadcast([P, NT, HEADS])).then_inc(v_ready, 1)
                    if kind == "OT":
                        dve.wait_ge(b_filled, b_order[e])
                        if g and k == 0:
                            pl, pn = divmod(g - 1, B)
                            dve.wait_ge(a_filled, a_order[(pl, "OF", pn, 1)])
                        heads = ps[:, B_BANK, :].rearrange("p (t j c) -> p t j c", t=NT, j=4)
                        link(dve.reciprocal(rec[:, :, :].unsqueeze(3), heads[:, :, :, HD:HD + 1]))
                        dve.tensor_tensor(o_tok[:, :, 64 * k:64 * k + 64].rearrange("p t (j c) -> p t j c", j=4),
                                          heads[:, :, :, 0:HD], rec[:, :, :].unsqueeze(3).to_broadcast([P, NT, 4, HD]),
                                          ALU.mult).then_inc(b_drained, 1)
                    if kind == "OP":
                        dve.wait_ge(b_filled, b_order[e])
                        junk_written()
                        dve.tensor_tensor(upd[:, :, :], ps[:, B_BANK, :].rearrange("p (t n) -> p t n", t=2),
                                          bo_bc[:, :].unsqueeze(1).to_broadcast([P, 2, D]), ALU.add).then_inc(b_drained, 1)
                        dve.wait_ge(b_drained, b_order[e])
                        for t in range(2):
                            r = n * NT + 2 * k + t
                            gt = tok_gate[:, r:r + 1] if l == 0 else tanhg[:, 1:2]
                            last = dve.scalar_tensor_tensor(x[:, r, :], upd[:, t, :], gt, x[:, r, :], ALU.mult, ALU.add)
                        last.then_inc(x_upd, 1)
                        dve.wait_ge(x_upd, 2 * g + k + 1)

            def key_mask_row(l, g):
                dve.wait_ge(mrow_in, 16 * (g + 1))
                if g:
                    dve.wait_ge(slot_in[(g - 1) % 2][0], 16 * FILLS[0] * ((g - 1) // 2 + 1))
                ops = (-1.0, BIG, ALU.add, ALU.mult) if l == 0 else (0.0, None, ALU.mult)
                dve.tensor_scalar(mask_row[:, :], mrow8[:, :], *ops).then_inc(maskrow, 1)

            def mask_piece(e, n, k):
                if k < 4:
                    h = k % 2
                    dve.wait_ge(mstage_in, 16 * (4 * n + k + 1))
                    if k == 0 and n:
                        dve.wait_ge(m_ready, n)
                    dve.tensor_scalar(m_on[:, 2 * h:2 * h + 2, :], m_stage[:, :, :], 0.0, None,
                                      ALU.not_equal).then_inc(m_stage_free, 1)
                if k == 1:
                    dve.wait_ge(m_stage_free, 4 * n + 2)
                    link(dve.tensor_reduce(row_any[:, 0, :], m_on[:, :, :], AX.X, ALU.max))
                    link(dve.tensor_scalar(row_any[:, 1, :], row_any[:, 0, :], BIG, None, ALU.mult))
                    for t in range(NT):
                        last = dve.tensor_scalar(m_add_q[:, n % 2, t, :], m_on[:, t, :], -1.0, row_any[:, 1, t:t + 1],
                                                 ALU.add, ALU.mult)
                    link(last)
                if k == 4:
                    dve.wait_ge(b_filled, b_order[e])
                    dve.wait_ge(source_ok, sources(1, n, 1))
                    dve.tensor_scalar(any_bc, ps[:, B_BANK, :], 1.0, None, ALU.min).then_inc(b_drained, 1)
                    dve.wait_ge(b_drained, b_order[e])
                    link(dve.tensor_scalar(any_big, any_bc, BIG, None, ALU.mult))
                    for t in range(NT):
                        last = dve.scalar_tensor_tensor(m_add_k[:, (B + n) % 3, t, :], m_on[:, t, :], -1.0, any_big,
                                                        ALU.add, ALU.mult)
                    last.then_inc(m_ready, 1)

            maxima = [0]

            def junk_written():
                if maxima[0]:
                    dve.wait_ge(max_drained, maxima[0])

            def row_max(l, g, h, qt):
                o = 64 * g + 4 * h + qt
                maxima[0] = o + 1
                if h % 4 == 0 and qt == 0 and g:
                    pl, pn = divmod(g - 1, B)
                    dve.wait_ge(b_filled, b_order[(pl, "M", pn, h // 4)])
                dve.wait_ge(max_filled, o + 1)
                to, bank = max_q[:, 4 * h + qt:4 * h + qt + 1], ps[:, MAX_BANK[o % 2], :]
                if l == 0:
                    dve.tensor_reduce(to, bank, AX.X, ALU.max).then_inc(max_drained, 1)
                else:
                    dve.wait_ge(max_drained, o)
                    dve.tensor_tensor_reduce(junk, bank, m_add_q[:, (g - B) % 2, qt, :], 1.0, LOWEST,
                                             ALU.add, ALU.max, to).then_inc(max_drained, 1)

            count_from_one(dve, "dve")
            dve.wait_ge(const_in, 16 * CONSTS)
            dve.wait_ge(const_ok, 3)
            link(dve.memset(ps[:, PV_BANK, :], 0.0))
            link(dve.tensor_copy(key_on[:, :], km8[:, :]))
            dve.wait_ge(gate_ok, 1)
            link(dve.tensor_scalar(tok_gate[:, :], key_on[:, :], tanhg[:, 0:1], None, ALU.mult))
            attention(0)

            def norm_piece(s, l, n, count, piece):
                if piece == 0:
                    dve.wait_ge(x_upd, n * 2 + 2 + 2 * B * l)
                if piece == 3:
                    dve.wait_ge(s["t_filled"], 1 + n * KT)
                last = layer_norm(x[:, bass.ds(n * NT, NT), :], count, piece)
                if piece == 3:
                    last.then_inc(s["ln"], 1)

            def ff_norm(s, l, n, count):
                for piece in range(4):
                    norm_piece(s, l, n, count, piece)

            def token_rest(s, n, high, low, whole):
                for k in range(KT):
                    dve.wait_ge(s["t_hi"], n * KT + k + 1)
                    if whole is not None:
                        dve.tensor_copy(whole[:, k, :], ps[:, T_BANK, :])
                    dve.tensor_tensor(low[:, k, :], ps[:, T_BANK, :], high[:, k, :].bitcast(F32),
                                      ALU.subtract).then_inc(s["t_drained"], 1)

            s = ff[0]
            dve.wait_ge(a_filled, A_END[0])
            ff_norm(s, 0, 0, link)
            dve.wait_ge(s["w_in"], 16 * 5)
            link(dve.tensor_reduce(alpha1[:, :], w1_n[:, :, :], AX.X, ALU.add, apply_absolute_value=True))
            dve.tensor_scalar(alpha1[:, :], alpha1[:, :], 1.0 / D, None, ALU.mult).then_inc(alpha_ok, 1)
            dve.wait_ge(w2_sums, 1)
            dve.tensor_scalar(alpha2[:, :], ps[:, D_BANK[0], 0:D], 1.0 / HID, None, ALU.mult).then_inc(alpha_ok, 1)
            dve.wait_ge(alpha_ok, 2)
            token_rest(s, 0, xT_hi, xT_lo, None)

            def looped(sem_, per, n, start):
                made = [start]

                def count(ins):
                    made[0] += 1
                    ins.then_inc(sem_, 1)
                    dve.wait_ge(sem_, n * per + made[0])
                return count

            def output0(n, count):
                for half in range(2):
                    dve.wait_ge(s["d_filled"], 1 + n * 2 + half + 1)
                    dve.tensor_tensor(upd[:, :, :], ps[:, D_BANK[half], :].rearrange("p (t n) -> p t n", t=2),
                                      alpha2[:, :].unsqueeze(1).to_broadcast([P, 2, D]), ALU.mult).then_inc(s["d_drained"], 1)
                    dve.wait_ge(s["d_drained"], 1 + n * 2 + half + 1)
                    count(dve.tensor_tensor(upd[:, :, :], upd[:, :, :], b2_bc[:, :].unsqueeze(1).to_broadcast([P, 2, D]),
                                            ALU.add))
                    rows = x[:, bass.ds(n * NT + 2 * half, 2), :]
                    dve.scalar_tensor_tensor(rows, upd[:, :, :], tanhg[:, 2:3], rows, ALU.mult,
                                             ALU.add).then_inc(s["x_done"], 1)
                    dve.wait_ge(s["x_done"], n * 2 + half + 1)

            PER0 = LN_LINKS + 2
            with dve.Fori(0, B - 1) as n:
                c = looped(chain0, PER0, n, 0)
                ff_norm(s, 0, n + 1, c)
                token_rest(s, n + 1, xT_hi, xT_lo, None)
                output0(n, c)
            output0(B - 1, looped(chain0, PER0, B - 1, 0))

            attention(1)

            s = ff[1]

            def gating(n, count):
                dve.wait_ge(s["r_filled"], n * 1 + 1)
                count(dve.tensor_copy(logit[:, :, :], ps[:, R_BANK, 0:NT * EXPERTS].rearrange("p (t n) -> p t n", t=NT)))
                stand()
                for t in range(NT):
                    last = dve.max(top[:, t, :], logit[:, t, :])
                count(last)
                stand()
                for t in range(NT):
                    last = dve.max_index(top_i[:, t, :], top[:, t, :], logit[:, t, :])
                count(last)
                count(dve.tensor_copy(top_f[:, :, :], top_i[:, :, 0:2]))
                dve.tensor_tensor(g_w[:, :, 0:1], top[:, :, 1:2], top[:, :, 0:1], ALU.subtract).then_inc(s["g_diff"], 1)
                dve.wait_ge(s["g_exp"], n * 1 + 1)
                count(dve.tensor_scalar(g_w[:, :, 2:3], g_w[:, :, 1:2], 1.0, None, ALU.add))
                count(dve.reciprocal(g_w[:, :, 2:3], g_w[:, :, 2:3]))
                count(dve.tensor_scalar(g_w[:, :, 2:3], g_w[:, :, 2:3], tanhg[:, 3:4], None, ALU.mult))
                count(dve.tensor_tensor(g_w[:, :, 3:4], g_w[:, :, 1:2], g_w[:, :, 2:3], ALU.mult))
                for t in range(NT):
                    count(dve.tensor_scalar(hot[:, 0, :], iota_e[:, :], top_f[:, t, 0:1], g_w[:, t, 2:3], ALU.is_equal, ALU.mult))
                    count(dve.tensor_scalar(hot[:, 1, :], iota_e[:, :], top_f[:, t, 1:2], g_w[:, t, 3:4], ALU.is_equal, ALU.mult))
                    count(dve.tensor_tensor(gate[:, t, SHARED:UNITS], hot[:, 0, :], hot[:, 1, :], ALU.add))
                    last = dve.tensor_scalar(gate[:, t, 0:SHARED], ones_f[:, 0:SHARED], tanhg[:, 3:4], None, ALU.mult)
                last.then_inc(s["gate"], 1)
                dve.wait_ge(s["gate"], 1 + n * 1 + 1)

            def output1(n, e):
                for half in range(2):
                    u = 2 * e + half
                    dve.wait_ge(s["d_filled"], 1 + n * 2 * UNITS + u + 1)
                    dve.wait_ge(s["d_drained"], 1 + n * 2 * UNITS + u)
                    for t in range(2):
                        rows = x[:, bass.ds(n * NT + 2 * half + t, 1), :]
                        last = dve.scalar_tensor_tensor(rows, ps[:, D_BANK[half], t * D:(t + 1) * D].unsqueeze(1),
                                                        gate[:, 2 * half + t, e:e + 1], rows, ALU.mult, ALU.add)
                    last.then_inc(s["d_drained"], 1)

            def squares(n, e):
                for t in range(UT):
                    o = UT * e + t
                    dve.wait_ge(s["u_drained"], 1 + n * UNITS * UT + o + 1)
                    h = raw1[:, o % 4, :]
                    dve.tensor_tensor(h, h, h, ALU.mult).then_inc(s["squared"], 1)

            PER1 = LN_LINKS + GATE_LINKS

            def experts(n, last):
                c = looped(chain1, PER1, n, 0)
                for e in range(UNITS + 2):
                    if e < UNITS:
                        squares(n, e)
                    if e == 1:
                        gating(n, c)
                    if e == UNITS and not last:
                        token_rest(s, n + 1, xT_hi1, xT_lo1, xT)
                    if e >= 2:
                        output1(n, e - 2)
                    if 3 <= e < 7 and not last:
                        norm_piece(s, 1, n + 1, c, e - 3)

            dve.wait_ge(a_filled, A_END[1])
            ff_norm(s, 1, 0, link)
            token_rest(s, 0, xT_hi1, xT_lo1, xT)
            with dve.Fori(0, B - 1) as n:
                experts(n, False)
            experts(B - 1, True)


def tables_of_shape():
    inv = (1.0 / np.float32(10000.0) ** (np.arange(0, HD, 2, dtype=np.float32) / np.float32(HD))).astype(np.float32)
    angle = np.outer(np.arange(S, dtype=np.float32), inv).astype(np.float32)
    angle = np.concatenate([angle, angle], axis=1)
    rot = np.zeros((P, P), np.float32)
    for m in range(P):
        low = m % HD < HD // 2
        rot[m + HD // 2 if low else m - HD // 2, m] = -1.0 if low else 1.0
    return {
        "ident": np.eye(P, dtype=np.float32), "rot": rot,
        "cosT": np.tile(np.cos(angle).T, (P // HD, 1)).astype(np.float32),
        "sinT": np.tile(np.sin(angle).T, (P // HD, 1)).astype(np.float32),
        "iota": np.arange(EXPERTS, dtype=np.float32),
        "ones_row": np.full((4, 2 * HEADS * S), 0x3F80, np.uint16)
    }


def expert_units(ws1, ws2, w1, w2):
    up = np.concatenate([ws1.reshape(SHARED, EF, D), w1]).transpose(0, 2, 1)
    down = np.concatenate([ws2.reshape(D, SHARED, EF).transpose(1, 2, 0), w2.transpose(0, 2, 1)])
    tiles = np.stack([up.reshape(UNITS, KT, P, EF), down.reshape(UNITS, UT, P, D)], axis=1)
    return tiles.transpose(0, 1, 3, 2, 4).reshape(UNITS, 2, P, UT * D)


def kernel(x, ctx_1024, mask_BxS2_bf1, mask_Bx1xSxS2_if1, g_xattn, g_ffn,
           L0_xattn_Wq, L0_xattn_bq, L0_xattn_Wk, L0_xattn_bk, L0_xattn_Wv, L0_xattn_bv, L0_xattn_Wp, L0_xattn_bp,
           L0_ffn_w1, L0_ffn_b1, L0_ffn_w2, L0_ffn_b2,
           L1_xattn_W_q, L1_xattn_b_q, L1_xattn_W_k, L1_xattn_b_k, L1_xattn_W_v, L1_xattn_b_v, L1_xattn_W_o, L1_xattn_b_o,
           L1_ffn_w_router, L1_ffn_w1_stack, L1_ffn_w2_stack, L1_ffn_ws1, L1_ffn_ws2):
    import concourse.bacc as bacc
    from concourse.bass_utils import run_bass_kernel_spmd

    A = np.asarray
    key_mask = A(mask_BxS2_bf1).view(np.uint8)
    pair_mask = A(mask_Bx1xSxS2_if1)[:, 0]
    arrays = {
        "x": A(x), "ctxT": A(ctx_1024).transpose(0, 2, 1), "g_xattn": A(g_xattn), "g_ffn": A(g_ffn),
        "mask_col": key_mask.reshape(B * NT, P).T, "mask_row": key_mask,
        "mask_q": pair_mask, "mask_k": pair_mask.transpose(0, 2, 1),
        "l0_wq": A(L0_xattn_Wq).T, "l0_wk": A(L0_xattn_Wk).T, "l0_wv": A(L0_xattn_Wv).T, "l0_wo": A(L0_xattn_Wp).T,
        "l0_bqk": np.concatenate([A(L0_xattn_bk).reshape(KT, P), A(L0_xattn_bq).reshape(KT, P)]).T,
        "l0_bv": A(L0_xattn_bv), "l0_bo": A(L0_xattn_bp),
        "l1_wq": A(L1_xattn_W_q), "l1_wk": A(L1_xattn_W_k), "l1_wv": A(L1_xattn_W_v), "l1_wo": A(L1_xattn_W_o),
        "l1_bqk": np.concatenate([A(L1_xattn_b_k).reshape(KT, P), A(L1_xattn_b_q).reshape(KT, P)]).T,
        "l1_bv": A(L1_xattn_b_v), "l1_bo": A(L1_xattn_b_o),
        "w1": A(L0_ffn_w1), "w1T": A(L0_ffn_w1).T, "b1": A(L0_ffn_b1).reshape(HT, P).T, "w2T": A(L0_ffn_w2).T, "b2": A(L0_ffn_b2),
        "w_router": A(L1_ffn_w_router).T,
        "units": expert_units(A(L1_ffn_ws1), A(L1_ffn_ws2), A(L1_ffn_w1_stack), A(L1_ffn_w2_stack)),
        **tables_of_shape(),
    }
    arrays = {name: np.ascontiguousarray(a) for name, a in arrays.items()}
    nc = bacc.Bacc("TRN2", target_bir_lowering=False, num_devices=1)
    d = {name: nc.dram_tensor(f"in_{name}", a.shape, mybir.dt.from_np(a.dtype), kind="ExternalInput").ap()
         for name, a in arrays.items()}
    out = nc.dram_tensor("out", [B, S, D], F32, kind="ExternalOutput").ap()
    bass_flamingo(nc, d, out)
    r = run_bass_kernel_spmd(nc, [{f"in_{name}": a for name, a in arrays.items()}], core_ids=[0])
    return r.results[0]["out"]
```

```python
from contextlib import ExitStack

import numpy as np
import concourse.bass as bass
from concourse import mybir

F32 = mybir.dt.float32
F32R = mybir.dt.float32r
BF16 = mybir.dt.bfloat16
I32 = mybir.dt.int32
U32 = mybir.dt.uint32
U16 = mybir.dt.uint16
U8 = mybir.dt.uint8
ALU = mybir.AluOpType
ACT = mybir.ActivationFunctionType
AX = mybir.AxisListType

P = 128
B, S, D = 4, 512, 256
HEADS, HD = 16, 16
NT = S // P
KT = D // P
HID = 1024
HT = HID // P
EXPERTS, EF, SF = 8, 256, 512
SHARED = SF // EF
UNITS = SHARED + EXPERTS
POOL_TILES = 6
DVE_TILES = HT - POOL_TILES
UT = EF // P
EPS = 1e-5
BIG = 1e30
LOWEST = -3e38
SCALE = HD ** -0.5
VW = HD + 1

PARTS = 6 * HD
MAX_K = PARTS + 1
ST_K = MAX_K + 3
Q_PART = [0, 1, 2, 0, 1, 0]
K_PART = [0, 0, 0, 1, 1, 2]
ITEMS = 4
FILLS = (6 + 6 + 1, 6 + 6)
CONSTS = 8
NEWTON = 3
LN_LINKS, GATE_LINKS = 5 + 3 * NEWTON, 19
EARLY_UNITS = 4
LAG = 9
EARLY = 14
STEPS = 16


def plan_layer(masked):
    prep = {1: [("LN", 0), ("LN", 1)], 2: [("LN", 2), ("LN", 3)], 3: [("T", 0), ("T", 1)]}
    if not masked:
        prep |= {4: [("J", 0)], 5: [("J", 1), ("R", 0)], 6: [("H", 0), ("R", 1)], 7: [("D", 0), ("H", 1)],
                 8: [("D", 1)], 9: [("J", 2)], 10: [("J", 3), ("R", 2)], 11: [("H", 2), ("R", 3)],
                 12: [("D", 2), ("H", 3)], 13: [("D", 3)]}
    else:
        prep |= {4: [("J", 0), ("C", 0)], 5: [("J", 1), ("H", 0)], 6: [("D", 0), ("C", 1)], 7: [("H", 1)],
                 8: [("D", 1), ("C", 2)], 9: [("J", 2)], 10: [("J", 3), ("C", 3)], 11: [("C", 4), ("C", 5)],
                 12: [("H", 2)], 13: [("D", 2), ("H", 3)], 14: [("D", 3)]}

    if masked:
        norm = [("LN", 0, k) for k in range(4)]
        queries = [("T", 0, 0), ("T", 0, 1), ("J", 0, 2), ("J", 0, 3), ("F", 0, 0), ("F", 0, 1), ("LN", 1, 0), ("H", 0, 2),
                   ("LN", 1, 1), ("D", 0, 2), ("F", 0, 2), ("H", 0, 3), ("LN", 1, 2), ("D", 0, 3), ("F", 0, 3), ("LN", 1, 3)]
        plan = [("C", 0, 5)]
    else:
        norm, queries = [("LN", 0, k) for k in range(4)] + [("J", 0, 0)], []
        plan = [("R", 0, 0), ("J", 0, 1), ("H", 0, 0), ("R", 0, 1), ("D", 0, 0), ("F", 0, 0), ("T", 0, 0),
                 ("T", 0, 1), ("H", 0, 1), ("J", 0, 2), ("R", 0, 2), ("D", 0, 1), ("F", 0, 1), ("LN", 1, 0), ("J", 0, 3),
                 ("H", 0, 2), ("LN", 1, 1), ("R", 0, 3), ("D", 0, 2), ("F", 0, 2), ("LN", 1, 2), ("H", 0, 3), ("D", 0, 3),
                 ("F", 0, 3), ("LN", 1, 3)]
    plan += [("V", 0, 0), ("V", 0, 1)]
    for q in range(3 - EARLY, B * STEPS + 5):
        n, s = q // STEPS, q % STEPS
        side = []
        done = q + LAG - 2
        if 0 <= done < B * STEPS and done % 4 == 3:
            side.append(("M", done // STEPS, done % STEPS // 4))
        if q >= 5 and q % 4 == 1 and q <= B * STEPS + 1:
            side.append(("OT", (q - 2) // STEPS, (q - 2) % STEPS // 4))
        if n >= 1:
            side += {2: [("OF", n - 1, 0), ("OF", n - 1, 1)], 3: [("OP", n - 1, 0)], 4: [("OP", n - 1, 1)]}.get(s, [])
        if n + 1 < B and q >= 0 and s in (14, 15):
            side.append(("V", n + 1, s - 14))
        if 0 <= q and n + 2 < B:
            side += [(kind, n + 2, k) for kind, k in prep.get(s, [])]
        side += [(kind, 1, k) for kind, k in prep.get(q + EARLY, []) if kind != "LN"]
        if n >= 1 and n + 1 < B and s < 2:
            side += [("F", n + 1, s), ("F", n + 1, 2 + s)]
        if q in (2, 3):
            side += [("F", 1, q - 2), ("F", 1, q)]
        if n == B - 1:
            side += {1: [("LOAD", 0, 0)], 4: [("NORM", 0, 0)], 5: [("NORM", 0, 1)], 6: [("NORM", 0, 2)],
                     7: [("NORM", 0, 3)], 9: [("NEXT", 0, 0)], 10: [("NEXT", 0, 1)]}.get(s, [])
            if masked and 10 <= s < 10 + EARLY_UNITS:
                side.append(("UNIT", 0, s - 10))
            if not masked:
                side += {3: [("C1", 0, 0)], 5: [("J1", 0, 0), ("C1", 0, 1)], 6: [("J1", 0, 1), ("H1", 0, 0)], 7: [("D1", 0, 0)],
                         8: [("H1", 0, 1), ("C1", 0, 2)], 11: [("D1", 0, 1)], 12: [("C1", 0, 3)], 14: [("C1", 0, 4)]}.get(s, [])
        for j in range(4):
            if 0 <= q < B * STEPS:
                plan.append(("SCORE", n, 4 * s + j))
            if 0 <= q + LAG < B * STEPS:
                plan.append(("MAX", (q + LAG) // STEPS, 4 * ((q + LAG) % STEPS) + j))
            if j == 1 and 0 < q <= B * STEPS:
                plan.append(("PV", (q - 1) // STEPS, (q - 1) % STEPS))
            plan += side[j * len(side) // 4:(j + 1) * len(side) // 4]
        if q >= 4 and q % 4 == 0 and q <= B * STEPS:
            plan.append(("E", (q - 1) // STEPS, (q - 1) % STEPS // 4))
    return norm, queries, plan


def bass_flamingo(nc, d, out):
    ctx = ExitStack()
    with ctx:
        def sb(name, shape, dt=F32):
            return ctx.enter_context(nc.sbuf_tensor(name, shape, dt))

        def sem(name):
            return ctx.enter_context(nc.semaphore(name))

        x = sb("x_tok", [P, B * NT, D])
        xn = sb("xn", [P, NT, D])
        v_tmp = sb("v_tmp", [P, 2, D])
        upd = v_tmp
        junk = v_tmp[:, 0, :].bitcast(BF16)
        ident = sb("ident", [P, P])
        ident_b = sb("ident_b", [P, P], BF16)
        ones_b = sb("ones_b", [P, P], BF16)
        ones_f = sb("ones_f", [P, HEADS])
        gates = sb("gates", [P, 4])
        tanhg = sb("tanhg", [P, 4])
        km8 = sb("km8", [P, B * NT], U8)
        key_on = sb("key_on", [P, B * NT])
        tok_gate = sb("tok_gate", [P, B * NT])
        stats = sb("stats", [P, NT, 6])
        mv = sb("mv", [P, NT, 2])
        nw = sb("nw", [P, 4, NT])
        alpha1 = sb("alpha1", [P, HT])
        b1_col = sb("b1_col", [P, HT])
        w_rt = sb("w_rt", [P, KT, EXPERTS])
        logit = sb("logit", [P, NT, EXPERTS])
        top = sb("top", [P, NT, 8])
        top_i = sb("top_i", [P, NT, 8], U32)
        top_f = sb("top_f", [P, NT, 2])
        g_w = sb("g_w", [P, NT, 4])
        hot = sb("hot", [P, 2, EXPERTS])
        gate = sb("gate", [P, NT, UNITS])
        iota_e = sb("iota_e", [P, EXPERTS])

        with ExitStack() as stack:
            def over(name, shape, dt=F32):
                return stack.enter_context(nc.sbuf_tensor(name, shape, dt))
            w1_f = over("w1_float", [P, KT, HID])
            w1_n = over("w1_natural", [P, HT, D])
            w1_s = over("w1_sign", [P, KT, HID], F32R)
            w2_s = over("w2_sign", [P, HT, D], F32R)
            w2_f = over("w2_float", [P, HT, D])
            xT_hi = over("xT_hi", [P, KT, S], F32R)
            xT_lo = over("xT_lo", [P, KT, S], F32R)
            alpha2 = over("alpha2", [P, D])
            b2_bc = over("b2_bc", [P, D])
        with ExitStack() as stack:
            def over(name, shape, dt=F32):
                return stack.enter_context(nc.sbuf_tensor(name, shape, dt))
            we_f = [over(f"we_float{j}", [P, 2, 2, UT * D]) for j in range(2)]
            we_f.append(over("we_float2", [P, 2, 2, UT * D]))
            raw1 = over("raw1", [P, 4, S])
            xT = over("xT", [P, KT, S])
            xT_hi1 = over("xT_hi1", [P, KT, S], F32R)
            xT_lo1 = over("xT_lo1", [P, KT, S], F32R)
            over("unused", [P, KT, S])
            we_f += [over(f"we_float{j}", [P, 2, 2, UT * D]) for j in (3, 4)]

        big = sb("operands", [P, 2 * 2 * HEADS * S], BF16)
        q_op = big[:, 0:2 * HEADS * S].rearrange("p (s h n) -> p s h n", s=2, h=HEADS)
        k_op = big[:, 2 * HEADS * S:].rearrange("p (s h n) -> p s h n", s=2, h=HEADS)

        with ExitStack() as stack:
            def over(name, shape, dt=F32):
                return stack.enter_context(nc.sbuf_tensor(name, shape, dt))
            we = over("we_parts", [P, UNITS, 2, 2, UT * D], F32R)
            hid1 = over("hid1", [P, 2, 2, UT, S], F32R)

        parts = sb("parts", [P, ITEMS, 3, S], BF16)
        ctx_k = sb("ctx_k", [P, KT, S])
        ctx_v = sb("ctx_v", [P, KT, S])
        xnT = sb("xnT", [P, KT, S])
        f = sb("f", [P, ITEMS, S])
        w_att = sb("w_att", [P, 4, KT, D])
        bqk = sb("bqk", [P, 2, ITEMS])
        bv_bc = sb("bv_bc", [P, D])
        bo_bc = sb("bo_bc", [P, D])
        tables = sb("tables", [P, 2, S])
        cos_t, sin_t = tables[:, 0, :], tables[:, 1, :]
        any_bc, any_big = tables[:, 0, :], tables[:, 1, :]
        rot_m = sb("rot_m", [P, P])
        rotated = sb("rotated", [P, S])
        rest = sb("rest", [P, S])
        mrow8 = sb("mrow8", [1, S], U8)
        mask_row = sb("mask_row", [1, S], BF16)
        m_stage = sb("m_stage", [P, 2, S], I32)
        rot_tmp = m_stage[:, 0, :].bitcast(F32)
        m_off = sb("m_off", [P, NT, S], BF16)
        m_add_q = sb("m_add_q", [P, 2, NT, S], BF16)
        row_any = sb("row_any", [P, 2, NT])

        with ExitStack() as stack:
            def over(name, shape, dt=F32):
                return stack.enter_context(nc.sbuf_tensor(name, shape, dt))
            raw0 = over("raw0", [P, 4, S])
            hid0_hi = over("hid0_hi", [P, HT, S], F32R)
            hid0_lo = over("hid0_lo", [P, HT, S], F32R)

        probs = sb("probs", [P, 2, 4, S])
        values = sb("values", [P, 2, NT, HEADS, VW])
        m_add_k = sb("m_add_k", [P, 3, NT, S], BF16)
        o_tok = sb("o_tok", [P, NT, D])
        o_heads = sb("o_heads", [P, 2, S])
        o_feat = sb("o_feat", [P, KT, S])
        max_q = sb("max_q", [P, HEADS * NT])
        m_rest = sb("m_rest", [4 * NT, 2, P])
        m_parts = sb("m_parts", [4 * NT, 2, 3, P], BF16)
        rec = sb("rec", [P, NT, 4])

        ps = ctx.enter_context(nc.psum_tensor("ps", [P, 8, S], F32))
        ST_BANK, MAX_BANK, PV_BANK, A_BANK, B_BANK = (0, 1), (2, 3, 4), 5, 6, 7

        x_in = [sem(f"x_in{n}") for n in range(B)]
        const_in = sem("const_in")
        wk_in = sem("wk_in")
        w_in = sem("w_in")
        wo_in = sem("wo_in")
        const_ok = sem("const_ok")
        gate_ok = sem("gate_ok")
        pool_chain = sem("pool_chain")
        chain = sem("dve_chain")
        ln_done = sem("ln_done")
        a_filled, a_drained = sem("a_filled"), sem("a_drained")
        b_filled, b_drained = sem("b_filled"), sem("b_drained")
        ctxk_in, ctxv_in = sem("ctxk_in"), sem("ctxv_in")
        cos_done = sem("cos_done")
        source_ok = sem("source_ok")
        hi_done, mid_done = sem("hi_done"), sem("mid_done")
        rest_done, split_done = sem("rest_done"), sem("split_done")
        spill = [sem(f"spill{i}") for i in range(ITEMS)]
        slot_in = [[sem(f"slot_in{i}{h}") for h in range(2)] for i in range(2)]
        maxrow_in = [sem(f"maxrow_in{i}") for i in range(2)]
        maskrow = sem("maskrow")
        mrow_in = sem("mrow_in")
        max_filled, max_drained = sem("max_filled"), sem("max_drained")
        st_filled, exp_done = sem("st_filled"), sem("exp_done")
        pv_done, heads_out = sem("pv_done"), sem("heads_out")
        v_ready = sem("v_ready")
        m_split = sem("m_split")
        key_ok = sem("key_ok")
        x_upd = sem("x_upd")
        mstage_in = sem("mstage_in")
        m_stage_free = sem("m_stage_free")
        rows_in = sem("rows_in")
        out_done = sem("out_done")
        q_mask = sem("q_mask")
        any_ok = sem("any_ok")
        m_ready = sem("m_ready")

        stretches = [[[(1, kind[0], n, k) if kind[1:] == "1" else (l, kind, n, k) for kind, n, k in part]
                      for part in plan_layer(masked=l == 1)] for l in range(2)]
        plans = [a + b + c for a, b, c in stretches]
        plan = plans[0] + plans[1]
        a_order = {e: j + 1 for j, e in enumerate(e for e in plan if e[1] in ("T", "J", "OF", "NEXT"))}
        b_order = {e: j + 1 for j, e in enumerate(e for e in plan if e[1] in ("R", "V", "M", "OT", "OP") or e[1:4:2] == ("C", 4))}
        A_END, B_END = [], []
        for l in range(2):
            A_END.append(a_order[(l, "OF", B - 1, 1)])
            B_END.append(b_order[(l, "OP", B - 1, 1)])

        scratch = nc.dram_tensor("qk_parts", [2 * B * ITEMS, 8, HD, 3, S], BF16, kind="Internal").ap()

        def batch(l, n):
            return l * B + n

        def sources(l, n, k):
            return ITEMS * n + k + 1 if l == 0 else ITEMS * B + 2 * n + k - 1

        ff = [dict((k, sem(f"ff{l}_{k}")) for k in (
            "ln",
            "t_filled",
            "t_hi", "t_drained",
            "u_filled",
            "u_drained",
            "squared",
            "h_hi", "h_lo",
            "h_lo_dve",
            "d_filled",
            "d_drained",
            "w_in", "w_hi", "w_lo", "r_filled", "g_diff", "g_exp", "gate", "x_done")) for l in range(2)]
        units_in = [sem(f"units_in{j}") for j in range(UNITS // 2)]
        FROM_ONE = {"pe": [(0, "t_filled"), (0, "d_filled"), (1, "t_filled"), (1, "d_filled")],
                    "act": [(0, "u_drained"), (1, "u_drained")],
                    "dve": [(0, "h_lo_dve"), (0, "t_drained"), (0, "d_drained"), (1, "t_drained"), (1, "d_drained"), (1, "gate")],
                    "pool": [(0, "h_lo"), (1, "h_lo")]}

        def count_from_offe(eng, who):
            for l, k in FROM_ONE[who]:
                eng.sem_inc(ff[l][k], 1 + KT if k in ("t_filled", "t_drained") else 1)

        alpha_ok = sem("alpha_ok")
        w2_sums = sem("w2_sums")
        stood = sem("stood")
        chain0, chain1 = sem("dve_chain_ff0"), sem("dve_chain_ff1")

        U_BANK, D_BANK, T_BANK, R_BANK = (0, 1, 2, 3), (4, 5), (6, 7), 7

        block = ctx.enter_context(nc.Block())

        @block.sync
        def _(sp):
            def load(dst, src, s):
                sp.dma_start(dst, src).then_inc(s, 16)

            def load_weights(l):
                if l:
                    sp.wait_ge(a_filled, a_order[(0, "J", B - 1, 3)])
                    sp.wait_ge(b_drained, b_order[(0, "V", B - 1, 1)])
                load(w_att[:, 1, :, :], d[f"l{l}_wk"].rearrange("(k p) n -> p k n", p=P), wk_in)
                load(bqk[:, l, :], d[f"l{l}_bqk"], wk_in)
                if l == 0:
                    ctx_k_load(0, 0)
                    constants()
                load(w_att[:, 0, :, :], d[f"l{l}_wq"].rearrange("(k p) n -> p k n", p=P), w_in)
                load(w_att[:, 2, :, :], d[f"l{l}_wv"].rearrange("(k p) n -> p k n", p=P), w_in)
                load(bv_bc[:, :], d[f"l{l}_bv"].partition_broadcast(P), w_in)

            def load_output_weights(l):
                if l:
                    sp.wait_ge(x_upd, 2 * B)
                load(w_att[:, 3, :, :], d[f"l{l}_wo"].rearrange("(k p) n -> p k n", p=P), wo_in)
                load(bo_bc[:, :], d[f"l{l}_bo"].partition_broadcast(P), wo_in)

            def load_ctx(dst, n, s):
                load(dst[:, :, :], d["ctxT"][n].rearrange("(k p) n -> p k n", p=P), s)

            def ctx_k_load(l, n):
                if batch(l, n):
                    pl, pn = divmod(batch(l, n) - 1, B)
                    sp.wait_ge(a_filled, a_order[(pl, "J", pn, 1)])
                load_ctx(ctx_k, n, ctxk_in)

            def ctx_v_load(l, n):
                if batch(l, n):
                    pl, pn = divmod(batch(l, n) - 1, B)
                    sp.wait_ge(b_filled, b_order[(pl, "V", pn, 1)])
                load_ctx(ctx_v, n, ctxv_in)

            def mask_load(n, j):
                if n or j:
                    sp.wait_ge(m_stage_free, 4 * n + j)
                else:
                    sp.wait_ge(source_ok, ITEMS * B)
                src = d["mask_q"] if j < 2 else d["mask_k"]
                h = j % 2
                load(m_stage[:, :, :], src[n].rearrange("(t p) k -> p t k", p=P)[:, 2 * h:2 * h + 2, :], mstage_in)

            def spill_parts(g, k):
                sp.wait_ge(split_done, ITEMS * g + k + 1)
                load(scratch[ITEMS * g + k].rearrange("h d j n -> (h d) j n"), parts[:, k, :, :], spill[k])

            def fill_slot(g, item):
                sl, half = g % 2, item % 2
                if g >= 2 and item == 0:
                    sp.wait_ge(st_filled, 64 * (g - 1))
                operand, order = (k_op, K_PART) if item < 2 else (q_op, Q_PART)
                if item == 2:
                    sp.wait_ge(maskrow, g + 1)
                    load(k_op[PARTS:PARTS + 1, sl, :, :], mask_row[:, :].unsqueeze(1).to_broadcast([1, HEADS, S]), slot_in[sl][half])
                sp.wait_ge(spill[item], 16 * (g + 1))
                for b, j in enumerate(order):
                    load(operand[b * HD:(b + 1) * HD, sl, 8 * half:8 * half + 8, :],
                         scratch[ITEMS * g + item][:, :, j, :].rearrange("h d n -> d h n"), slot_in[sl][half])

            def fill_max_rows(g, gg):
                mg = 4 * g + gg
                sp.wait_ge(m_split, mg + 1)
                for j in range(3):
                    r = MAX_K + j
                    load(q_op[r:r + 1, g % 2, 4 * gg:4 * gg + 4, :].rearrange("p h (t n) -> p (h t) n", n=P),
                         m_parts[:, mg % 2, j, :], maxrow_in[mg % 2])

            def row_mask(l, n):
                g = batch(l, n)
                if g:
                    sp.wait_ge(maskrow, g)
                load(mrow8[:, :], d["mask_row"][n:n + 1, :], mrow_in)

            def constants():
                load(ident[:, :], d["ident"], const_in)
                load(rot_m[:, :], d["rot"], const_in)
                load(cos_t, d["cosT"], const_in)
                load(sin_t, d["sinT"], const_in)
                load(gates[:, 0:2], d["g_xattn"].partition_broadcast(P), const_in)
                load(gates[:, 2:4], d["g_ffn"].partition_broadcast(P), const_in)
                load(km8[:, :], d["mask_col"], const_in)
                load(iota_e[:, :], d["iota"].partition_broadcast(P), const_in)

            rows = [0]

            def ones_rows(sl):
                load(q_op[PARTS:MAX_K, sl, :, :].bitcast(U16), d["ones_row"][0:1], rows_in)
                load(k_op[PARTS:ST_K, sl, :, :].bitcast(U16), d["ones_row"], rows_in)
                rows[0] += 32
                sp.wait_ge(rows_in, rows[0])

            def next_weights(l):
                sp.wait_ge(st_filled, 64 * (B * (l + 1) - 1))
                w = ff[l]["w_in"]
                if l == 0:
                    load(w1_n[:, :, :], d["w1"].rearrange("(k p) n -> p k n", p=P), w)
                    load(w1_f[:, :, :], d["w1T"].rearrange("(k p) n -> p k n", p=P), w)
                    load(w2_f[:, :, :], d["w2T"].rearrange("(k p) n -> p k n", p=P), w)
                    load(b1_col[:, :], d["b1"], w)
                else:
                    load(w_rt[:, :, :], d["w_router"].rearrange("(k p) n -> p k n", p=P), w)
                    for j in range(2):
                        unit_pair(j)

            def unit_pair(j):
                load(we_f[j][:, :, :, :], d["units"][2 * j:2 * j + 2].rearrange("e j p c -> p (e j) c"), units_in[j])

            load(x[:, 0:NT, :], d["x"][0].rearrange("(t p) n -> p t n", p=P), x_in[0])
            load_weights(0)
            load_output_weights(0)
            for n in range(1, B):
                load(x[:, n * NT:(n + 1) * NT, :], d["x"][n].rearrange("(t p) n -> p t n", p=P), x_in[n])

            for layer in range(2):
                if layer:
                    load_output_weights(1)
                else:
                    ones_rows(0)
                    ones_rows(1)
                ctx_v_load(layer, 0)
                for l, kind, n, k in plans[layer]:
                    g = batch(l, n)
                    if kind == "F" and l == 1 and n == 0 and k == 0:
                        sp.wait_ge(ff[0]["u_filled"], HT * B)
                        ones_rows(0)
                    if kind == "J" and l == 1 and n == 1 and k == 0:
                        sp.wait_ge(ff[0]["x_done"], 2 * B)
                        ones_rows(1)
                    if kind == "LOAD":
                        if l == 0:
                            mask_load(0, 0)
                            load_weights(1)
                            ctx_k_load(1, 0)
                        next_weights(l)
                    if kind == "LN" and k == 0 and n:
                        ctx_k_load(l, n)
                    if kind == "J" and k == 2:
                        row_mask(l, n)
                    if kind == "C" and k < 4 and (k < 3 or n + 1 < B):
                        mask_load(n + (k == 3), (k + 1) % 4)
                    if kind == "D":
                        spill_parts(g, k)
                    if kind == "F":
                        fill_slot(g, k)
                    if kind == "M":
                        fill_max_rows(g, k)
                    if kind == "V" and k == 1 and n + 1 < B:
                        ctx_v_load(l, n + 1)
                sp.wait_ge(st_filled, 64 * B * (layer + 1))
                if layer == 0:
                    load(b2_bc[:, :], d["b2"].partition_broadcast(P), ff[0]["w_in"])
                else:
                    for j in range(2, UNITS // 2):
                        unit_pair(j)
            with sp.Fori(0, B) as n:
                sp.wait_ge(ff[1]["d_drained"], 1 + n * 2 * UNITS + 2 * UNITS)
                sp.dma_start(out[bass.ds(n, 1), :, :].rearrange("a (t p) n -> p (a t) n", p=P),
                             x[:, bass.ds(n * NT, NT), :]).then_inc(out_done, 16)
            sp.wait_ge(out_done, 16 * B)

        @block.gpsimd
        def _(pool):
            count_from_offe(pool, "pool")
            pool.memset(ones_b[:, :], 1.0).then_inc(const_ok, 1)
            pool.memset(ones_f[:, :], 1.0).then_inc(const_ok, 1)
            pool.wait_ge(const_in, 16 * CONSTS)
            pool.tensor_copy(ident_b[:, :], ident[:, :]).then_inc(const_ok, 1)

            links = [0]

            def link(ins):
                links[0] += 1
                ins.then_inc(pool_chain, 1)
                pool.wait_ge(pool_chain, links[0])

            def attention(layer, stretch):
                for e in stretches[layer][stretch]:
                    l, kind, n, k = e
                    g = batch(l, n)
                    item = ITEMS * g + k
                    if kind == "R" or kind == "H" and l == 1 and k >= 2:
                        if item:
                            pool.wait_ge(hi_done, item)
                            pool.wait_ge(rest_done, item)
                        pool.wait_ge(a_drained, a_order[(l, "J", n, k)])
                        if l == 0:
                            pool.tensor_tensor(rotated[:, :], f[:, k, :], cos_t, ALU.mult).then_inc(cos_done, 1)
                            pool.wait_ge(cos_done, item + 1)
                            pool.wait_ge(b_drained, b_order[(l, "R", n, k)])
                            pool.tensor_tensor(rotated[:, :], rotated[:, :], rot_tmp, ALU.add).then_inc(source_ok, 1)
                        else:
                            pool.wait_ge(any_ok, n + 1)
                            pool.tensor_tensor(rotated[:, :], f[:, k, :], any_bc, ALU.mult).then_inc(source_ok, 1)
                    if kind == "C" and k < 4:
                        h = k % 2
                        pool.wait_ge(mstage_in, 16 * (4 * n + k + 1))
                        if k == 0 and n:
                            pool.wait_ge(m_ready, n)
                        if k >= 2:
                            pool.wait_ge(q_mask, 2 * n + h + 1)
                        pool.tensor_scalar(m_off[:, 2 * h:2 * h + 2, :], m_stage[:, :, :], 0.0, None,
                                           ALU.is_equal).then_inc(m_stage_free, 1)
                    if kind == "UNIT":
                        early_unit(k)
                    if kind == "C" and k == 5:
                        if n == 0:
                            pool.wait_ge(ff[0]["d_filled"], 1 + 2 * B)
                        pool.wait_ge(any_ok, n + 1)
                        for t in range(NT):
                            last = pool.tensor_tensor(m_add_k[:, (B + n) % 3, t, :], m_off[:, t, :], any_big, ALU.mult)
                        last.then_inc(m_ready, 1)
                    if kind == "M":
                        mg = 4 * g + k
                        pool.wait_ge(b_drained, b_order[e])
                        if mg >= 2:
                            pool.wait_ge(maxrow_in[mg % 2], 48 * (mg // 2))
                        part = m_parts[:, mg % 2, :, :]
                        link(pool.tensor_copy(part[:, 0, :], m_rest[:, 0, :]))
                        link(pool.tensor_tensor(m_rest[:, 1, :], m_rest[:, 0, :], part[:, 0, :], ALU.subtract))
                        link(pool.tensor_copy(part[:, 1, :], m_rest[:, 1, :]))
                        pool.tensor_tensor(part[:, 2, :], m_rest[:, 1, :], part[:, 1, :],
                                           ALU.subtract).then_inc(m_split, 1)
                        pool.wait_ge(m_split, mg + 1)
                    if kind == "H":
                        src = f[:, k, :] if l == 1 and k < 2 else rotated[:, :]
                        pool.wait_ge(hi_done, item + 1)
                        if item:
                            pool.wait_ge(mid_done, item)
                            pool.wait_ge(split_done, item)
                        pool.tensor_tensor(rest[:, :], src, parts[:, k, 0, :], ALU.subtract).then_inc(rest_done, 1)
                    if kind == "D":
                        pool.wait_ge(mid_done, item + 1)
                        pool.wait_ge(rest_done, item + 1)
                        pool.tensor_tensor(parts[:, k, 2, :], rest[:, :], parts[:, k, 1, :],
                                           ALU.subtract).then_inc(split_done, 1)

            s0, s1 = ff

            def early_unit(e):
                if e == 0:
                    for i in range(ITEMS):
                        pool.wait_ge(spill[i], 16 * 2 * B)
                    pool.wait_ge(a_filled, a_order[(1, "J", B - 1, 3)])
                    pool.wait_ge(b_filled, b_order[(1, "V", B - 1, 1)])
                if e % 2 == 0:
                    pool.wait_ge(units_in[e // 2], 16)
                link(pool.tensor_copy(we[:, e, 0, :, :], we_f[e // 2][:, e % 2, :, :]))
                weight_rest(e)

            def weight_rest(e):
                pool.tensor_tensor(we[:, e, 1, :, :], we_f[e // 2][:, e % 2, :, :], we[:, e, 0, :, :].bitcast(F32),
                                   ALU.subtract).then_inc(s1["w_lo"], 1)


            def hidden_rest(n):
                for t in range(POOL_TILES):
                    pool.wait_ge(s0["h_hi"], n * HT + t + 1)
                    pool.tensor_tensor(hid0_lo[:, t, :], raw0[:, t % 4, :], hid0_hi[:, t, :].bitcast(F32),
                                       ALU.subtract).then_inc(s0["h_lo"], 1)

            attention(0, 2)
            with pool.Fori(0, B - 1) as n:
                hidden_rest(n)
            attention(1, 0)
            hidden_rest(B - 1)
            attention(1, 1)
            attention(1, 2)

            def unit_rest(n, e):
                for t in range(UT):
                    o = UT * e + t
                    pool.wait_ge(s1["h_hi"], n * UNITS * UT + o + 1)
                    pool.tensor_tensor(hid1[:, 1, e % 2, t, :], raw1[:, o % 4, :], hid1[:, 0, e % 2, t, :].bitcast(F32),
                                       ALU.subtract).then_inc(s1["h_lo"], 1)

            for e in range(UNITS):
                unit_rest(0, e)
                if EARLY_UNITS + e < UNITS:
                    pool.wait_ge(s1["w_hi"], e + 1)
                    weight_rest(EARLY_UNITS + e)
            with pool.Fori(1, B) as n:
                for e in range(UNITS):
                    unit_rest(n, e)

        @block.scalar
        def _(act):
            count_from_offe(act, "act")

            def attention(layer, stretch):
                for e in stretches[layer][stretch]:
                    l, kind, n, k = e
                    g = batch(l, n)
                    if kind == "NEXT":
                        act.wait_ge(a_filled, a_order[e])
                        high = (xT_hi, xT_hi1)[l]
                        act.copy(high[:, k, :], ps[:, A_BANK, :]).then_inc(ff[l]["t_hi"], 1)
                    if kind == "T":
                        act.wait_ge(a_filled, a_order[e])
                        act.copy(xnT[:, k, :], ps[:, A_BANK, :]).then_inc(a_drained, 1)
                    if kind == "J":
                        act.wait_ge(a_filled, a_order[e])
                        if g:
                            act.wait_ge(split_done, ITEMS * (g - 1) + k + 1)
                        act.activation(f[:, k, :], ps[:, A_BANK, :], ACT.Identity,
                                       bias=bqk[:, l, k:k + 1]).then_inc(a_drained, 1)
                    if kind == "SCORE":
                        o = 64 * g + k
                        G, j = o // 4, o % 4
                        act.wait_ge(st_filled, o + 1)
                        if G >= 2 and j == 0:
                            act.wait_ge(pv_done, G - 1)
                        act.activation(probs[:, G % 2, j, :], ps[:, ST_BANK[o % 2], :], ACT.Exp,
                                       scale=SCALE).then_inc(exp_done, 1)
                    if kind == "M":
                        mg = 4 * g + k
                        act.wait_ge(b_filled, b_order[e])
                        if mg:
                            act.wait_ge(m_split, mg)
                        act.activation(m_rest[:, 0, :], ps[0:4 * NT, B_BANK, 0:P], ACT.Copy,
                                       scale=-1.0).then_inc(b_drained, 1)
                    if kind == "E":
                        act.wait_ge(pv_done, STEPS * g + 4 * k + 4)
                        if 4 * g + k >= 2:
                            pl, pn = divmod((4 * g + k - 2) // 4, B)
                            act.wait_ge(b_filled, b_order[(pl, "OT", pn, (k - 2) % 4)])
                        act.copy(o_heads[:, k % 2, :], ps[:, PV_BANK, :]).then_inc(heads_out, 1)
                    if kind == "OF":
                        act.wait_ge(a_filled, a_order[e])
                        if g:
                            pl, pn = divmod(g - 1, B)
                            act.wait_ge(b_filled, b_order[(pl, "OP", pn, 1)])
                        act.copy(o_feat[:, k, :], ps[:, A_BANK, :]).then_inc(a_drained, 1)

            def transposed(s, n, high):
                for k in range(KT):
                    act.wait_ge(s["t_filled"], 1 + n * KT + k + 1)
                    act.copy(high[:, k, :], ps[:, T_BANK[k], :]).then_inc(s["t_hi"], 1)

            def gelu(n):
                s = ff[0]
                for t in range(HT):
                    act.wait_ge(s["u_filled"], n * HT + t + 1)
                    if t >= 4:
                        act.wait_ge(s["h_lo"], 1 + n * POOL_TILES + t - 3)
                    elif t >= DVE_TILES:
                        act.wait_ge(s["h_lo_dve"], 1 + n * DVE_TILES)
                    else:
                        act.wait_ge(s["h_lo"], 1 + n * POOL_TILES)
                    act.activation(raw0[:, t % 4, :], ps[:, U_BANK[t % 4], :], ACT.Gelu, bias=b1_col[:, t:t + 1],
                                   scale=alpha1[:, t:t + 1]).then_inc(s["u_drained"], 1)
                    act.wait_ge(s["u_drained"], 1 + n * HT + t + 1)
                    if t == 0:
                        act.wait_ge(s["d_filled"], 1 + n * 2)
                    act.copy(hid0_hi[:, t, :], raw0[:, t % 4, :]).then_inc(s["h_hi"], 1)

            attention(0, 0)
            act.wait_ge(const_in, 16 * CONSTS)
            act.activation(tanhg[:, :], gates[:, :], ACT.Tanh).then_inc(gate_ok, 1)
            attention(0, 2)
            s = ff[0]
            act.wait_ge(s["w_in"], 16 * 5)
            act.wait_ge(st_filled, 64 * B)
            act.activation(w1_s[:, :, :], w1_f[:, :, :], ACT.Sign).then_inc(s["w_hi"], 1)
            act.activation(w2_s[:, :, :], w2_f[:, :, :], ACT.Sign).then_inc(s["w_hi"], 1)
            act.wait_ge(s["w_hi"], 2)
            act.activation(w2_f[:, :, :], w2_f[:, :, :], ACT.Abs).then_inc(s["w_hi"], 1)
            act.wait_ge(alpha_ok, 1)
            with act.Fori(0, B - 1) as n:
                gelu(n)
                transposed(s, n + 1, xT_hi)
            attention(1, 0)
            gelu(B - 1)
            attention(1, 1)
            attention(1, 2)
            s = ff[1]
            act.wait_ge(x_upd, 4 * B)
            for e in range(EARLY_UNITS, UNITS):
                if e % 2 == 0:
                    act.wait_ge(units_in[e // 2], 16)
                act.copy(we[:, e, 0, :, :], we_f[e // 2][:, e % 2, :, :]).then_inc(s["w_hi"], 1)

            def rectify(n, e):
                for t in range(UT):
                    o = UT * e + t
                    act.wait_ge(s["u_filled"], n * UNITS * UT + o + 1)
                    act.wait_ge(s["h_lo"], 1 + n * UNITS * UT + max(0, o - 3))
                    act.activation(raw1[:, o % 4, :], ps[:, U_BANK[o % 4], :], ACT.Relu).then_inc(s["u_drained"], 1)

            def high_parts(n, e):
                for t in range(UT):
                    o = UT * e + t
                    act.wait_ge(s["squared"], n * UNITS * UT + o + 1)
                    if t == 0:
                        act.wait_ge(s["d_filled"], 1 + n * 2 * UNITS + max(0, 2 * (e - 1)))
                    act.copy(hid1[:, 0, e % 2, t, :], raw1[:, o % 4, :]).then_inc(s["h_hi"], 1)

            def second_weight(n):
                act.wait_ge(s["g_diff"], n * 1 + 1)
                act.activation(g_w[:, :, 1:2], g_w[:, :, 0:1], ACT.Exp).then_inc(s["g_exp"], 1)

            def experts(n, last):
                for e in range(UNITS):
                    rectify(n, e)
                    high_parts(n, e)
                    if e == 1:
                        second_weight(n)
                if not last:
                    transposed(s, n + 1, xT_hi1)

            with act.Fori(0, B - 1) as n:
                experts(n, False)
            experts(B - 1, True)

        @block.tensor
        def _(pe):
            def bank_a(e):
                if a_order[e] > 1:
                    pe.wait_ge(a_drained, a_order[e] - 1)
                return ps[:, A_BANK, :]

            def bank_b(e):
                if b_order[e] > 1:
                    pe.wait_ge(b_drained, b_order[e] - 1)
                return ps[:, B_BANK, :]

            def max_scores(l, g, s, qt):
                o, sl = 64 * g + 4 * s + qt, g % 2
                if s % 8 == 0 and qt == 0:
                    pe.wait_ge(slot_in[sl][s // 8], 16 * FILLS[s // 8] * (g // 2 + 1))
                if o >= 3:
                    pe.wait_ge(max_drained, o - 2)
                pe.matmul(ps[:, MAX_BANK[o % 3], :], q_op[0:MAX_K, sl, s, qt * P:(qt + 1) * P],
                          k_op[0:MAX_K, sl, s, :], start=True, stop=True).then_inc(max_filled, 1)

            def scores(l, g, s, j):
                o, sl, h, kt = 64 * g + 4 * s + j, g % 2, 4 * (s // 4) + j, s % 4
                if kt == 0 and j == 0:
                    mg = 4 * g + s // 4
                    pe.wait_ge(maxrow_in[mg % 2], 48 * (mg // 2 + 1))
                    if l and s == 0:
                        pe.wait_ge(m_ready, g - B + 1)
                if o >= 2:
                    pe.wait_ge(exp_done, o - 1)
                mm = pe.matmul(ps[:, ST_BANK[o % 2], :], k_op[0:ST_K, sl, h, kt * P:(kt + 1) * P],
                               q_op[0:ST_K, sl, h, :], start=True, stop=(l == 0))
                if l:
                    mm = pe.matmul(ps[:, ST_BANK[o % 2], :], ident_b[:, :], m_add_k[:, g % 3, kt, :],
                                   start=False, stop=True)
                mm.then_inc(st_filled, 1)

            def value_product(g, s):
                G, kt = STEPS * g + s, s % 4
                if s == 0:
                    pe.wait_ge(v_ready, g + 1)
                pe.wait_ge(exp_done, 4 * G + 4)
                if kt == 0 and G:
                    pe.wait_ge(heads_out, G // 4)
                for j in range(4):
                    mm = pe.matmul(ps[32 * j:32 * j + VW, PV_BANK, :], values[:, g % 2, kt, 4 * (s // 4) + j, :],
                                   probs[:, G % 2, j, :], start=(kt == 0), stop=(kt == 3))
                mm.then_inc(pv_done, 1)

            def attention(layer, stretch):
                for e in stretches[layer][stretch]:
                    l, kind, n, k = e
                    g = batch(l, n)
                    if kind == "NEXT":
                        bank = bank_a(e)
                        pe.wait_ge(ff[l]["ln"], 1)
                        for t in range(NT):
                            mm = pe.transpose(bank[:, t * P:(t + 1) * P], xn[:, t, k * P:(k + 1) * P], ident[:, :])
                        mm.then_inc(a_filled, 1)
                    if kind == "T":
                        bank = bank_a(e)
                        pe.wait_ge(ln_done, g + 1)
                        for t in range(NT):
                            mm = pe.transpose(bank[:, t * P:(t + 1) * P], xn[:, t, k * P:(k + 1) * P], ident[:, :])
                        mm.then_inc(a_filled, 1)
                    if kind == "C" and k == 4:
                        bank = bank_b(e)
                        pe.wait_ge(m_stage_free, 4 * n + 4)
                        for t in range(NT):
                            mm = pe.matmul(bank, ones_b[:, :], m_off[:, t, :], start=(t == 0), stop=(t == NT - 1))
                        mm.then_inc(b_filled, 1)
                    if kind == "J":
                        bank = bank_a(e)
                        if k == 0:
                            pe.wait_ge(wk_in, 32 * (l + 1))
                            pe.wait_ge(ctxk_in, 16 * (g + 1))
                        if k == 2:
                            pe.wait_ge(w_in, 48 * (l + 1))
                            pe.wait_ge(a_drained, a_order[(l, "T", n, 1)])
                        src, w, ft = (xnT if k >= 2 else ctx_k), 1 - k // 2, k % 2
                        for c in range(KT):
                            mm = pe.matmul(bank, w_att[:, w, c, ft * P:(ft + 1) * P], src[:, c, :],
                                           start=(c == 0), stop=(c == KT - 1))
                        mm.then_inc(a_filled, 1)
                    if kind == "R":
                        bank = bank_b(e)
                        pe.wait_ge(a_drained, a_order[(l, "J", n, k)])
                        pe.matmul(bank, rot_m[:, :], f[:, k, :], start=True, stop=True).then_inc(b_filled, 1)
                    if kind == "MAX":
                        max_scores(l, g, k // 4, k % 4)
                    if kind == "M":
                        bank = bank_b(e)
                        pe.wait_ge(max_drained, 64 * g + 16 * (k + 1))
                        pe.transpose(bank[0:4 * NT, 0:P], max_q[:, 16 * k:16 * k + 16], ident[:, :]).then_inc(b_filled, 1)
                    if kind == "V":
                        bank = bank_b(e)
                        pe.wait_ge(ctxv_in, 16 * (g + 1))
                        for t in range(2):
                            tok = (2 * k + t) * P
                            for c in range(KT):
                                mm = pe.matmul(bank[:, t * D:(t + 1) * D], ctx_v[:, c, tok:tok + P],
                                               w_att[:, 2, c, :], start=(c == 0), stop=(c == KT - 1))
                        mm.then_inc(b_filled, 1)
                    if kind == "SCORE":
                        scores(l, g, k // 4, k % 4)
                    if kind == "PV":
                        value_product(g, k)
                    if kind == "OT":
                        bank = bank_b(e)
                        pe.wait_ge(heads_out, 4 * g + k + 1)
                        for t in range(NT):
                            mm = pe.transpose(bank[:, t * P:(t + 1) * P], o_heads[:, k % 2, t * P:(t + 1) * P],
                                              ident[:, :])
                        mm.then_inc(b_filled, 1)
                    if kind == "OF":
                        bank = bank_a(e)
                        pe.wait_ge(b_drained, b_order[(l, "OT", n, 3)])
                        for t in range(NT):
                            mm = pe.transpose(bank[:, t * P:(t + 1) * P], o_tok[:, t, k * P:(k + 1) * P], ident[:, :])
                        mm.then_inc(a_filled, 1)
                    if kind == "OP":
                        bank = bank_b(e)
                        pe.wait_ge(a_drained, a_order[(l, "OF", n, 1)])
                        pe.wait_ge(wo_in, 32 * (l + 1))
                        for t in range(2):
                            tok = (2 * k + t) * P
                            for c in range(KT):
                                mm = pe.matmul(bank[:, t * D:(t + 1) * D], o_feat[:, c, tok:tok + P],
                                               w_att[:, 3, c, :], start=(c == 0), stop=(c == KT - 1))
                        mm.then_inc(b_filled, 1)

            def leave_attention(l):
                pe.wait_ge(a_drained, A_END[l])
                pe.wait_ge(b_drained, B_END[l])
                pe.wait_ge(exp_done, 64 * B * (l + 1))
                pe.wait_ge(max_drained, 64 * B * (l + 1))
                pe.wait_ge(heads_out, 4 * B * (l + 1))

            def tokens(s, n):
                pe.wait_ge(s["ln"], n * 1 + 1)
                if s is ff[1]:
                    pe.wait_ge(s["gate"], n * 1 + 1)
                for k in range(KT):
                    pe.wait_ge(s["t_drained"], 1 + (n - 1) * KT + k + 1)
                    for t in range(NT):
                        mm = pe.transpose(ps[:, T_BANK[k], t * P:(t + 1) * P], xn[:, t, k * P:(k + 1) * P], ident[:, :])
                    mm.then_inc(s["t_filled"], 1)

            def up0(n):
                s = ff[0]
                pe.wait_ge(s["t_drained"], 1 + n * KT + KT)
                for t in range(HT):
                    pe.wait_ge(s["u_drained"], 1 + n * HT + max(0, t - 3))
                    for c in range(KT):
                        for tokens_part in (xT_hi, xT_lo):
                            mm = pe.matmul(ps[:, U_BANK[t % 4], :], w1_s[:, c, t * P:(t + 1) * P], tokens_part[:, c, :],
                                           start=(c == 0 and tokens_part is xT_hi),
                                           stop=(c == KT - 1 and tokens_part is xT_lo))
                    mm.then_inc(s["u_filled"], 1)

            def down0(n):
                s = ff[0]
                for half in range(2):
                    pe.wait_ge(s["d_drained"], 1 + n * 2)
                    for t in range(2):
                        tok = (2 * half + t) * P
                        for c in range(HT):
                            if half == 0 and t == 0:
                                if c < POOL_TILES:
                                    pe.wait_ge(s["h_lo"], 1 + n * POOL_TILES + c + 1)
                                else:
                                    pe.wait_ge(s["h_lo_dve"], 1 + n * DVE_TILES + c - POOL_TILES + 1)
                            for part in (hid0_hi, hid0_lo):
                                mm = pe.matmul(ps[:, D_BANK[half], t * D:(t + 1) * D], part[:, c, tok:tok + P],
                                               w2_s[:, c, :], start=(c == 0 and part is hid0_hi),
                                               stop=(c == HT - 1 and part is hid0_lo))
                    mm.then_inc(s["d_filled"], 1)

            count_from_offe(pe, "pe")
            attention(0, 0)
            pe.wait_ge(const_in, 16 * CONSTS)
            pe.wait_ge(const_ok, 3)
            attention(0, 2)

            leave_attention(0)
            s = ff[0]
            pe.wait_ge(s["w_hi"], 3)
            for c in range(HT):
                mm = pe.matmul(ps[:, D_BANK[0], 0:D], ones_f[:, 0:1].to_broadcast([P, P]), w2_f[:, c, :], start=(c == 0), stop=(c == HT - 1))
            mm.then_inc(w2_sums, 1)
            pe.wait_ge(alpha_ok, 2)
            with pe.Fori(0, B - 1) as n:
                up0(n)
                tokens(s, n + 1)
                down0(n)
            pe.wait_ge(s["t_drained"], 1 + KT * B)
            attention(1, 0)
            up0(B - 1)
            attention(1, 1)
            down0(B - 1)

            pe.wait_ge(s["u_drained"], 1 + HT * B)
            pe.wait_ge(s["d_drained"], 1 + 2 * B)
            attention(1, 2)

            leave_attention(1)
            s = ff[1]

            def route(n):
                pe.wait_ge(s["t_drained"], 1 + n * KT + KT)
                pe.wait_ge(s["gate"], 1 + n * 1)
                for t in range(NT):
                    for c in range(KT):
                        mm = pe.matmul(ps[:, R_BANK, t * EXPERTS:(t + 1) * EXPERTS], xT[:, c, t * P:(t + 1) * P],
                                       w_rt[:, c, :], start=(c == 0), stop=(c == KT - 1))
                mm.then_inc(s["r_filled"], 1)

            HI_LO = ((0, 0), (0, 1), (1, 0))

            def up1(n, e):
                pe.wait_ge(s["w_lo"], e + 1)
                for t in range(UT):
                    o = UT * e + t
                    pe.wait_ge(s["u_drained"], 1 + n * UNITS * UT + max(0, o - 3))
                    for c in range(KT):
                        for j, (a, b) in enumerate(HI_LO):
                            w = we[:, e, a, 0, c * EF + t * P:c * EF + (t + 1) * P]
                            mm = pe.matmul(ps[:, U_BANK[o % 4], :], w, (xT_hi1, xT_lo1)[b][:, c, :],
                                           start=(c == 0 and j == 0), stop=(c == KT - 1 and j == 2))
                    mm.then_inc(s["u_filled"], 1)

            def down1(n, e):
                pe.wait_ge(s["h_lo"], 1 + n * UNITS * UT + UT * (e + 1))
                for half in range(2):
                    pe.wait_ge(s["d_drained"], 1 + n * 2 * UNITS + max(0, 2 * e + half - 1))
                    for t in range(2):
                        tok = (2 * half + t) * P
                        for c in range(UT):
                            for j, (a, b) in enumerate(HI_LO):
                                mm = pe.matmul(ps[:, D_BANK[half], t * D:(t + 1) * D], hid1[:, b, e % 2, c, tok:tok + P],
                                               we[:, e, a, 1, c * D:(c + 1) * D],
                                               start=(c == 0 and j == 0), stop=(c == UT - 1 and j == 2))
                    mm.then_inc(s["d_filled"], 1)

            pe.wait_ge(s["w_in"], 16)
            route(0)

            def experts(n, last):
                up1(n, 0)
                up1(n, 1)
                for e in range(2, UNITS):
                    up1(n, e)
                    down1(n, e - 2)
                if not last:
                    tokens(s, n + 1)
                down1(n, UNITS - 2)
                down1(n, UNITS - 1)
                if not last:
                    route(n + 1)

            with pe.Fori(0, B - 1) as n:
                experts(n, False)
            experts(B - 1, True)

        @block.vector
        def _(dve):
            links = [0]

            def link(ins):
                links[0] += 1
                ins.then_inc(chain, 1)
                dve.wait_ge(chain, links[0])

            def stand():
                dve.sem_inc(stood, 1)

            def layer_norm(rows, count, piece):
                v, y, a = nw[:, 0, :], nw[:, 1, :], nw[:, 2, :]

                def newton(steps):
                    for _ in range(steps):
                        count(dve.scalar_tensor_tensor(a, y, -0.5, y, ALU.mult, ALU.mult))
                        count(dve.tensor_tensor(a, a, v, ALU.mult))
                        count(dve.scalar_tensor_tensor(y, a, 1.5, y, ALU.add, ALU.mult))

                if piece == 0:
                    for t in range(NT):
                        last = dve.bn_stats(stats[:, t, :], rows[:, t, :])
                    count(last)
                if piece == 1:
                    stand()
                    for t in range(NT):
                        last = dve.bn_aggr(mv[:, t, :], stats[:, t, :])
                    count(last)
                    count(dve.tensor_scalar(v, mv[:, :, 1], EPS, None, ALU.add))
                    count(dve.tensor_scalar(nw[:, 3, :].bitcast(I32), v.bitcast(I32), 1, None, ALU.arith_shift_right))
                    count(dve.tensor_scalar(y.bitcast(I32), nw[:, 3, :].bitcast(I32), -1.0, float(0x5F3759DF),
                                            ALU.mult, ALU.add))
                    newton(1)
                if piece == 2:
                    newton(NEWTON - 1)
                if piece == 3:
                    for t in range(NT):
                        last = dve.tensor_scalar(xn[:, t, :], rows[:, t, :], mv[:, t, 0:1], nw[:, 1, t:t + 1],
                                                 ALU.subtract, ALU.mult)
                    return last

            def attention(layer, stretch):
                for e in stretches[layer][stretch]:
                    l, kind, n, k = e
                    g = batch(l, n)
                    item = ITEMS * g + k
                    if kind == "NORM":
                        if k == 3:
                            dve.wait_ge(a_filled, a_order[(l, "T", B - 1, 1)])
                        last = layer_norm(x[:, 0:NT, :], link, k)
                        if k == 3:
                            last.then_inc(ff[l]["ln"], 1)
                    if kind == "NEXT":
                        dve.wait_ge(ff[l]["t_hi"], k + 1)
                        if l:
                            dve.tensor_copy(xT[:, k, :], ps[:, A_BANK, :])
                        high, low = ((xT_hi, xT_lo), (xT_hi1, xT_lo1))[l]
                        dve.tensor_tensor(low[:, k, :], ps[:, A_BANK, :], high[:, k, :].bitcast(F32),
                                          ALU.subtract).then_inc(a_drained, 1)
                    if kind == "LN":
                        if k == 0 and l == 0:
                            dve.wait_ge(x_in[n], 16)
                        elif k == 0:
                            dve.wait_ge(ff[0]["x_done"], 2 * n + 2)
                        if k == 3 and n:
                            dve.wait_ge(a_filled, a_order[(l, "T", n - 1, 1)])
                        elif k == 3 and l:
                            dve.wait_ge(ff[0]["t_filled"], 1 + KT * B)
                        last = layer_norm(x[:, n * NT:(n + 1) * NT, :], link, k)
                        if k == 3:
                            last.then_inc(ln_done, 1)
                    if kind == "C":
                        mask_piece(e, n, k)
                    if kind == "R":
                        dve.wait_ge(b_filled, b_order[e])
                        if item:
                            dve.wait_ge(source_ok, item)
                        dve.tensor_tensor(rot_tmp, ps[:, B_BANK, :], sin_t, ALU.mult).then_inc(b_drained, 1)
                    if kind == "H":
                        if g:
                            dve.wait_ge(spill[k], 16 * g)
                        if l and k < 2:
                            src = f[:, k, :]
                            dve.wait_ge(a_drained, a_order[(l, "J", n, k)])
                        else:
                            src = rotated[:, :]
                            dve.wait_ge(source_ok, sources(l, n, k))
                        dve.tensor_copy(parts[:, k, 0, :], src).then_inc(hi_done, 1)
                    if kind == "D":
                        dve.wait_ge(rest_done, item + 1)
                        dve.tensor_copy(parts[:, k, 1, :], rest[:, :]).then_inc(mid_done, 1)
                        if k == 2:
                            key_mask_row(l, g)
                    if kind == "MAX":
                        row_max(l, g, k // 4, k % 4)
                    if kind == "V":
                        dve.wait_ge(b_filled, b_order[e])
                        if g >= 2 and k == 0:
                            dve.wait_ge(pv_done, STEPS * (g - 1))
                        dve.tensor_tensor(values[:, g % 2, 2 * k:2 * k + 2, :, 0:HD],
                                          ps[:, B_BANK, :].rearrange("p (t h c) -> p t h c", t=2, h=HEADS),
                                          bv_bc[:, :].rearrange("p (h c) -> p h c", h=HEADS).unsqueeze(1).to_broadcast([P, 2, HEADS, HD]),
                                          ALU.add).then_inc(b_drained, 1)
                        if k:
                            dve.wait_ge(b_drained, b_order[e])
                            on = key_on[:, n * NT:(n + 1) * NT] if l == 0 else ones_f[:, 0:NT]
                            dve.tensor_copy(values[:, g % 2, :, :, HD], on.unsqueeze(2).to_broadcast([P, NT, HEADS])).then_inc(v_ready, 1)
                    if kind == "OT":
                        dve.wait_ge(b_filled, b_order[e])
                        if g and k == 0:
                            pl, pn = divmod(g - 1, B)
                            dve.wait_ge(a_filled, a_order[(pl, "OF", pn, 1)])
                        heads = ps[:, B_BANK, :].rearrange("p (t j c) -> p t j c", t=NT, j=4)
                        link(dve.reciprocal(rec[:, :, :].unsqueeze(3), heads[:, :, :, HD:HD + 1]))
                        dve.tensor_tensor(o_tok[:, :, 64 * k:64 * k + 64].rearrange("p t (j c) -> p t j c", j=4),
                                          heads[:, :, :, 0:HD], rec[:, :, :].unsqueeze(3).to_broadcast([P, NT, 4, HD]),
                                          ALU.mult).then_inc(b_drained, 1)
                    if kind == "OP":
                        dve.wait_ge(b_filled, b_order[e])
                        junk_written()
                        dve.tensor_tensor(upd[:, :, :], ps[:, B_BANK, :].rearrange("p (t n) -> p t n", t=2),
                                          bo_bc[:, :].unsqueeze(1).to_broadcast([P, 2, D]), ALU.add).then_inc(b_drained, 1)
                        dve.wait_ge(b_drained, b_order[e])
                        for t in range(2):
                            r = n * NT + 2 * k + t
                            gt = tok_gate[:, r:r + 1] if l == 0 else tanhg[:, 1:2]
                            last = dve.scalar_tensor_tensor(x[:, r, :], upd[:, t, :], gt, x[:, r, :], ALU.mult, ALU.add)
                        last.then_inc(x_upd, 1)
                        dve.wait_ge(x_upd, 2 * g + k + 1)

            def key_mask_row(l, g):
                dve.wait_ge(mrow_in, 16 * (g + 1))
                if g:
                    dve.wait_ge(slot_in[(g - 1) % 2][0], 16 * FILLS[0] * ((g - 1) // 2 + 1))
                ops = (-1.0, BIG, ALU.add, ALU.mult) if l == 0 else (0.0, None, ALU.mult)
                dve.tensor_scalar(mask_row[:, :], mrow8[:, :], *ops).then_inc(maskrow, 1)

            def mask_piece(e, n, k):
                if k in (1, 2):
                    h = slice(2 * k - 2, 2 * k)
                    dve.wait_ge(m_stage_free, 4 * n + k)
                    if n:
                        dve.wait_ge(q_mask, 2 * n)
                    link(dve.tensor_reduce(row_any[:, 0, h], m_off[:, h, :], AX.X, ALU.min))
                    link(dve.tensor_scalar(row_any[:, 1, h], row_any[:, 0, h], -1.0, BIG, ALU.add, ALU.mult))
                    for t in range(NT)[h]:
                        last = dve.tensor_scalar(m_add_q[:, n % 2, t, :], m_off[:, t, :], row_any[:, 1, t:t + 1], None,
                                                 ALU.mult)
                    last.then_inc(q_mask, 1)
                    dve.wait_ge(q_mask, 2 * n + k)
                if k == 4:
                    dve.wait_ge(b_filled, b_order[e])
                    dve.wait_ge(source_ok, sources(1, n, 1))
                    if n:
                        dve.wait_ge(m_ready, n)
                    dve.tensor_scalar(any_big, ps[:, B_BANK, :], S - 1.0, float(S), ALU.max,
                                      ALU.subtract).then_inc(b_drained, 1)
                    dve.wait_ge(b_drained, b_order[e])
                    link(dve.tensor_scalar(any_bc, any_big, -1.0, None, ALU.mult))
                    dve.tensor_scalar(any_big, any_big, BIG, None, ALU.mult).then_inc(any_ok, 1)

            maxima = [0]

            def junk_written():
                if maxima[0]:
                    dve.wait_ge(max_drained, maxima[0])

            def row_max(l, g, h, qt):
                o = 64 * g + 4 * h + qt
                maxima[0] = o + 1
                if h % 4 == 0 and qt == 0 and g:
                    pl, pn = divmod(g - 1, B)
                    dve.wait_ge(b_filled, b_order[(pl, "M", pn, h // 4)])
                dve.wait_ge(max_filled, o + 1)
                to, bank = max_q[:, 4 * h + qt:4 * h + qt + 1], ps[:, MAX_BANK[o % 3], :]
                if l == 0:
                    dve.tensor_reduce(to, bank, AX.X, ALU.max).then_inc(max_drained, 1)
                else:
                    dve.wait_ge(max_drained, o)
                    dve.tensor_tensor_reduce(junk, bank, m_add_q[:, (g - B) % 2, qt, :], 1.0, LOWEST,
                                             ALU.add, ALU.max, to).then_inc(max_drained, 1)

            count_from_offe(dve, "dve")
            attention(0, 0)
            dve.wait_ge(const_in, 16 * CONSTS)
            dve.wait_ge(const_ok, 3)
            link(dve.memset(ps[:, PV_BANK, :], 0.0))
            link(dve.tensor_copy(key_on[:, :], km8[:, :]))
            dve.wait_ge(gate_ok, 1)
            link(dve.tensor_scalar(tok_gate[:, :], key_on[:, :], tanhg[:, 0:1], None, ALU.mult))
            attention(0, 2)

            def norm_piece(s, l, n, count, piece):
                if piece == 0:
                    dve.wait_ge(x_upd, n * 2 + 2 + 2 * B * l)
                if piece == 3:
                    dve.wait_ge(s["t_filled"], 1 + n * KT)
                last = layer_norm(x[:, bass.ds(n * NT, NT), :], count, piece)
                if piece == 3:
                    last.then_inc(s["ln"], 1)

            def token_rest(s, n, high, low, whole):
                for k in range(KT):
                    dve.wait_ge(s["t_hi"], n * KT + k + 1)
                    if whole is not None:
                        dve.tensor_copy(whole[:, k, :], ps[:, T_BANK[k], :])
                    dve.tensor_tensor(low[:, k, :], ps[:, T_BANK[k], :], high[:, k, :].bitcast(F32),
                                      ALU.subtract).then_inc(s["t_drained"], 1)

            s = ff[0]
            dve.wait_ge(s["w_in"], 16 * 5)
            link(dve.tensor_reduce(alpha1[:, :], w1_n[:, :, :], AX.X, ALU.add, apply_absolute_value=True))
            dve.tensor_scalar(alpha1[:, :], alpha1[:, :], 1.0 / D, None, ALU.mult).then_inc(alpha_ok, 1)
            dve.wait_ge(w2_sums, 1)
            dve.tensor_scalar(alpha2[:, :], ps[:, D_BANK[0], 0:D], 1.0 / HID, None, ALU.mult).then_inc(alpha_ok, 1)
            dve.wait_ge(alpha_ok, 2)
            def looped(sem_, per, n, start):
                made = [start]

                def count(ins):
                    made[0] += 1
                    ins.then_inc(sem_, 1)
                    dve.wait_ge(sem_, n * per + made[0])
                return count

            def hidden_rest(n):
                for t in range(POOL_TILES, HT):
                    dve.wait_ge(s["h_hi"], n * HT + t + 1)
                    dve.tensor_tensor(hid0_lo[:, t, :], raw0[:, t % 4, :], hid0_hi[:, t, :].bitcast(F32),
                                      ALU.subtract).then_inc(s["h_lo_dve"], 1)

            def output0(n, count):
                for half in range(2):
                    dve.wait_ge(s["d_filled"], 1 + n * 2 + half + 1)
                    dve.tensor_tensor(upd[:, :, :], ps[:, D_BANK[half], :].rearrange("p (t n) -> p t n", t=2),
                                      alpha2[:, :].unsqueeze(1).to_broadcast([P, 2, D]), ALU.mult).then_inc(s["d_drained"], 1)
                    dve.wait_ge(s["d_drained"], 1 + n * 2 + half + 1)
                    count(dve.tensor_tensor(upd[:, :, :], upd[:, :, :], b2_bc[:, :].unsqueeze(1).to_broadcast([P, 2, D]),
                                            ALU.add))
                    rows = x[:, bass.ds(n * NT + 2 * half, 2), :]
                    dve.scalar_tensor_tensor(rows, upd[:, :, :], tanhg[:, 2:3], rows, ALU.mult,
                                             ALU.add).then_inc(s["x_done"], 1)
                    dve.wait_ge(s["x_done"], n * 2 + half + 1)

            PER0 = LN_LINKS + 2
            with dve.Fori(0, B - 1) as n:
                c = looped(chain0, PER0, n, 0)
                for piece in range(4):
                    norm_piece(s, 0, n + 1, c, piece)
                hidden_rest(n)
                token_rest(s, n + 1, xT_hi, xT_lo, None)
                output0(n, c)
            attention(1, 0)
            hidden_rest(B - 1)
            attention(1, 1)
            output0(B - 1, looped(chain0, PER0, B - 1, 0))
            attention(1, 2)

            s = ff[1]

            def best_two(n, count):
                dve.wait_ge(s["r_filled"], n * 1 + 1)
                count(dve.tensor_copy(logit[:, :, :], ps[:, R_BANK, 0:NT * EXPERTS].rearrange("p (t n) -> p t n", t=NT)))
                stand()
                for t in range(NT):
                    last = dve.max(top[:, t, :], logit[:, t, :])
                count(last)
                stand()
                for t in range(NT):
                    last = dve.max_index(top_i[:, t, :], top[:, t, :], logit[:, t, :])
                count(last)
                count(dve.tensor_copy(top_f[:, :, :], top_i[:, :, 0:2]))
                dve.tensor_tensor(g_w[:, :, 0:1], top[:, :, 1:2], top[:, :, 0:1], ALU.subtract).then_inc(s["g_diff"], 1)

            def expert_weights(n, count):
                dve.wait_ge(s["g_exp"], n * 1 + 1)
                count(dve.tensor_scalar(g_w[:, :, 2:3], g_w[:, :, 1:2], 1.0, None, ALU.add))
                count(dve.reciprocal(g_w[:, :, 2:3], g_w[:, :, 2:3]))
                count(dve.tensor_scalar(g_w[:, :, 2:3], g_w[:, :, 2:3], tanhg[:, 3:4], None, ALU.mult))
                count(dve.tensor_tensor(g_w[:, :, 3:4], g_w[:, :, 1:2], g_w[:, :, 2:3], ALU.mult))

            def spread_weights(n, count):
                for t in range(NT):
                    count(dve.tensor_scalar(hot[:, 0, :], iota_e[:, :], top_f[:, t, 0:1], g_w[:, t, 2:3], ALU.is_equal, ALU.mult))
                    count(dve.tensor_scalar(hot[:, 1, :], iota_e[:, :], top_f[:, t, 1:2], g_w[:, t, 3:4], ALU.is_equal, ALU.mult))
                    last = dve.tensor_tensor(gate[:, t, SHARED:UNITS], hot[:, 0, :], hot[:, 1, :], ALU.add)
                    if t < NT - 1:
                        count(last)
                last.then_inc(s["gate"], 1)
                dve.wait_ge(s["gate"], 1 + n * 1 + 1)

            def output1(n, e):
                for half in range(2):
                    u = 2 * e + half
                    dve.wait_ge(s["d_filled"], 1 + n * 2 * UNITS + u + 1)
                    dve.wait_ge(s["d_drained"], 1 + n * 2 * UNITS + u)
                    for t in range(2):
                        rows = x[:, bass.ds(n * NT + 2 * half + t, 1), :]
                        last = dve.scalar_tensor_tensor(rows, ps[:, D_BANK[half], t * D:(t + 1) * D].unsqueeze(1),
                                                        gate[:, 2 * half + t, e:e + 1], rows, ALU.mult, ALU.add)
                    last.then_inc(s["d_drained"], 1)

            def squares(n, e):
                for t in range(UT):
                    o = UT * e + t
                    dve.wait_ge(s["u_drained"], 1 + n * UNITS * UT + o + 1)
                    h = raw1[:, o % 4, :]
                    dve.tensor_tensor(h, h, h, ALU.mult).then_inc(s["squared"], 1)

            PER1 = LN_LINKS + GATE_LINKS

            for t in range(NT):
                last = dve.tensor_scalar(gate[:, t, 0:SHARED], ones_f[:, 0:SHARED], tanhg[:, 3:4], None, ALU.mult)
            link(last)

            def experts(n, last):
                c = looped(chain1, PER1, n, 0)
                for e in range(UNITS + 2):
                    if e < UNITS:
                        squares(n, e)
                    if e == 1:
                        best_two(n, c)
                    if e == 2:
                        expert_weights(n, c)
                    if e == UNITS and not last:
                        token_rest(s, n + 1, xT_hi1, xT_lo1, xT)
                    if e >= 2:
                        output1(n, e - 2)
                    if e == 2:
                        spread_weights(n, c)
                    if 3 <= e < 7 and not last:
                        norm_piece(s, 1, n + 1, c, e - 3)

            with dve.Fori(0, B - 1) as n:
                experts(n, False)
            experts(B - 1, True)


def tables_of_shape():
    inv = (1.0 / np.float32(10000.0) ** (np.arange(0, HD, 2, dtype=np.float32) / np.float32(HD))).astype(np.float32)
    angle = np.outer(np.arange(S, dtype=np.float32), inv).astype(np.float32)
    angle = np.concatenate([angle, angle], axis=1)
    rot = np.zeros((P, P), np.float32)
    for m in range(P):
        low = m % HD < HD // 2
        rot[m + HD // 2 if low else m - HD // 2, m] = -1.0 if low else 1.0
    return {
        "ident": np.eye(P, dtype=np.float32), "rot": rot,
        "cosT": np.tile(np.cos(angle).T, (P // HD, 1)).astype(np.float32),
        "sinT": np.tile(np.sin(angle).T, (P // HD, 1)).astype(np.float32),
        "iota": np.arange(EXPERTS, dtype=np.float32),
        "ones_row": np.full((4, HEADS * S), 0x3F80, np.uint16)
    }


def expert_units(ws1, ws2, w1, w2):
    up = np.concatenate([ws1.reshape(SHARED, EF, D), w1]).transpose(0, 2, 1)
    down = np.concatenate([ws2.reshape(D, SHARED, EF).transpose(1, 2, 0), w2.transpose(0, 2, 1)])
    tiles = np.stack([up.reshape(UNITS, KT, P, EF), down.reshape(UNITS, UT, P, D)], axis=1)
    return tiles.transpose(0, 1, 3, 2, 4).reshape(UNITS, 2, P, UT * D)


def kernel(x, ctx_1024, mask_BxS2_bf1, mask_Bx1xSxS2_if1, g_xattn, g_ffn,
           L0_xattn_Wq, L0_xattn_bq, L0_xattn_Wk, L0_xattn_bk, L0_xattn_Wv, L0_xattn_bv, L0_xattn_Wp, L0_xattn_bp,
           L0_ffn_w1, L0_ffn_b1, L0_ffn_w2, L0_ffn_b2,
           L1_xattn_W_q, L1_xattn_b_q, L1_xattn_W_k, L1_xattn_b_k, L1_xattn_W_v, L1_xattn_b_v, L1_xattn_W_o, L1_xattn_b_o,
           L1_ffn_w_router, L1_ffn_w1_stack, L1_ffn_w2_stack, L1_ffn_ws1, L1_ffn_ws2):
    import concourse.bacc as bacc
    from concourse.bass_utils import run_bass_kernel_spmd

    A = np.asarray
    key_mask = A(mask_BxS2_bf1).view(np.uint8)
    pair_mask = A(mask_Bx1xSxS2_if1)[:, 0]
    arrays = {
        "x": A(x), "ctxT": A(ctx_1024).transpose(0, 2, 1), "g_xattn": A(g_xattn), "g_ffn": A(g_ffn),
        "mask_col": key_mask.reshape(B * NT, P).T, "mask_row": key_mask,
        "mask_q": pair_mask, "mask_k": pair_mask.transpose(0, 2, 1),
        "l0_wq": A(L0_xattn_Wq).T, "l0_wk": A(L0_xattn_Wk).T, "l0_wv": A(L0_xattn_Wv).T, "l0_wo": A(L0_xattn_Wp).T,
        "l0_bqk": np.concatenate([A(L0_xattn_bk).reshape(KT, P), A(L0_xattn_bq).reshape(KT, P)]).T,
        "l0_bv": A(L0_xattn_bv), "l0_bo": A(L0_xattn_bp),
        "l1_wq": A(L1_xattn_W_q), "l1_wk": A(L1_xattn_W_k), "l1_wv": A(L1_xattn_W_v), "l1_wo": A(L1_xattn_W_o),
        "l1_bqk": np.concatenate([A(L1_xattn_b_k).reshape(KT, P), A(L1_xattn_b_q).reshape(KT, P)]).T,
        "l1_bv": A(L1_xattn_b_v), "l1_bo": A(L1_xattn_b_o),
        "w1": A(L0_ffn_w1), "w1T": A(L0_ffn_w1).T, "b1": A(L0_ffn_b1).reshape(HT, P).T, "w2T": A(L0_ffn_w2).T, "b2": A(L0_ffn_b2),
        "w_router": A(L1_ffn_w_router).T,
        "units": expert_units(A(L1_ffn_ws1), A(L1_ffn_ws2), A(L1_ffn_w1_stack), A(L1_ffn_w2_stack)),
        **tables_of_shape(),
    }
    arrays = {name: np.ascontiguousarray(a) for name, a in arrays.items()}
    nc = bacc.Bacc("TRN2", target_bir_lowering=False, num_devices=1)
    d = {name: nc.dram_tensor(f"in_{name}", a.shape, mybir.dt.from_np(a.dtype), kind="ExternalInput").ap()
         for name, a in arrays.items()}
    out = nc.dram_tensor("out", [B, S, D], F32, kind="ExternalOutput").ap()
    bass_flamingo(nc, d, out)
    r = run_bass_kernel_spmd(nc, [{f"in_{name}": a for name, a in arrays.items()}], core_ids=[0])
    return r.results[0]["out"]
```
